# Optimizing a Trainium2 kernel written in Bass

```python
import numpy as np
import jax
import jax.numpy as jnp

def _softmax(x, axis=-1):
    return jax.nn.softmax(x, axis=axis)

def _gelu(x):
    return jax.nn.gelu(x, approximate=True)

def _silu(x):
    return jax.nn.silu(x)

def _sigmoid(x):
    return jax.nn.sigmoid(x)

def _layernorm(x, axis=-1, eps=1e-05):
    m = jnp.mean(x, axis=axis, keepdims=True)
    v = jnp.var(x, axis=axis, keepdims=True)
    return (x - m) / jnp.sqrt(v + eps)

def _scatter_add(tgt, idx, src, axis=0):
    return tgt.at[idx].add(src)

def _segment_sum(src, seg, n):
    return jax.ops.segment_sum(src, seg, n)
kernel_name = 'mk_adj_resnorm_d2_adj_r2_69a643'

def setup_inputs(seed: int=0):
    np.random.seed(seed)
    _w = jnp.asarray

    def _rec_inputs():
        import jax
        import jax.numpy as jnp
        _gk = jax.random.key(seed)
        x = -0.0002928 + 1 * jax.random.normal(jax.random.fold_in(_gk, 1), (128, 128, 256), jnp.float32)
        _a = jax.random.bernoulli(jax.random.fold_in(_gk, 2), 0.0625, (128, 128, 128))
        _a = jnp.logical_or(_a, jnp.eye(128, dtype=bool))
        adj = _a.astype(jnp.int32)
        return (x, adj)
    x, adj = _rec_inputs()

    def _L0_gnn_setup():
        import jax, jax.numpy as jnp
        import numpy as np
        B, N, D = (8, 512, 256)
        NH = 8
        DK = D // NH
        key = jax.random.key(seed)
        ks = jax.random.split(key, 6)
        x = jax.random.normal(ks[0], (B, N, D), dtype=jnp.float32)
        adj = jax.random.randint(ks[1], (B, N, N), 0, 2, dtype=jnp.int32)
        adj = jnp.maximum(adj, jnp.eye(N, dtype=jnp.int32)[None])
        s = 1.0 / np.sqrt(D)
        Wq = jax.random.normal(ks[2], (D, D), dtype=jnp.float32) * s
        Wk = jax.random.normal(ks[3], (D, D), dtype=jnp.float32) * s
        Wv = jax.random.normal(ks[4], (D, D), dtype=jnp.float32) * s
        Wo = jax.random.normal(ks[5], (D, D), dtype=jnp.float32) * s
        return {'x': x, 'adj': adj, 'Wq': Wq, 'Wk': Wk, 'Wv': Wv, 'Wo': Wo}
    _L0_gnn_all = _L0_gnn_setup()
    _L0_gnn_in = {k: v for k, v in _L0_gnn_all.items() if k in ('Wq', 'Wk', 'Wv', 'Wo')}
    del _L0_gnn_all

    def _L1_gnn_setup():
        import jax, jax.numpy as jnp
        import numpy as np
        L = 3
        D = 256
        B, N = (8, 512)
        EPS = 1e-05

        def layernorm(x, gamma, beta):
            mu = jnp.mean(x, axis=-1, keepdims=True)
            var = jnp.var(x, axis=-1, keepdims=True)
            return (x - mu) * jax.lax.rsqrt(var + EPS) * gamma + beta
        key = jax.random.key(seed)
        ks = jax.random.split(key, 12)
        s = 1.0 / np.sqrt(D)
        node_features = jax.random.normal(ks[0], (B, N, D), dtype=jnp.float32)
        adjacency_matrix = jax.random.randint(ks[1], (B, N, N), 0, 2, dtype=jnp.int32)
        return {'node_features': node_features, 'adjacency_matrix': adjacency_matrix, 'attn_w': jax.random.normal(ks[2], (L, 2 * D), dtype=jnp.float32) * (1.0 / np.sqrt(2 * D)), 'attn_b': jax.random.normal(ks[3], (L,), dtype=jnp.float32) * 0.01, 'W1': jax.random.normal(ks[4], (L, D, 4 * D), dtype=jnp.float32) * s, 'b1': jnp.zeros((L, 4 * D), dtype=jnp.float32), 'W2': jax.random.normal(ks[5], (L, 4 * D, D), dtype=jnp.float32) * (1.0 / np.sqrt(4 * D)), 'b2': jnp.zeros((L, D), dtype=jnp.float32), 'g1': jnp.ones((L, D), dtype=jnp.float32), 'beta1': jnp.zeros((L, D), dtype=jnp.float32), 'g2': jnp.ones((L, D), dtype=jnp.float32), 'beta2': jnp.zeros((L, D), dtype=jnp.float32)}
    _L1_gnn_all = _L1_gnn_setup()
    _L1_gnn_in = {k: v for k, v in _L1_gnn_all.items() if k in ('attn_w', 'attn_b', 'W1', 'b1', 'W2', 'b2', 'g1', 'beta1', 'g2', 'beta2')}
    del _L1_gnn_all
    return {'x': x, 'adj': adj, 'L0_gnn_Wq': _L0_gnn_in['Wq'], 'L0_gnn_Wk': _L0_gnn_in['Wk'], 'L0_gnn_Wv': _L0_gnn_in['Wv'], 'L0_gnn_Wo': _L0_gnn_in['Wo'], 'L1_gnn_attn_w': _L1_gnn_in['attn_w'], 'L1_gnn_attn_b': _L1_gnn_in['attn_b'], 'L1_gnn_W1': _L1_gnn_in['W1'], 'L1_gnn_b1': _L1_gnn_in['b1'], 'L1_gnn_W2': _L1_gnn_in['W2'], 'L1_gnn_b2': _L1_gnn_in['b2'], 'L1_gnn_g1': _L1_gnn_in['g1'], 'L1_gnn_beta1': _L1_gnn_in['beta1'], 'L1_gnn_g2': _L1_gnn_in['g2'], 'L1_gnn_beta2': _L1_gnn_in['beta2']}

def reference(x, adj, L0_gnn_Wq, L0_gnn_Wk, L0_gnn_Wv, L0_gnn_Wo, L1_gnn_attn_w, L1_gnn_attn_b, L1_gnn_W1, L1_gnn_b1, L1_gnn_W2, L1_gnn_b2, L1_gnn_g1, L1_gnn_beta1, L1_gnn_g2, L1_gnn_beta2):
    import jax
    import jax.numpy as jnp

    def _L0_gnn_ref(x, adj, Wq, Wk, Wv, Wo):
        import jax, jax.numpy as jnp
        import numpy as np
        B, N, D = (8, 512, 256)
        NH = 8
        DK = D // NH
        b, n, d = x.shape
        sqrt_dk = jnp.asarray(np.sqrt(DK), dtype=x.dtype)

        def heads(t):
            return t.reshape(b, n, NH, DK).transpose(0, 2, 1, 3)
        q = heads(x @ Wq)
        k = heads(x @ Wk)
        v = heads(x @ Wv)
        scores = jnp.einsum('bhnd,bhmd->bhnm', q, k) / sqrt_dk
        mask = adj.astype(bool)[:, None]
        scores = jnp.where(mask, scores, -jnp.inf)
        attn = jax.nn.softmax(scores, axis=-1)
        out = jnp.einsum('bhnm,bhmd->bhnd', attn, v)
        out = out.transpose(0, 2, 1, 3).reshape(b, n, d)
        return jax.nn.relu(out) @ Wo

    def _L1_gnn_ref(node_features, adjacency_matrix, attn_w, attn_b, W1, b1, W2, b2, g1, beta1, g2, beta2):
        import jax, jax.numpy as jnp
        import numpy as np
        L = 3
        D = 256
        B, N = (8, 512)
        EPS = 1e-05

        def layernorm(x, gamma, beta):
            mu = jnp.mean(x, axis=-1, keepdims=True)
            var = jnp.var(x, axis=-1, keepdims=True)
            return (x - mu) * jax.lax.rsqrt(var + EPS) * gamma + beta
        n = adjacency_matrix.shape[-1]
        mask = adjacency_matrix.astype(jnp.float32) + jnp.eye(n, dtype=jnp.float32) > 0
        x = node_features
        d = x.shape[-1]
        for l in range(attn_w.shape[0]):
            si = x @ attn_w[l, :d]
            sj = x @ attn_w[l, d:]
            scores = si[:, :, None] + sj[:, None, :] + attn_b[l]
            scores = jnp.where(scores >= 0, scores, 0.2 * scores)
            scores = jnp.where(mask, scores, -jnp.inf)
            attn = jax.nn.softmax(scores, axis=-1)
            agg = jnp.einsum('bij,bjd->bid', attn, x)
            h = layernorm(x + agg, g1[l], beta1[l])
            ff = jax.nn.gelu(h @ W1[l] + b1[l], approximate=False) @ W2[l] + b2[l]
            x = layernorm(h + ff, g2[l], beta2[l])
        return x
    x = _layernorm(x + _L0_gnn_ref(x, adj, L0_gnn_Wq, L0_gnn_Wk, L0_gnn_Wv, L0_gnn_Wo), axis=-1)
    x = _layernorm(x + _L1_gnn_ref(x, adj, L1_gnn_attn_w, L1_gnn_attn_b, L1_gnn_W1, L1_gnn_b1, L1_gnn_W2, L1_gnn_b2, L1_gnn_g1, L1_gnn_beta1, L1_gnn_g2, L1_gnn_beta2), axis=-1)
    return x

_drawn_inputs = setup_inputs


def setup_inputs(seed=0):
    import zlib

    import numpy as np

    out = dict(_drawn_inputs(seed))
    spreads = {'L1_gnn_b1': (0.0, 0.1),
     'L1_gnn_b2': (0.0, 0.1),
     'L1_gnn_g1': (1.0, 0.2),
     'L1_gnn_beta1': (0.0, 0.1),
     'L1_gnn_g2': (1.0, 0.2),
     'L1_gnn_beta2': (0.0, 0.1)}
    factors = {'L1_gnn_attn_b': 64.0}
    for name, (base, spread) in spreads.items():
        noise = np.random.default_rng([zlib.crc32(name.encode()), seed]).standard_normal(out[name].shape)
        drawn = base * np.exp(spread * noise) if base else spread * noise
        out[name] = jnp.asarray(drawn.astype(out[name].dtype))
    for name, factor in factors.items():
        out[name] = (out[name] * factor).astype(out[name].dtype)
    return out
```

```python
import concourse.bass as bass
from concourse import mybir
from contextlib import ExitStack

fp32 = mybir.dt.float32
fp32r = mybir.dt.float32r
bf16 = mybir.dt.bfloat16
ALU = mybir.AluOpType
ACT = mybir.ActivationFunctionType

P = 128
Q = 4
R = Q * P
D = 256
DT = D // P
FF = 1024
FT = FF // P
EPS = 1e-5
MASKED = -1e30


def at_least_0(count):
    return max(count, 0) if isinstance(count, int) else count


def worked_out(eng, count):
    return count if isinstance(count, int) else eng.to_reg(count)


def gnn_layers(nc, mem, layers, groups, x1, masks, x_mid, out):
    total = layers * groups
    ctx = ExitStack()
    with ctx:
        def sb(name, shape, dt=fp32):
            return ctx.enter_context(nc.sbuf_tensor(name, shape, dt))

        def bank(name, dt=fp32):
            return ctx.enter_context(nc.psum_tensor(name, [P, R], dt))

        def sem(name):
            return ctx.enter_context(nc.semaphore(name))

        ident = mem["ident"]
        x = [sb(f"x{i}", [P, Q, D]) for i in range(2)]
        mask = [sb(f"mask{i}", [P, R], bf16) for i in range(2)]
        x_hi = sb("x_hi", [P, Q, D], fp32r)
        x_lo = sb("x_lo", [P, Q, D], fp32r)
        dump = sb("dump", [P, 2 * Q, D], bf16)
        si = sb("si", [P, Q])
        sj = sb("sj", [P, Q])
        si_b = sb("si_b", [P, Q])
        top = sb("top", [P, Q])
        top_s = sb("top_s", [P, Q])
        top_l = sb("top_l", [P, Q])
        shift = sb("shift", [P, Q])
        s = sb("s", [P, R])
        e = sb("e", [P, R])
        e_sum = sb("e_sum", [P, Q])
        e_inv = sb("e_inv", [P, Q])
        eT_hi = sb("eT_hi", [P, R], fp32r)
        eT_lo = sb("eT_lo", [P, R], fp32r)
        u = sb("u", [P, Q, D])
        u_n = sb("u_n", [P, Q, D])
        stats1 = sb("stats1", [P, Q, 6])
        mv1 = sb("mv1", [P, Q, 2])
        var1 = sb("var1", [P, Q])
        rstd1 = sb("rstd1", [P, Q])
        hT = [sb(f"hT{i}", [P, DT, R]) for i in range(2)]
        hT_hi = [sb(f"hT_hi{i}", [P, DT, R], fp32r) for i in range(2)]
        hT_lo = [sb(f"hT_lo{i}", [P, DT, R], fp32r) for i in range(2)]
        g = [sb(f"g{i}", [P, R]) for i in range(2)]
        g_hi = [sb(f"g_hi{i}", [P, R], fp32r) for i in range(2)]
        g_lo = [sb(f"g_lo{i}", [P, R], fp32r) for i in range(2)]
        yT = sb("yT", [P, DT, R])
        stats2 = sb("stats2", [P, Q, 6])
        mv2 = sb("mv2", [P, Q, 2])
        var2 = sb("var2", [P, Q])
        rstd2 = sb("rstd2", [P, Q])
        shift2 = sb("shift2", [P, Q])
        y_n = sb("y_n", [P, Q, D])
        x_new = sb("x_new", [P, Q, D])
        x_first = sb("x_first", [P, Q, D])
        stats3 = sb("stats3", [P, Q, 6])
        mv3 = sb("mv3", [P, Q, 2])
        var3 = sb("var3", [P, Q])
        rstd3 = sb("rstd3", [P, Q])
        x_out = sb("x_out", [P, Q, D])
        half = sb("half", [P, Q])

        ps_ff = [bank(f"ps_ff{i}") for i in range(2)]
        ps_y = [bank(f"ps_y{i}") for i in range(DT)]
        ps_s = bank("ps_s")
        ps_a = bank("ps_a")
        ps_b = bank("ps_b")
        ps_c = bank("ps_c")
        ps_u = [ps_a, ps_b]
        ps_h = [ps_b, ps_c]
        ps_r = [ps_c, ps_a]

        x_in = [sem(f"x_in{i}") for i in range(2)]
        x_hi_ready, x_lo_ready = sem("x_hi_ready"), sem("x_lo_ready")
        sij_ready, sib_ready = sem("sij_ready"), sem("sib_ready")
        sj_spread = sem("sj_spread")
        s_ready = sem("s_ready")
        shift_steps = sem("shift_steps")
        s_biased, lrelu_ready, e_ready = sem("s_biased"), sem("lrelu_ready"), sem("e_ready")
        einv_ready = sem("einv_ready")
        eT_psum, eT_hi_ready, eT_lo_ready = sem("eT_psum"), sem("eT_hi_ready"), sem("eT_lo_ready")
        agg_psum = sem("agg_psum")
        u_ready, stats1_ready, mv1_ready = sem("u_ready"), sem("stats1_ready"), sem("mv1_ready")
        var1_ready, rstd1_ready, un_ready = sem("var1_ready"), sem("rstd1_ready"), sem("un_ready")
        hT_psum, hT_ready = sem("hT_psum"), sem("hT_ready")
        hT_hi_ready, hT_lo_ready = sem("hT_hi_ready"), sem("hT_lo_ready")
        ff_psum = sem("ff_psum")
        g_ready, g_hi_ready, g_lo_ready = sem("g_ready"), sem("g_hi_ready"), sem("g_lo_ready")
        y_psum, yT_ready = sem("y_psum"), sem("yT_ready")
        rows_psum = sem("rows_psum")
        stats2_ready, mv2_ready, var2_ready = sem("stats2_ready"), sem("mv2_ready"), sem("var2_ready")
        rstd2_ready, shift2_ready, yn_ready = sem("rstd2_ready"), sem("shift2_ready"), sem("yn_ready")
        gain_done, xnew_ready = sem("gain_done"), sem("xnew_ready")
        x_stored = sem("x_stored")
        begun = sem("begun")
        first_in = sem("first_in")
        z_ready, stats3_ready, mv3_ready = sem("z_ready"), sem("stats3_ready"), sem("mv3_ready")
        var3_ready, rstd3_ready, xout_ready = sem("var3_ready"), sem("rstd3_ready"), sem("xout_ready")
        out_stored = sem("out_stored")

        def run(eng, step):
            def peeled(n):
                step(n, n % 2, lambda k: (n + k) // groups if 0 <= n + k < total else None)

            for n in range(-3, 0):
                peeled(n)
            for layer in range(layers):
                base = layer * groups
                first = base + (4 if layer == layers - 1 else 2)
                end = base + groups - 4
                for n in range(base, first):
                    peeled(n)
                with eng.Fori(first, end - 1, 2) as t:
                    step(t, 0, lambda k: layer)
                    step(t + 1, 1, lambda k: layer)
                for n in range(end, base + groups):
                    peeled(n)
            peeled(total)
            peeled(total + 1)

        block = ctx.enter_context(nc.Block())

        @block.sync
        def _(sp):
            def step(n, par, layer_of):
                m = n + 3
                layer = layer_of(3)
                if layer is not None:
                    q = m % 2 if isinstance(m, int) else 1 - par
                    src = x1 if layer == 0 else x_mid[layer - 1]
                    row = m - layer * groups
                    u_ready_count = worked_out(sp, at_least_0(4 * (m - 2) + 4))
                    x_stored_count = worked_out(sp, at_least_0(16 * (m - groups) + 16)) if layer > 0 else 0
                    sp.wait_ge(begun, 1)
                    sp.wait_ge(u_ready, u_ready_count)
                    if layer > 0:
                        sp.wait_ge(x_stored, x_stored_count)
                    sp.dma_start(x[q][:, :, :], src[bass.ds(row, 1), :, :].rearrange("o p (q d) -> (o p) q d", q=Q))\
                      .then_inc(x_in[q], 16)
                    sp.dma_start(mask[q][:, :], masks[bass.ds(row, 1), :, :].rearrange("o p n -> (o p) n"))\
                      .then_inc(x_in[q], 16)
                if layer_of(-1) is not None:
                    m, layer = n - 1, layer_of(-1)
                    if layer < layers - 1:
                        xnew_ready_count = worked_out(sp, m + 1)
                        sp.wait_ge(begun, 1)
                        sp.wait_ge(xnew_ready, xnew_ready_count)
                        sp.dma_start(x_mid[layer][bass.ds(m - layer * groups, 1), :, :].rearrange("o p (q d) -> (o p) q d", q=Q),
                                     x_new[:, :, :]).then_inc(x_stored, 16)
                    else:
                        k = m - layer * groups
                        xout_ready_count = worked_out(sp, at_least_0(4 * k))
                        sp.wait_ge(begun, 1)
                        sp.wait_ge(xout_ready, xout_ready_count)
                        sp.dma_start(x_first[:, :, :], x1[bass.ds(k, 1), :, :].rearrange("o p (q d) -> (o p) q d", q=Q))\
                          .then_inc(first_in, 16)
                if layer_of(-2) == layers - 1:
                    k = n - 2 - (layers - 1) * groups
                    xout_ready_count = worked_out(sp, 4 * k + 4)
                    sp.wait_ge(begun, 1)
                    sp.wait_ge(xout_ready, xout_ready_count)
                    for i in range(Q):
                        sp.dma_start(out[bass.ds(Q * k + i, 1), :, :].rearrange("o p d -> (o p) d"),
                                     x_out[:, i, :]).then_inc(out_stored, 16)
            run(sp, step)
            sp.wait_ge(out_stored, 16 * Q * groups)
            sp.wait_ge(x_stored, 16 * (layers - 1) * groups)

        @block.gpsimd
        def _(pool):
            pool.memset(half[:, :], -0.5).then_inc(begun, 1)
            pool.wait_ge(begun, 1)

            def step(n, par, layer_of):
                if layer_of(2) is not None:
                    m = n + 2
                    x_in_count = worked_out(pool, at_least_0(16 * (m - par) + 32))
                    agg_psum_count = worked_out(pool, at_least_0(4 * (m - 1) + 4))
                    pool.wait_ge(begun, 1)
                    pool.wait_ge(x_in[par], x_in_count)
                    pool.wait_ge(agg_psum, agg_psum_count)
                    nc.gpsimd.tensor_scalar(x_hi[:, :, :], x[par][:, :, :], 1.0, 0.0, ALU.mult, ALU.add)\
                      .then_inc(x_hi_ready, 1)
                    pool.wait_ge(x_hi_ready, m + 1)
                    nc.gpsimd.tensor_tensor(x_lo[:, :, :], x[par][:, :, :], x_hi[:, :, :].bitcast(fp32), ALU.subtract)\
                      .then_inc(x_lo_ready, 1)
                if layer_of(1) is not None:
                    m = n + 1
                    pool.wait_ge(var1_ready, m + 1)
                    pool.wait_ge(un_ready, at_least_0(4 * (m - 1) + 4))
                    nc.gpsimd.tensor_tensor(rstd1[:, :], var1[:, :], half[:, :], ALU.pow).then_inc(rstd1_ready, 1)
                if layer_of(-1) is not None:
                    m, layer = n - 1, layer_of(-1)
                    pool.wait_ge(var2_ready, m + 1)
                    pool.wait_ge(yn_ready, at_least_0(4 * (m - 1) + 4))
                    nc.gpsimd.tensor_tensor(rstd2[:, :], var2[:, :], half[:, :], ALU.pow).then_inc(rstd2_ready, 1)
                if layer_of(-2) == layers - 1:
                    k = n - 2 - (layers - 1) * groups
                    pool.wait_ge(var3_ready, k + 1)
                    pool.wait_ge(xout_ready, at_least_0(4 * k))
                    nc.gpsimd.tensor_tensor(rstd3[:, :], var3[:, :], half[:, :], ALU.pow).then_inc(rstd3_ready, 1)
                if layer_of(-1) is not None:
                    m, layer = n - 1, layer_of(-1)
                    gain = mem["g2_row"][:, layer, :].unsqueeze(1).broadcast_to([P, Q, D])
                    beta = mem["beta2_row"][:, layer, :].unsqueeze(1).broadcast_to([P, Q, D])
                    pool.wait_ge(yn_ready, 4 * m + 4)
                    if layer < layers - 1:
                        pool.wait_ge(x_stored, at_least_0(16 * m))
                    else:
                        k = m - layer * groups
                        pool.wait_ge(x_stored, 16 * (layers - 1) * groups)
                        pool.wait_ge(z_ready, at_least_0(k))
                    nc.gpsimd.tensor_tensor(x_new[:, :, :], y_n[:, :, :], gain, ALU.mult).then_inc(gain_done, 1)
                    pool.wait_ge(gain_done, m + 1)
                    nc.gpsimd.tensor_tensor(x_new[:, :, :], x_new[:, :, :], beta, ALU.add).then_inc(xnew_ready, 1)
            run(pool, step)

        @block.scalar
        def _(act):
            def up(n, layer, f):
                act.wait_ge(ff_psum, 8 * n + f + 1)
                act.wait_ge(g_lo_ready, at_least_0(8 * n + f - 1))
                nc.scalar.activation(g[f % 2][:, :], ps_ff[f % 2][:, :], ACT.Gelu,
                                     bias=mem["b1"][:, layer, f:f + 1]).then_inc(g_ready, 1)
                act.wait_ge(y_psum, at_least_0(8 * n + f - 1))
                act.wait_ge(g_ready, 8 * n + f + 1)
                nc.scalar.activation(g_hi[f % 2][:, :], g[f % 2][:, :], ACT.Copy).then_inc(g_hi_ready, 1)

            def step(n, par, layer_of):
                for f in range(FT):
                    if f == 4 and layer_of(2) is not None:
                        m = n + 2
                        act.wait_ge(s_ready, m + 1)
                        act.wait_ge(sib_ready, m + 1)
                        for i in range(Q):
                            at = slice(i * P, (i + 1) * P)
                            nc.scalar.activation(s[:, at], s[:, at], ACT.Identity, bias=si_b[:, i:i + 1])\
                              .then_inc(s_biased, 1)
                    if f == 5 and layer_of(2) is not None:
                        m = n + 2
                        act.wait_ge(lrelu_ready, m + 1)
                        act.wait_ge(shift_steps, 4 * m + 4)
                        act.wait_ge(eT_psum, at_least_0(m))
                        act.wait_ge(einv_ready, at_least_0(m))
                        for i in range(Q):
                            at = slice(i * P, (i + 1) * P)
                            nc.scalar.activation(e[:, at], s[:, at], ACT.Exp, bias=shift[:, i:i + 1],
                                                 accum_out=e_sum[:, i:i + 1]).then_inc(e_ready, 1)
                    if f == 6 and layer_of(-1) is not None:
                        m = n - 1
                        act.wait_ge(shift2_ready, m + 1)
                        act.wait_ge(rstd2_ready, m + 1)
                        act.wait_ge(gain_done, at_least_0(m))
                        for i in range(Q):
                            nc.scalar.activation(y_n[:, i, :], ps_r[i // 2][:, (i % 2) * D:(i % 2 + 1) * D], ACT.Identity,
                                                 bias=shift2[:, i:i + 1], scale=rstd2[:, i:i + 1]).then_inc(yn_ready, 1)
                    if f == 7 and layer_of(1) is not None:
                        m, layer = n + 1, layer_of(1)
                        act.wait_ge(yT_ready, at_least_0(2 * (m - 2) + 2))
                        for t in range(DT):
                            act.wait_ge(hT_psum, 2 * m + t + 1)
                            nc.scalar.activation(hT[1 - par][:, t, :], ps_h[t][:, :], ACT.Identity,
                                                 bias=mem["beta1"][:, layer, t:t + 1],
                                                 scale=mem["g1"][:, layer, t:t + 1]).then_inc(hT_ready, 1)
                    if f == 7 and layer_of(2) is not None:
                        m = n + 2
                        act.wait_ge(eT_psum, m + 1)
                        act.wait_ge(agg_psum, at_least_0(4 * m))
                        nc.scalar.activation(eT_hi[:, :], ps_s[:, :], ACT.Copy).then_inc(eT_hi_ready, 1)
                    if layer_of(0) is not None:
                        up(n, layer_of(0), f)
            run(act, step)

        @block.vector
        def _(dve):
            v = nc.vector

            def low(n, f):
                dve.wait_ge(g_hi_ready, 8 * n + f + 1)
                dve.wait_ge(y_psum, at_least_0(8 * n + f - 1))
                v.tensor_tensor(g_lo[f % 2][:, :], g[f % 2][:, :], g_hi[f % 2][:, :].bitcast(fp32), ALU.subtract)\
                 .then_inc(g_lo_ready, 1)

            def mean_and_variance(stats, mv, var, stats_ready, mv_ready, var_ready, m):
                stats_ready_count = worked_out(dve, 4 * m + 4)
                dve.wait_ge(begun, 1)
                dve.wait_ge(stats_ready, stats_ready_count)
                for i in range(Q):
                    v.bn_aggr(mv[:, i, :], stats[:, i, :]).then_inc(mv_ready, 1)
                dve.wait_ge(mv_ready, 4 * m + 4)
                v.tensor_scalar(var[:, :], mv[:, :, 1], EPS, None, ALU.add).then_inc(var_ready, 1)

            def step(n, par, layer_of):
                if layer_of(-1) is not None:
                    low(n - 1, 7)
                if layer_of(2) is not None:
                    m, layer = n + 2, layer_of(2)
                    dve.wait_ge(x_in[par], 16 * (m - par) + 32)
                    dve.wait_ge(sj_spread, at_least_0(m))
                    dve.wait_ge(s_biased, at_least_0(4 * m))
                    for i in range(Q):
                        for j, dst in enumerate((si, sj)):
                            last = v.tensor_tensor_reduce(
                                out=dump[:, 2 * i + j, :], in0=x[par][:, i, :],
                                in1=mem["attn_w"][:, layer, j * D:(j + 1) * D], scale=1.0, scalar=0.0,
                                op0=ALU.mult, op1=ALU.add, accum_out=dst[:, i:i + 1])
                    last.then_inc(sij_ready, 1)
                    dve.wait_ge(sij_ready, m + 1)
                    v.tensor_scalar(si_b[:, :], si[:, :], mem["attn_b"][:, layer:layer + 1], None, ALU.add)\
                     .then_inc(sib_ready, 1)
                if layer_of(0) is not None:
                    low(n, 0)
                if layer_of(-2) == layers - 1:
                    m = n - 2
                    k = m - (layers - 1) * groups
                    dve.wait_ge(xnew_ready, m + 1)
                    dve.wait_ge(first_in, 16 * k + 16)
                    v.tensor_tensor(x_first[:, :, :], x_first[:, :, :], x_new[:, :, :], ALU.add).then_inc(z_ready, 1)
                if layer_of(-1) is not None:
                    m, layer = n - 1, layer_of(-1)
                    dve.wait_ge(y_psum, 8 * m + 8)
                    dve.wait_ge(rows_psum, at_least_0(2 * m))
                    for t in range(DT):
                        v.scalar_tensor_tensor(out=yT[:, t, :], in0=ps_y[t][:, :], scalar=mem["b2"][:, layer, t:t + 1],
                                               in1=hT[1 - par][:, t, :], op0=ALU.add, op1=ALU.add).then_inc(yT_ready, 1)
                if layer_of(0) is not None:
                    low(n, 1)
                if layer_of(1) is not None:
                    m = n + 1
                    for i in range(Q):
                        dve.wait_ge(agg_psum, 4 * m + 2 * (i // 2) + 2)
                        v.scalar_tensor_tensor(out=u[:, i, :], in0=ps_u[i // 2][:, (i % 2) * D:(i % 2 + 1) * D],
                                               scalar=e_inv[:, i:i + 1], in1=x[1 - par][:, i, :],
                                               op0=ALU.mult, op1=ALU.add).then_inc(u_ready, 1)
                    for i in range(Q):
                        dve.wait_ge(u_ready, 4 * m + i + 1)
                        v.bn_stats(stats1[:, i, :], u[:, i, :]).then_inc(stats1_ready, 1)
                    mean_and_variance(stats1, mv1, var1, stats1_ready, mv1_ready, var1_ready, m)
                if layer_of(0) is not None:
                    low(n, 2)
                if layer_of(2) is not None:
                    m = n + 2
                    sj_spread_count = worked_out(dve, at_least_0(m + 1))
                    e_ready_count = worked_out(dve, at_least_0(4 * m))
                    dve.wait_ge(begun, 1)
                    dve.wait_ge(sj_spread, sj_spread_count)
                    dve.wait_ge(e_ready, e_ready_count)
                    for i in range(Q):
                        at = slice(i * P, (i + 1) * P)
                        last = v.tensor_tensor_reduce(out=s[:, at], in0=ps_s[:, at], in1=mask[par][:, at], scale=1.0,
                                                      scalar=2 * MASKED, op0=ALU.add, op1=ALU.max,
                                                      accum_out=top[:, i:i + 1])
                    last.then_inc(s_ready, 1)
                    dve.wait_ge(s_ready, m + 1)
                    dve.wait_ge(sib_ready, m + 1)
                    v.tensor_tensor(top_s[:, :], top[:, :], si_b[:, :], ALU.add).then_inc(shift_steps, 1)
                    dve.wait_ge(shift_steps, 4 * m + 1)
                    v.tensor_scalar(top_l[:, :], top_s[:, :], 0.2, None, ALU.mult).then_inc(shift_steps, 1)
                    dve.wait_ge(shift_steps, 4 * m + 2)
                    v.tensor_tensor(top_l[:, :], top_s[:, :], top_l[:, :], ALU.max).then_inc(shift_steps, 1)
                    dve.wait_ge(shift_steps, 4 * m + 3)
                    v.tensor_scalar(shift[:, :], top_l[:, :], -1.0, None, ALU.mult).then_inc(shift_steps, 1)
                if layer_of(0) is not None:
                    low(n, 3)
                if layer_of(-1) is not None:
                    m = n - 1
                    for i in range(Q):
                        dve.wait_ge(rows_psum, 2 * m + i // 2 + 1)
                        v.bn_stats(stats2[:, i, :], ps_r[i // 2][:, (i % 2) * D:(i % 2 + 1) * D]).then_inc(stats2_ready, 1)
                    mean_and_variance(stats2, mv2, var2, stats2_ready, mv2_ready, var2_ready, m)
                if layer_of(2) is not None:
                    m = n + 2
                    dve.wait_ge(s_biased, 4 * m + 4)
                    v.scalar_tensor_tensor(out=s[:, :], in0=s[:, :], scalar=0.2, in1=s[:, :], op0=ALU.mult, op1=ALU.max)\
                     .then_inc(lrelu_ready, 1)
                if layer_of(0) is not None:
                    low(n, 4)
                if layer_of(1) is not None:
                    m = n + 1
                    dve.wait_ge(rstd1_ready, m + 1)
                    dve.wait_ge(hT_psum, at_least_0(2 * m))
                    for i in range(Q):
                        v.tensor_scalar(u_n[:, i, :], u[:, i, :], mv1[:, i, 0:1], rstd1[:, i:i + 1],
                                        ALU.subtract, ALU.mult).then_inc(un_ready, 1)
                if layer_of(-1) is not None:
                    m = n - 1
                    dve.wait_ge(rstd2_ready, m + 1)
                    dve.wait_ge(yn_ready, at_least_0(4 * m))
                    v.scalar_tensor_tensor(out=shift2[:, :], in0=mv2[:, :, 0], scalar=-1.0, in1=rstd2[:, :],
                                           op0=ALU.mult, op1=ALU.mult).then_inc(shift2_ready, 1)
                if layer_of(0) is not None:
                    low(n, 5)
                if layer_of(2) is not None:
                    m = n + 2
                    dve.wait_ge(e_ready, 4 * m + 4)
                    v.reciprocal(e_inv[:, :], e_sum[:, :]).then_inc(einv_ready, 1)
                if layer_of(-2) == layers - 1:
                    k = n - 2 - (layers - 1) * groups
                    dve.wait_ge(z_ready, k + 1)
                    for i in range(Q):
                        v.bn_stats(stats3[:, i, :], x_first[:, i, :]).then_inc(stats3_ready, 1)
                    mean_and_variance(stats3, mv3, var3, stats3_ready, mv3_ready, var3_ready, k)
                    dve.wait_ge(rstd3_ready, k + 1)
                    dve.wait_ge(out_stored, at_least_0(16 * Q * k))
                    for i in range(Q):
                        v.tensor_scalar(x_out[:, i, :], x_first[:, i, :], mv3[:, i, 0:1], rstd3[:, i:i + 1],
                                        ALU.subtract, ALU.mult).then_inc(xout_ready, 1)
                if layer_of(0) is not None:
                    low(n, 6)
                if layer_of(1) is not None:
                    m = n + 1
                    dve.wait_ge(ff_psum, at_least_0(8 * (m - 2) + 8))
                    for t in range(DT):
                        dve.wait_ge(hT_ready, 2 * m + t + 1)
                        v.tensor_copy(hT_hi[1 - par][:, t, :], hT[1 - par][:, t, :]).then_inc(hT_hi_ready, 1)
                        dve.wait_ge(hT_hi_ready, 2 * m + t + 1)
                        v.tensor_tensor(hT_lo[1 - par][:, t, :], hT[1 - par][:, t, :],
                                        hT_hi[1 - par][:, t, :].bitcast(fp32), ALU.subtract).then_inc(hT_lo_ready, 1)
                if layer_of(2) is not None:
                    m = n + 2
                    dve.wait_ge(eT_hi_ready, m + 1)
                    v.tensor_tensor(eT_lo[:, :], ps_s[:, :], eT_hi[:, :].bitcast(fp32), ALU.subtract)\
                     .then_inc(eT_lo_ready, 1)
            run(dve, step)

        @block.tensor
        def _(pe):
            def up(n, par, layer, f):
                pe.wait_ge(g_ready, at_least_0(8 * n + f - 1))
                if f == 0:
                    pe.wait_ge(hT_lo_ready, 2 * n + 2)
                at = slice(f * P, (f + 1) * P)
                parts = [(w, t, h) for t in range(DT)
                         for w, h in ((mem["w1_hi"], hT_hi), (mem["w1_hi"], hT_lo), (mem["w1_lo"], hT_hi))]
                for c, (w, t, h) in enumerate(parts):
                    last = nc.tensor.matmul(ps_ff[f % 2][:, :], w[layer][:, t, at], h[par][:, t, :],
                                            start=(c == 0), stop=(c == len(parts) - 1))
                last.then_inc(ff_psum, 1)

            def down(n, layer, f):
                pe.wait_ge(g_hi_ready, 8 * n + f + 1)
                if f == 0:
                    pe.wait_ge(yT_ready, at_least_0(2 * n))
                last = None
                for t in range(DT):
                    at = slice(t * P, (t + 1) * P)
                    nc.tensor.matmul(ps_y[t][:, :], mem["w2_hi"][layer][:, f, at], g_hi[f % 2][:, :],
                                     start=(f == 0), stop=False)
                    nc.tensor.matmul(ps_y[t][:, :], mem["w2_lo"][layer][:, f, at], g_hi[f % 2][:, :],
                                     start=False, stop=False)
                pe.wait_ge(g_lo_ready, 8 * n + f + 1)
                for t in range(DT):
                    at = slice(t * P, (t + 1) * P)
                    last = nc.tensor.matmul(ps_y[t][:, :], mem["w2_hi"][layer][:, f, at], g_lo[f % 2][:, :],
                                            start=False, stop=(f == FT - 1))
                last.then_inc(y_psum, 1)

            def step(n, par, layer_of):
                for f in range(FT):
                    if f == 7 and layer_of(1) is not None:
                        m = n + 1
                        for t in range(DT):
                            if t == 0:
                                pe.wait_ge(u_ready, 4 * m + 4)
                            else:
                                pe.wait_ge(yn_ready, at_least_0(4 * (n - 1) + 2))
                            for i in range(Q):
                                if t == 0:
                                    pe.wait_ge(un_ready, 4 * m + i + 1)
                                last = nc.tensor.transpose(ps_h[t][:, i * P:(i + 1) * P],
                                                           u_n[:, i, t * P:(t + 1) * P], ident[:, :])
                            last.then_inc(hT_psum, 1)
                    if f < 2:
                        if layer_of(-1) is not None:
                            down(n - 1, layer_of(-1), FT - 2 + f)
                    elif layer_of(0) is not None:
                        down(n, layer_of(0), f - 2)
                    if layer_of(0) is not None:
                        up(n, par, layer_of(0), f)
                    if f == 1 and layer_of(1) is not None:
                        m = n + 1
                        pe.wait_ge(x_lo_ready, m + 1)
                        pe.wait_ge(eT_lo_ready, m + 1)
                        pe.wait_ge(yn_ready, at_least_0(4 * (n - 2) + 4))
                        pe.wait_ge(hT_ready, at_least_0(2 * n + 2))
                        for i in range(Q):
                            at = slice(i * P, (i + 1) * P)
                            dst = ps_u[i // 2][:, (i % 2) * D:(i % 2 + 1) * D]
                            nc.tensor.matmul(dst, eT_hi[:, at], x_hi[:, i, :], start=True, stop=False)
                            nc.tensor.matmul(dst, eT_hi[:, at], x_lo[:, i, :], start=False, stop=False)
                            nc.tensor.matmul(dst, eT_lo[:, at], x_hi[:, i, :], start=False, stop=True)\
                              .then_inc(agg_psum, 1)
                    if f == 2 and layer_of(2) is not None:
                        m = n + 2
                        pe.wait_ge(sij_ready, m + 1)
                        pe.wait_ge(eT_lo_ready, at_least_0(m))
                        for i in range(Q):
                            last = nc.tensor.transpose(ps_s[:, i * P:(i + 1) * P],
                                                       sj[:, i:i + 1].broadcast_to([P, P]), ident[:, :])
                        last.then_inc(sj_spread, 1)
                    if f == 3 and layer_of(-1) is not None:
                        m = n - 1
                        pe.wait_ge(yT_ready, 2 * m + 2)
                        if layer_of(0) is not None:
                            pe.wait_ge(hT_ready, 2 * n + 2)
                        for b in range(2):
                            if b == 1 and layer_of(1) is not None:
                                pe.wait_ge(u_ready, 4 * (n + 1) + 2)
                            for i in (2 * b, 2 * b + 1):
                                for t in range(DT):
                                    last = nc.tensor.transpose(
                                        ps_r[b][:, (i % 2) * D + t * P:(i % 2) * D + (t + 1) * P],
                                        yT[:, t, i * P:(i + 1) * P], ident[:, :])
                            last.then_inc(rows_psum, 1)
                    if f == 6 and layer_of(2) is not None:
                        m = n + 2
                        pe.wait_ge(s_ready, m + 1)
                        for i in range(Q):
                            pe.wait_ge(e_ready, 4 * m + i + 1)
                            last = nc.tensor.transpose(ps_s[:, i * P:(i + 1) * P], e[:, i * P:(i + 1) * P], ident[:, :])
                        last.then_inc(eT_psum, 1)
            run(pe, step)
HEADS = 8
HD = D // HEADS
HALF = HEADS // 2
STACK = 3 * HD
SCALE = HD ** -0.5


def first_layer(nc, mem, groups, x_in_dram, adj_dram, weights, x1, masks):
    ctx = ExitStack()
    with ctx:
        def sb(name, shape, dt=fp32):
            return ctx.enter_context(nc.sbuf_tensor("l0_" + name, shape, dt))

        def bank(name):
            return ctx.enter_context(nc.psum_tensor("l0_" + name, [P, R], fp32))

        def sem(name):
            return ctx.enter_context(nc.semaphore("l0_" + name))

        ident = mem["ident"]
        w_raw = sb("w_raw", [P, 4, DT, D])
        w_hi = sb("w_hi", [P, 4, DT, D], fp32r)
        w_lo = sb("w_lo", [P, 4, DT, D], fp32r)
        xp = sb("xp", [P, Q, D])
        adj = sb("adj", [P, Q, P], mybir.dt.int32)
        reach = sb("reach", [P, Q, P])
        mask0 = [sb(f"mask0_{i}", [P, Q, P], bf16) for i in range(2)]
        mask1 = sb("mask1", [P, Q, P], bf16)
        xT_hi = sb("xT_hi", [P, DT, R], fp32r)
        xT_lo = sb("xT_lo", [P, DT, R], fp32r)
        qk_hi = sb("qk_hi", [P, 2 * DT, R], fp32r)
        qk_lo = sb("qk_lo", [P, 2 * DT, R], fp32r)
        q_st = sb("q_st", [STACK, DT, HALF, R], fp32r)
        k_st = sb("k_st", [STACK, DT, HALF, R], fp32r)
        v_hi = [sb(f"v_hi{i}", [P, Q, D], fp32r) for i in range(2)]
        v_lo = [sb(f"v_lo{i}", [P, Q, D], fp32r) for i in range(2)]
        s = sb("s0", [P, HEADS, P])
        top = sb("top0", [P, HEADS])
        shift = sb("shift0", [P, HEADS])
        e = sb("e0", [P, HEADS, P])
        e_sum = sb("e_sum0", [P, HEADS])
        e_inv = sb("e_inv0", [P, 2, HEADS])
        pT_hi = sb("pT_hi", [P, DT, R], fp32r)
        pT_lo = sb("pT_lo", [P, DT, R], fp32r)
        o = [sb(f"o{i}", [P, Q, D]) for i in range(2)]
        oT_hi = sb("oT_hi", [P, DT, R], fp32r)
        oT_lo = sb("oT_lo", [P, DT, R], fp32r)
        xo = sb("xo", [P, Q, D])
        y = sb("y0", [P, Q, D])
        stats = sb("stats0", [P, Q, 6])
        mv = sb("mv0", [P, Q, 2])
        var = sb("var0", [P, Q])
        rstd = sb("rstd0", [P, Q])
        yn = sb("yn0", [P, Q, D])
        half = sb("half0", [P, Q])

        ps_s = [bank(f"ps_s{i}") for i in range(DT)]
        ps_t = [bank(f"ps_t{i}") for i in range(DT)]
        ps_o = bank("ps_o")
        ps_r = [bank(f"ps_r{i}") for i in range(3)]

        w_in, w_hi_ready, w_lo_ready = sem("w_in"), sem("w_hi_ready"), sem("w_lo_ready")
        begun = sem("begun")
        xp_in, xo_in, stack_a_in, stack_b_in = sem("xp_in"), sem("xo_in"), sem("stack_a_in"), sem("stack_b_in")
        mask0_ready, reach_ready, mask1_ready, mask1_stored = (
            sem("mask0_ready"), sem("reach_ready"), sem("mask1_ready"), sem("mask1_stored"))
        xT_psum, xT_hi_ready, xT_lo_ready = sem("xT_psum"), sem("xT_hi_ready"), sem("xT_lo_ready")
        qk_psum, qk_hi_ready, qk_lo_ready = sem("qk_psum"), sem("qk_hi_ready"), sem("qk_lo_ready")
        v_psum, v_hi_ready, v_lo_ready = sem("v_psum"), sem("v_hi_ready"), sem("v_lo_ready")
        s_psum, s_ready, shift_ready = sem("s0_psum"), sem("s0_ready"), sem("shift0_ready")
        e_ready, e_inv_ready = sem("e0_ready"), sem("e_inv0_ready")
        pT_psum, pT_hi_ready, pT_lo_ready = sem("pT_psum"), sem("pT_hi_ready"), sem("pT_lo_ready")
        o_psum, o_ready = sem("o_psum"), sem("o_ready")
        oT_psum, oT_hi_ready, oT_lo_ready = sem("oT_psum"), sem("oT_hi_ready"), sem("oT_lo_ready")
        w_psum, y_ready = sem("w_psum"), sem("y_ready")
        stats_ready, mv_ready, var_ready = sem("stats0_ready"), sem("mv0_ready"), sem("var0_ready")
        rstd_ready, yn_ready, x1_stored = sem("rstd0_ready"), sem("yn0_ready"), sem("x1_stored")

        def run(eng, step):
            def peeled(n):
                step(n, n % 2, lambda k: 0 <= n + k < groups)

            for n in range(-1, 2):
                peeled(n)
            if groups > 6:
                with eng.Fori(2, groups - 3, 2) as t:
                    step(t, 0, lambda k: True)
                    step(t + 1, 1, lambda k: True)
            else:
                for n in range(2, groups - 2):
                    peeled(n)
            for n in range(groups - 2, groups + 1):
                peeled(n)

        def upto(count, limit):
            return min(count, limit) if isinstance(count, int) else count

        block = ctx.enter_context(nc.Block())

        @block.sync
        def _(sp):
            for j, w in enumerate(weights):
                sp.dma_start(w_raw[:, j, :, :], w.rearrange("(t p) n -> p t n", p=P)).then_inc(w_in, 16)

            def load(m):
                row = Q * m
                sp.dma_start(xp[:, :, :], x_in_dram[bass.ds(row, Q), :, :].rearrange("q p d -> p q d")).then_inc(xp_in, 16)
                sp.dma_start(adj[:, :, :], adj_dram[bass.ds(row, Q), :, :].rearrange("q p n -> p q n")).then_inc(xp_in, 16)

            def stack(m, sem, pair):
                at = slice(pair * 2 * P, (pair + 1) * 2 * P)
                for h in range(HALF):
                    rows = slice(h * HD, (h + 1) * HD)
                    for dst, part, srcs in ((q_st, 0, (qk_hi, qk_hi, qk_lo)), (k_st, DT, (qk_hi, qk_lo, qk_hi))):
                        for b, src in enumerate(srcs):
                            sp.dma_start(dst[b * HD:(b + 1) * HD, :, h, at].bitcast(fp32),
                                         src[rows, part:part + DT, at].bitcast(fp32)).then_inc(sem, 16)

            load(0)

            def step(n, par, has):
                if has(1):
                    m = n + 1
                    if has(2):
                        xT_psum_count = worked_out(sp, 2 * m + 2)
                        mask1_ready_count = worked_out(sp, m + 1)
                        sp.wait_ge(begun, 1)
                        sp.wait_ge(xT_psum, xT_psum_count)
                        sp.wait_ge(mask1_ready, mask1_ready_count)
                        load(m + 1)
                    mask1_ready_count = worked_out(sp, m + 1)
                    sp.wait_ge(begun, 1)
                    sp.wait_ge(mask1_ready, mask1_ready_count)
                    sp.dma_start(masks[bass.ds(m, 1), :, :].rearrange("o p n -> (o p) n"),
                                 mask1[:, :, :].rearrange("p q n -> p (q n)")).then_inc(mask1_stored, 16)
                if has(-1):
                    m = n - 1
                    y_ready_count = worked_out(sp, at_least_0(2 * m))
                    sp.wait_ge(begun, 1)
                    sp.wait_ge(y_ready, y_ready_count)
                    sp.dma_start(xo[:, :, :], x_in_dram[bass.ds(Q * m, Q), :, :].rearrange("q p d -> p q d")).then_inc(xo_in, 16)
                if has(1):
                    m = n + 1
                    qk_lo_ready_count = worked_out(sp, at_least_0(4 * m + 4))
                    s_psum_count = worked_out(sp, at_least_0(4 * n + 2))
                    sp.wait_ge(begun, 1)
                    sp.wait_ge(qk_lo_ready, qk_lo_ready_count)
                    sp.wait_ge(s_psum, s_psum_count)
                    stack(m, stack_a_in, 0)
                    s_psum_count = worked_out(sp, at_least_0(4 * n + 4))
                    sp.wait_ge(begun, 1)
                    sp.wait_ge(s_psum, s_psum_count)
                    stack(m, stack_b_in, 1)
                if has(-1):
                    m = n - 1
                    yn_ready_count = worked_out(sp, 4 * m + 4)
                    sp.wait_ge(begun, 1)
                    sp.wait_ge(yn_ready, yn_ready_count)
                    sp.dma_start(x1[bass.ds(m, 1), :, :].rearrange("o p n -> (o p) n"),
                                 yn[:, :, :].rearrange("p q d -> p (q d)")).then_inc(x1_stored, 16)
            run(sp, step)
            sp.wait_ge(x1_stored, 16 * groups)
            sp.wait_ge(mask1_stored, 16 * groups)

        @block.gpsimd
        def _(pool):
            pool.memset(half[:, :], -0.5).then_inc(begun, 1)
            pool.wait_ge(begun, 1)

            def step(n, par, has):
                if has(-1):
                    m = n - 1
                    pool.wait_ge(var_ready, m + 1)
                    pool.wait_ge(yn_ready, at_least_0(4 * m))
                    nc.gpsimd.tensor_tensor(rstd[:, :], var[:, :], half[:, :], ALU.pow).then_inc(rstd_ready, 1)
                    pool.wait_ge(rstd_ready, m + 1)
            run(pool, step)

        @block.scalar
        def _(act):
            def copy(dst, src, ready):
                nc.scalar.activation(dst, src, ACT.Copy).then_inc(ready, 1)

            def step(n, par, has):
                for i in range(Q):
                    gi = 4 * n + i
                    if has(-1) if i == 0 else has(0):
                        act.wait_ge(pT_psum, gi)
                        act.wait_ge(o_psum, at_least_0(gi - 1))
                        for t in range(DT):
                            copy(pT_hi[:, t, :], ps_t[t][:, :], pT_hi_ready)
                    if i == 0 and has(1):
                        m = n + 1
                        act.wait_ge(v_psum, at_least_0(2 * m))
                        for t in range(DT):
                            act.wait_ge(xT_psum, 2 * m + t + 1)
                            copy(xT_hi[:, t, :], ps_r[t][:, :], xT_hi_ready)
                    if i == 1 and has(1):
                        m = n + 1
                        act.wait_ge(stack_a_in, at_least_0(384 * m))
                        act.wait_ge(stack_b_in, at_least_0(384 * m))
                        for c in range(4):
                            act.wait_ge(qk_psum, 4 * m + c + 1)
                            copy(qk_hi[:, c, :], ps_r[(2 + c) % 3][:, :], qk_hi_ready)
                    if i == 2 and has(-1):
                        m = n - 1
                        act.wait_ge(w_psum, at_least_0(2 * m))
                        for t in range(DT):
                            act.wait_ge(oT_psum, 2 * m + t + 1)
                            copy(oT_hi[:, t, :], ps_r[t][:, :], oT_hi_ready)
                    if i == 2 and has(1):
                        m = n + 1
                        act.wait_ge(o_psum, at_least_0(4 * n))
                        for b in range(2):
                            act.wait_ge(v_psum, 2 * m + b + 1)
                            copy(v_hi[1 - par][:, 2 * b:2 * b + 2, :], ps_r[(2 + b) % 3][:, :].rearrange("p (q d) -> p q d", q=2),
                                 v_hi_ready)
                    if has(0):
                        act.wait_ge(shift_ready, gi + 1)
                        act.wait_ge(pT_psum, at_least_0(gi))
                        act.wait_ge(e_inv_ready, at_least_0(gi))
                        for h in range(HEADS):
                            nc.scalar.activation(e[:, h, :], s[:, h, :], ACT.Exp, bias=shift[:, h:h + 1], scale=SCALE,
                                                 accum_out=e_sum[:, h:h + 1]).then_inc(e_ready, 1)
            run(act, step)

        @block.vector
        def _(dve):
            v = nc.vector
            dve.wait_ge(w_in, 64)
            for j in range(4):
                v.tensor_copy(w_hi[:, j, :, :], w_raw[:, j, :, :]).then_inc(w_hi_ready, 1)
            for j in range(4):
                dve.wait_ge(w_hi_ready, j + 1)
                v.tensor_tensor(w_lo[:, j, :, :], w_raw[:, j, :, :], w_hi[:, j, :, :].bitcast(fp32), ALU.subtract)\
                 .then_inc(w_lo_ready, 1)

            def low(dst, src, hi, ready):
                v.tensor_tensor(dst, src, hi.bitcast(fp32), ALU.subtract).then_inc(ready, 1)

            def step(n, par, has):
                for i in range(Q):
                    gi = 4 * n + i
                    if has(0):
                        s_psum_count = worked_out(dve, at_least_0(gi + 1))
                        e_ready_count = worked_out(dve, at_least_0(8 * gi))
                        dve.wait_ge(begun, 1)
                        dve.wait_ge(s_psum, s_psum_count)
                        dve.wait_ge(e_ready, e_ready_count)
                        for h in range(HEADS):
                            last = v.tensor_tensor_reduce(
                                out=s[:, h, :], in0=ps_s[h // HALF][:, (h % HALF) * P:(h % HALF + 1) * P],
                                in1=mask0[par][:, i, :], scale=1.0, scalar=2 * MASKED, op0=ALU.add, op1=ALU.max,
                                accum_out=top[:, h:h + 1])
                        last.then_inc(s_ready, 1)
                        dve.wait_ge(s_ready, gi + 1)
                        v.tensor_scalar(shift[:, :], top[:, :], -SCALE, None, ALU.mult).then_inc(shift_ready, 1)
                    if has(-1) if i == 0 else has(0):
                        for t in range(DT):
                            dve.wait_ge(pT_hi_ready, 2 * (gi - 1) + t + 1)
                            low(pT_lo[:, t, :], ps_t[t][:, :], pT_hi[:, t, :], pT_lo_ready)
                    if has(-1) if i < 2 else has(0):
                        k = (i - 2) % Q
                        q = par if i >= 2 else 1 - par
                        dve.wait_ge(o_psum, gi - 1)
                        dve.wait_ge(e_inv_ready, gi - 1)
                        v.scalar_tensor_tensor(
                            out=o[q][:, k, :].rearrange("p (h c) -> p h c", h=HEADS),
                            in0=ps_o[:, 0:D].rearrange("p (h c) -> p h c", h=HEADS), scalar=0.0,
                            in1=e_inv[:, i % 2, :].unsqueeze(2).broadcast_to([P, HEADS, HD]), op0=ALU.max, op1=ALU.mult)\
                         .then_inc(o_ready, 1)
                    if has(-1) if i == 0 else has(0):
                        dve.wait_ge(e_ready, 8 * gi)
                        dve.wait_ge(o_ready, at_least_0(gi - 2))
                        v.reciprocal(e_inv[:, (i - 1) % 2, :], e_sum[:, :]).then_inc(e_inv_ready, 1)
                    if i == 0 and has(1):
                        m = n + 1
                        for t in range(DT):
                            dve.wait_ge(xT_hi_ready, 2 * m + t + 1)
                            low(xT_lo[:, t, :], ps_r[t][:, :], xT_hi[:, t, :], xT_lo_ready)
                        dve.wait_ge(xp_in, 32 * m + 32)
                        v.tensor_scalar(mask0[1 - par][:, :, :], adj[:, :, :], 0.0, MASKED, ALU.is_equal, ALU.mult)\
                         .then_inc(mask0_ready, 1)
                        v.tensor_tensor(reach[:, :, :], adj[:, :, :], ident[:, :].unsqueeze(1).broadcast_to([P, Q, P]),
                                        ALU.add).then_inc(reach_ready, 1)
                        dve.wait_ge(reach_ready, m + 1)
                        dve.wait_ge(mask1_stored, at_least_0(16 * m))
                        v.tensor_scalar(mask1[:, :, :], reach[:, :, :], 0.0, MASKED, ALU.is_le, ALU.mult)\
                         .then_inc(mask1_ready, 1)
                    if i == 1 and has(1):
                        m = n + 1
                        for c in range(4):
                            dve.wait_ge(qk_hi_ready, 4 * m + c + 1)
                            low(qk_lo[:, c, :], ps_r[(2 + c) % 3][:, :], qk_hi[:, c, :], qk_lo_ready)
                    if i == 2 and has(-1):
                        m = n - 1
                        for t in range(DT):
                            dve.wait_ge(oT_hi_ready, 2 * m + t + 1)
                            low(oT_lo[:, t, :], ps_r[t][:, :], oT_hi[:, t, :], oT_lo_ready)
                    if i == 2 and has(1):
                        m = n + 1
                        for b in range(2):
                            at = slice(2 * b, 2 * b + 2)
                            dve.wait_ge(v_hi_ready, 2 * m + b + 1)
                            low(v_lo[1 - par][:, at, :], ps_r[(2 + b) % 3][:, :].rearrange("p (q d) -> p q d", q=2),
                                v_hi[1 - par][:, at, :], v_lo_ready)
                    if i == 3 and has(-1):
                        m = n - 1
                        dve.wait_ge(xo_in, 16 * m + 16)
                        for b in range(2):
                            at = slice(2 * b, 2 * b + 2)
                            dve.wait_ge(w_psum, 2 * m + b + 1)
                            v.tensor_tensor(y[:, at, :], ps_r[1 + b][:, :].rearrange("p (q d) -> p q d", q=2),
                                            xo[:, at, :], ALU.add).then_inc(y_ready, 1)
                        for q in range(Q):
                            dve.wait_ge(y_ready, 2 * m + q // 2 + 1)
                            v.bn_stats(stats[:, q, :], y[:, q, :]).then_inc(stats_ready, 1)
                        stats_ready_count = worked_out(dve, 4 * m + 4)
                        dve.wait_ge(begun, 1)
                        dve.wait_ge(stats_ready, stats_ready_count)
                        for q in range(Q):
                            v.bn_aggr(mv[:, q, :], stats[:, q, :]).then_inc(mv_ready, 1)
                        dve.wait_ge(mv_ready, 4 * m + 4)
                        v.tensor_scalar(var[:, :], mv[:, :, 1], EPS, None, ALU.add).then_inc(var_ready, 1)
                        dve.wait_ge(rstd_ready, m + 1)
                        dve.wait_ge(x1_stored, at_least_0(16 * m))
                        for q in range(Q):
                            v.tensor_scalar(yn[:, q, :], y[:, q, :], mv[:, q, 0:1], rstd[:, q:q + 1],
                                            ALU.subtract, ALU.mult).then_inc(yn_ready, 1)
            run(dve, step)

        @block.tensor
        def _(pe):
            def split_product(dst, pairs, signal):
                n = 3 * len(pairs)
                c = 0
                for (l_hi, l_lo), (r_hi, r_lo) in pairs:
                    for left, right in ((l_hi, r_hi), (l_hi, r_lo), (l_lo, r_hi)):
                        last = nc.tensor.matmul(dst, left, right, start=(c == 0), stop=(c == n - 1))
                        c += 1
                if signal is not None:
                    last.then_inc(signal, 1)

            def transposes(dst, srcs, signal):
                for j, src in enumerate(srcs):
                    last = nc.tensor.transpose(dst[:, j * P:(j + 1) * P], src, ident[:, :])
                last.then_inc(signal, 1)

            def step(n, par, has):
                for i in range(Q):
                    gi = 4 * n + i
                    if has(0):
                        pe.wait_ge(stack_a_in if i < 2 else stack_b_in, 384 * n + 384)
                        pe.wait_ge(s_ready, at_least_0(gi))
                        for h in range(HEADS):
                            at = slice(i * P, (i + 1) * P)
                            last = nc.tensor.matmul(ps_s[h // HALF][:, (h % HALF) * P:(h % HALF + 1) * P],
                                                    q_st[:, h // HALF, h % HALF, at], k_st[:, h // HALF, h % HALF, at],
                                                    start=True, stop=True)
                        last.then_inc(s_psum, 1)
                    if has(-1) if i < 2 else has(0):
                        k = (i - 2) % Q
                        q = par if i >= 2 else 1 - par
                        pe.wait_ge(pT_lo_ready, 2 * (gi - 2) + 2)
                        pe.wait_ge(o_ready, at_least_0(gi - 2))
                        if i == 2:
                            pe.wait_ge(v_lo_ready, 2 * n + 2)
                        for h in range(HEADS):
                            at = slice((h % HALF) * P, (h % HALF + 1) * P)
                            cols = slice(h * HD, (h + 1) * HD)
                            split_product(ps_o[:, cols], [((pT_hi[:, h // HALF, at], pT_lo[:, h // HALF, at]),
                                                           (v_hi[q][:, k, cols], v_lo[q][:, k, cols]))],
                                          o_psum if h == HEADS - 1 else None)
                    if has(-1) if i == 0 else has(0):
                        pe.wait_ge(pT_lo_ready, at_least_0(2 * (gi - 1)))
                        for t in range(DT):
                            for j in range(HALF):
                                pe.wait_ge(e_ready, 8 * (gi - 1) + HALF * t + j + 1)
                                last = nc.tensor.transpose(ps_t[t][:, j * P:(j + 1) * P], e[:, HALF * t + j, :], ident[:, :])
                        last.then_inc(pT_psum, 1)
                    if i == 0 and has(1):
                        m = n + 1
                        pe.wait_ge(xp_in, 32 * m + 32)
                        for t in range(DT):
                            if t == 0:
                                pe.wait_ge(v_lo_ready, at_least_0(2 * m))
                            else:
                                pe.wait_ge(y_ready, at_least_0(2 * (n - 2) + 1))
                            transposes(ps_r[t], [xp[:, q, t * P:(t + 1) * P] for q in range(Q)], xT_psum)
                    if i == 1 and has(1):
                        m = n + 1
                        if isinstance(n, int):
                            pe.wait_ge(w_lo_ready, 4)
                        pe.wait_ge(xT_lo_ready, 2 * m + 2)
                        pe.wait_ge(y_ready, at_least_0(2 * (n - 2) + 2))
                        for c in range(4):
                            if c == 3:
                                pe.wait_ge(qk_lo_ready, 4 * m + 1)
                            at = slice((c % 2) * P, (c % 2 + 1) * P)
                            split_product(ps_r[(2 + c) % 3][:, :],
                                          [((w_hi[:, c // 2, t, at], w_lo[:, c // 2, t, at]),
                                            (xT_hi[:, t, :], xT_lo[:, t, :])) for t in range(DT)], qk_psum)
                    if i == 2 and has(-1):
                        m = n - 1
                        pe.wait_ge(o_ready, 4 * m + 4)
                        for t in range(DT):
                            pe.wait_ge(qk_lo_ready, upto(4 * (n + 1) + 2 + t, 4 * groups))
                            transposes(ps_r[t], [o[1 - par][:, q, t * P:(t + 1) * P] for q in range(Q)], oT_psum)
                    if i == 2 and has(1):
                        m = n + 1
                        for b in range(2):
                            if b == 0:
                                pe.wait_ge(qk_lo_ready, 4 * m + 4)
                            else:
                                pe.wait_ge(oT_lo_ready, at_least_0(2 * (n - 1) + 1))
                            for q in (2 * b, 2 * b + 1):
                                rows = slice(q * P, (q + 1) * P)
                                split_product(ps_r[(2 + b) % 3][:, (q % 2) * D:(q % 2 + 1) * D],
                                              [((xT_hi[:, t, rows], xT_lo[:, t, rows]),
                                                (w_hi[:, 2, t, :], w_lo[:, 2, t, :])) for t in range(DT)],
                                              v_psum if q % 2 else None)
                    if i == 3 and has(-1):
                        m = n - 1
                        pe.wait_ge(oT_lo_ready, 2 * m + 2)
                        pe.wait_ge(v_lo_ready, upto(2 * (n + 1) + 1, 2 * groups))
                        for b in range(2):
                            for q in (2 * b, 2 * b + 1):
                                rows = slice(q * P, (q + 1) * P)
                                split_product(ps_r[1 + b][:, (q % 2) * D:(q % 2 + 1) * D],
                                              [((oT_hi[:, t, rows], oT_lo[:, t, rows]),
                                                (w_hi[:, 3, t, :], w_lo[:, 3, t, :])) for t in range(DT)],
                                              w_psum if q % 2 else None)
            run(pe, step)
def load_constants(nc, mem, layers, raw):
    with ExitStack() as ctx:
        def sem(name):
            return ctx.enter_context(nc.semaphore(name))

        stage = [ctx.enter_context(nc.sbuf_tensor(f"stage{i}", [P, DT * FF], fp32)) for i in range(2)]
        stage_in = [sem(f"stage_in{i}") for i in range(2)]
        consts_in, hi_ready, lo_ready = sem("consts_in"), sem("hi_ready"), sem("lo_ready")
        pieces = []
        for l in range(layers):
            pieces.append((raw["W1"][l, :, :].rearrange("(t p) n -> p t n", p=P), mem["w1_hi"][l], mem["w1_lo"][l], DT))
            pieces.append((raw["W2"][l, :, :].rearrange("(t p) n -> p t n", p=P), mem["w2_hi"][l], mem["w2_lo"][l], FT))
        block = ctx.enter_context(nc.Block())

        @block.sync
        def _(sp):
            for i, (src, _, _, t) in enumerate(pieces):
                if i >= 2:
                    sp.wait_ge(lo_ready, i - 1)
                sp.dma_start(stage[i % 2][:, :].rearrange("p (t n) -> p t n", t=t), src).then_inc(stage_in[i % 2], 16)

        @block.scalar
        def _(act):
            count = 0
            for dst, src in ((mem["attn_w"][:, :, :], raw["attn_w"]), (mem["attn_b"][:, :], raw["attn_b"]),
                             (mem["g2_row"][:, :, :], raw["g2"]), (mem["beta2_row"][:, :, :], raw["beta2"])):
                act.dma_start(dst, src.partition_broadcast(P)).then_inc(consts_in, 16)
                count += 16
            for name in ("g1", "beta1", "b1", "b2"):
                for l in range(layers):
                    act.dma_start(mem[name][:, l, :], raw[name][l, :].rearrange("(t p) -> p t", p=P),
                                  allow_slow_non_contiguous=True).then_inc(consts_in, 16)
                    count += 16
            act.wait_ge(consts_in, count)

        @block.vector
        def _(dve):
            for i, (_, hi, lo, t) in enumerate(pieces):
                src = stage[i % 2][:, :].rearrange("p (t n) -> p t n", t=t)
                dve.wait_ge(stage_in[i % 2], 16 * (i // 2 + 1))
                nc.vector.tensor_copy(hi[:, :, :], src).then_inc(hi_ready, 1)
                dve.wait_ge(hi_ready, i + 1)
                nc.vector.tensor_tensor(lo[:, :, :], src, hi[:, :, :].bitcast(fp32), ALU.subtract).then_inc(lo_ready, 1)


def program(nc, x, adj, Wq, Wk, Wv, Wo, attn_w, attn_b, W1, b1, W2, b2, g1, beta1, g2, beta2, out):
    graphs = x.shape[0]
    groups = graphs // Q
    layers = attn_w.shape[0]
    x1 = nc.dram_tensor("x1_kept", (groups, P, Q * D), fp32, kind="Internal").ap()
    masks = nc.dram_tensor("masks_kept", (groups, P, Q * P), bf16, kind="Internal").ap()
    x_mid = [nc.dram_tensor(f"x_kept{i}", (groups, P, Q * D), fp32, kind="Internal").ap() for i in range(layers - 1)]
    raw = dict(W1=W1, W2=W2, attn_w=attn_w, attn_b=attn_b, g1=g1, beta1=beta1, g2=g2, beta2=beta2, b1=b1, b2=b2)
    with ExitStack() as ctx:
        def sb(name, shape, dt=fp32):
            return ctx.enter_context(nc.sbuf_tensor(name, shape, dt))

        mem = {"ident": sb("ident", [P, P])}
        ident_ready = ctx.enter_context(nc.semaphore("ident_ready"))
        with nc.Block() as block:
            @block.gpsimd
            def _(pool):
                pool.memset(mem["ident"][:, :], 0.0).then_inc(ident_ready, 1)
                pool.wait_ge(ident_ready, 1)
                pool.affine_select(out=mem["ident"][:, :], in_=mem["ident"][:, :], compare_op=ALU.not_equal, fill=1.0,
                                   base=0, pattern=[[-1, P]], channel_multiplier=1).then_inc(ident_ready, 1)
        first_layer(nc, mem, groups, x, adj, (Wq, Wk, Wv, Wo), x1, masks)
        mem["attn_w"] = sb("attn_w_row", [P, layers, 2 * D])
        mem["attn_b"] = sb("attn_b_row", [P, layers])
        mem["g2_row"] = sb("g2_row", [P, layers, D])
        mem["beta2_row"] = sb("beta2_row", [P, layers, D])
        for name, tiles in (("g1", DT), ("beta1", DT), ("b2", DT), ("b1", FT)):
            mem[name] = sb(f"{name}_col", [P, layers, tiles])
        for part in ("hi", "lo"):
            mem[f"w1_{part}"] = [sb(f"w1_{part}{l}", [P, DT, FF], fp32r) for l in range(layers)]
            mem[f"w2_{part}"] = [sb(f"w2_{part}{l}", [P, FT, D], fp32r) for l in range(layers)]
        load_constants(nc, mem, layers, raw)
        gnn_layers(nc, mem, layers, groups, x1, masks, x_mid, out)


_INS = ["x", "adj", "L0_gnn_Wq", "L0_gnn_Wk", "L0_gnn_Wv", "L0_gnn_Wo", "L1_gnn_attn_w", "L1_gnn_attn_b",
        "L1_gnn_W1", "L1_gnn_b1", "L1_gnn_W2", "L1_gnn_b2", "L1_gnn_g1", "L1_gnn_beta1", "L1_gnn_g2", "L1_gnn_beta2"]


def kernel(**inputs):
    import numpy as _np
    import concourse.bacc as _bacc
    from concourse import mybir as _mybir
    from concourse.bass_utils import run_bass_kernel_spmd as _run

    nc = _bacc.Bacc("TRN2", target_bir_lowering=False, num_devices=1)
    arrays, args = {}, []
    for name in _INS:
        a = _np.ascontiguousarray(inputs[name])
        arrays[f"in_{name}"] = a
        args.append(nc.dram_tensor(f"in_{name}", a.shape, _mybir.dt.from_np(a.dtype), kind="ExternalInput").ap())
    shape = tuple(inputs["x"].shape)
    args.append(nc.dram_tensor("result", shape, _mybir.dt.float32, kind="ExternalOutput").ap())
    program(nc, *args)
    r = _run(nc, [arrays], core_ids=[0])
    return r.results[0]["result"]
```

```python
import concourse.bass as bass
from concourse import mybir
from contextlib import ExitStack

fp32 = mybir.dt.float32
fp32r = mybir.dt.float32r
bf16 = mybir.dt.bfloat16
ALU = mybir.AluOpType
ACT = mybir.ActivationFunctionType

P = 128
Q = 4
R = Q * P
D = 256
DT = D // P
FF = 1024
FT = FF // P
EPS = 1e-5
MASKED = -1e30

AT_BIAS, AT_EXP, AT_YN, AT_HT = 1, 2, 5, 6
AT_ROWS, AT_ET, AT_HT_PE = 3, 4, 6


def at_least_0(count):
    return max(count, 0) if isinstance(count, int) else count


def worked_out(eng, count):
    return count if isinstance(count, int) else eng.to_reg(count)


def gnn_layers(nc, mem, layers, groups, x1, masks, x_mid, out):
    total = layers * groups
    ctx = ExitStack()
    with ctx:
        def sb(name, shape, dt=fp32):
            return ctx.enter_context(nc.sbuf_tensor(name, shape, dt))

        def bank(name, dt=fp32):
            return ctx.enter_context(nc.psum_tensor(name, [P, R], dt))

        def sem(name):
            return ctx.enter_context(nc.semaphore(name))

        ident = mem["ident"]
        x = [sb(f"x{i}", [P, Q, D]) for i in range(2)]
        mask = [sb(f"mask{i}", [P, R], bf16) for i in range(2)]
        x_hi = sb("x_hi", [P, Q, D], fp32r)
        x_lo = sb("x_lo", [P, Q, D], fp32r)
        dump = sb("dump", [P, 2 * Q, D], bf16)
        si = sb("si", [P, Q])
        sj = sb("sj", [P, Q])
        si_b = sb("si_b", [P, Q])
        top = sb("top", [P, Q])
        top_n = sb("top_n", [P, Q])
        shift = sb("shift", [P, Q])
        s = sb("s", [P, R])
        e = sb("e", [P, R])
        e_sum = sb("e_sum", [P, Q])
        e_inv = sb("e_inv", [P, Q])
        eT_hi = sb("eT_hi", [P, R], fp32r)
        eT_lo = sb("eT_lo", [P, R], fp32r)
        u = sb("u", [P, Q, D])
        u_n = sb("u_n", [P, Q, D])
        stats1 = sb("stats1", [P, Q, 6])
        mv1 = sb("mv1", [P, Q, 2])
        var1 = sb("var1", [P, Q])
        rstd1 = sb("rstd1", [P, Q])
        hT = [sb(f"hT{i}", [P, DT, R]) for i in range(2)]
        hT_hi = [sb(f"hT_hi{i}", [P, DT, R], fp32r) for i in range(2)]
        hT_lo = [sb(f"hT_lo{i}", [P, DT, R], fp32r) for i in range(2)]
        g = [sb(f"g{i}", [P, R]) for i in range(2)]
        g_hi = [sb(f"g_hi{i}", [P, R], fp32r) for i in range(2)]
        g_lo = [sb(f"g_lo{i}", [P, R], fp32r) for i in range(2)]
        yT = sb("yT", [P, DT, R])
        stats2 = sb("stats2", [P, Q, 6])
        mv2 = sb("mv2", [P, Q, 2])
        var2 = sb("var2", [P, Q])
        rstd2 = sb("rstd2", [P, Q])
        shift2 = sb("shift2", [P, Q])
        y_n = sb("y_n", [P, Q, D])
        x_new = sb("x_new", [P, Q, D])
        x_first = sb("x_first", [P, Q, D])
        stats3 = sb("stats3", [P, Q, 6])
        mv3 = sb("mv3", [P, Q, 2])
        var3 = sb("var3", [P, Q])
        rstd3 = sb("rstd3", [P, Q])
        x_out = sb("x_out", [P, Q, D])
        half = sb("half", [P, Q])

        ps_ff = [bank(f"ps_ff{i}") for i in range(2)]
        ps_y = [bank(f"ps_y{i}") for i in range(DT)]
        ps_s = bank("ps_s")
        ps_a = bank("ps_a")
        ps_b = bank("ps_b")
        ps_c = bank("ps_c")
        ps_u = [ps_a, ps_b]
        ps_h = [ps_b, ps_c]
        ps_r = [ps_c, ps_a]

        x_in = [sem(f"x_in{i}") for i in range(2)]
        x_hi_ready, x_lo_ready = sem("x_hi_ready"), sem("x_lo_ready")
        sij_ready, sib_ready = sem("sij_ready"), sem("sib_ready")
        sj_spread = sem("sj_spread")
        s_ready = sem("s_ready")
        shift_steps = sem("shift_steps")
        s_biased, lrelu_ready, e_ready = sem("s_biased"), sem("lrelu_ready"), sem("e_ready")
        einv_ready = sem("einv_ready")
        eT_psum, eT_hi_ready, eT_lo_ready = sem("eT_psum"), sem("eT_hi_ready"), sem("eT_lo_ready")
        agg_psum = sem("agg_psum")
        u_ready, stats1_ready, mv1_ready = sem("u_ready"), sem("stats1_ready"), sem("mv1_ready")
        rstd1_ready, un_ready = sem("rstd1_ready"), sem("un_ready")
        hT_psum, hT_ready = sem("hT_psum"), sem("hT_ready")
        hT_hi_ready, hT_lo_ready = sem("hT_hi_ready"), sem("hT_lo_ready")
        ff_psum = sem("ff_psum")
        g_ready, g_hi_ready, g_lo_ready = sem("g_ready"), sem("g_hi_ready"), sem("g_lo_ready")
        y_psum, yT_ready = sem("y_psum"), sem("yT_ready")
        rows_psum = sem("rows_psum")
        stats2_ready, mv2_ready = sem("stats2_ready"), sem("mv2_ready")
        var1_ready, var2_ready, var3_ready = sem("var1_ready"), sem("var2_ready"), sem("var3_ready")
        rstd2_ready, shift2_ready, yn_ready = sem("rstd2_ready"), sem("shift2_ready"), sem("yn_ready")
        gain_done, xnew_ready = sem("gain_done"), sem("xnew_ready")
        x_stored = sem("x_stored")
        begun = sem("begun")
        first_in = sem("first_in")
        z_ready, stats3_ready, mv3_ready = sem("z_ready"), sem("stats3_ready"), sem("mv3_ready")
        rstd3_ready, xout_ready = sem("rstd3_ready"), sem("xout_ready")
        out_stored = sem("out_stored")

        def run(eng, step):
            def peeled(n):
                step(n, n % 2, lambda k: (n + k) // groups if 0 <= n + k < total else None)

            for n in range(-3, 0):
                peeled(n)
            for layer in range(layers):
                base = layer * groups
                first = base + (4 if layer == layers - 1 else 2)
                end = base + groups - 4
                for n in range(base, first):
                    peeled(n)
                with eng.Fori(first, end - 1, 2) as t:
                    step(t, 0, lambda k: layer)
                    step(t + 1, 1, lambda k: layer)
                for n in range(end, base + groups):
                    peeled(n)
            peeled(total)
            peeled(total + 1)

        block = ctx.enter_context(nc.Block())

        @block.sync
        def _(sp):
            def step(n, par, layer_of):
                m = n + 3
                layer = layer_of(3)
                if layer is not None:
                    q = m % 2 if isinstance(m, int) else 1 - par
                    src = x1 if layer == 0 else x_mid[layer - 1]
                    row = m - layer * groups
                    u_ready_count = worked_out(sp, at_least_0(4 * (m - 2) + 4))
                    x_stored_count = worked_out(sp, at_least_0(16 * (m - groups) + 16)) if layer > 0 else 0
                    sp.wait_ge(begun, 1)
                    sp.wait_ge(u_ready, u_ready_count)
                    if layer > 0:
                        sp.wait_ge(x_stored, x_stored_count)
                    sp.dma_start(x[q][:, :, :], src[bass.ds(row, 1), :, :].rearrange("o p (q d) -> (o p) q d", q=Q))\
                      .then_inc(x_in[q], 16)
                    sp.dma_start(mask[q][:, :], masks[bass.ds(row, 1), :, :].rearrange("o p n -> (o p) n"))\
                      .then_inc(x_in[q], 16)
                if layer_of(-1) is not None:
                    m, layer = n - 1, layer_of(-1)
                    if layer < layers - 1:
                        xnew_ready_count = worked_out(sp, m + 1)
                        sp.wait_ge(begun, 1)
                        sp.wait_ge(xnew_ready, xnew_ready_count)
                        sp.dma_start(x_mid[layer][bass.ds(m - layer * groups, 1), :, :].rearrange("o p (q d) -> (o p) q d", q=Q),
                                     x_new[:, :, :]).then_inc(x_stored, 16)
                    else:
                        k = m - layer * groups
                        xout_ready_count = worked_out(sp, at_least_0(4 * k))
                        sp.wait_ge(begun, 1)
                        sp.wait_ge(xout_ready, xout_ready_count)
                        sp.dma_start(x_first[:, :, :], x1[bass.ds(k, 1), :, :].rearrange("o p (q d) -> (o p) q d", q=Q))\
                          .then_inc(first_in, 16)
                if layer_of(-2) == layers - 1:
                    k = n - 2 - (layers - 1) * groups
                    xout_ready_count = worked_out(sp, 4 * k + 4)
                    sp.wait_ge(begun, 1)
                    sp.wait_ge(xout_ready, xout_ready_count)
                    for i in range(Q):
                        sp.dma_start(out[bass.ds(Q * k + i, 1), :, :].rearrange("o p d -> (o p) d"),
                                     x_out[:, i, :]).then_inc(out_stored, 16)
            run(sp, step)
            sp.wait_ge(out_stored, 16 * Q * groups)
            sp.wait_ge(x_stored, 16 * (layers - 1) * groups)

        @block.gpsimd
        def _(pool):
            pool.memset(half[:, :], -0.5).then_inc(begun, 1)
            pool.wait_ge(begun, 1)

            def inverse_deviation(rstd, var, ready):
                nc.gpsimd.tensor_tensor(rstd[:, :], var[:, :], half[:, :], ALU.pow).then_inc(ready, 1)

            def step(n, par, layer_of):
                if layer_of(2) is not None:
                    m = n + 2
                    x_in_count = worked_out(pool, 16 * (m - par) + 32)
                    agg_psum_count = worked_out(pool, at_least_0(4 * (m - 1) + 4))
                    pool.wait_ge(begun, 1)
                    pool.wait_ge(x_in[par], x_in_count)
                    pool.wait_ge(agg_psum, agg_psum_count)
                    nc.gpsimd.tensor_scalar(x_hi[:, :, :], x[par][:, :, :], 1.0, 0.0, ALU.mult, ALU.add)\
                      .then_inc(x_hi_ready, 1)
                    pool.wait_ge(x_hi_ready, m + 1)
                    nc.gpsimd.tensor_tensor(x_lo[:, :, :], x[par][:, :, :], x_hi[:, :, :].bitcast(fp32), ALU.subtract)\
                      .then_inc(x_lo_ready, 1)
                if layer_of(1) is not None:
                    m = n + 1
                    pool.wait_ge(var1_ready, m + 1)
                    pool.wait_ge(un_ready, at_least_0(4 * (m - 1) + 4))
                    inverse_deviation(rstd1, var1, rstd1_ready)
                if layer_of(-1) is not None:
                    m = n - 1
                    pool.wait_ge(var2_ready, m + 1)
                    pool.wait_ge(yn_ready, at_least_0(4 * (m - 1) + 4))
                    inverse_deviation(rstd2, var2, rstd2_ready)
                if layer_of(-2) == layers - 1:
                    k = n - 2 - (layers - 1) * groups
                    pool.wait_ge(var3_ready, k + 1)
                    pool.wait_ge(xout_ready, at_least_0(4 * k))
                    inverse_deviation(rstd3, var3, rstd3_ready)
                if layer_of(-1) is not None:
                    m, layer = n - 1, layer_of(-1)
                    gain = mem["g2_row"][:, layer, :].unsqueeze(1).broadcast_to([P, Q, D])
                    beta = mem["beta2_row"][:, layer, :].unsqueeze(1).broadcast_to([P, Q, D])
                    pool.wait_ge(yn_ready, 4 * m + 4)
                    if layer < layers - 1:
                        pool.wait_ge(x_stored, at_least_0(16 * m))
                    else:
                        k = m - layer * groups
                        pool.wait_ge(x_stored, 16 * (layers - 1) * groups)
                        pool.wait_ge(z_ready, at_least_0(k))
                    nc.gpsimd.tensor_tensor(x_new[:, :, :], y_n[:, :, :], gain, ALU.mult).then_inc(gain_done, 1)
                    pool.wait_ge(gain_done, m + 1)
                    nc.gpsimd.tensor_tensor(x_new[:, :, :], x_new[:, :, :], beta, ALU.add).then_inc(xnew_ready, 1)
                    if layer == layers - 1:
                        pool.wait_ge(xnew_ready, m + 1)
                        pool.wait_ge(first_in, 16 * k + 16)
                        nc.gpsimd.tensor_tensor(x_first[:, :, :], x_first[:, :, :], x_new[:, :, :], ALU.add)\
                          .then_inc(z_ready, 1)
            run(pool, step)

        @block.scalar
        def _(act):
            def up(n, layer, f):
                act.wait_ge(ff_psum, 8 * n + f + 1)
                act.wait_ge(g_lo_ready, at_least_0(8 * n + f - 1))
                nc.scalar.activation(g[f % 2][:, :], ps_ff[f % 2][:, :], ACT.Gelu,
                                     bias=mem["b1"][:, layer, f:f + 1]).then_inc(g_ready, 1)
                act.wait_ge(y_psum, at_least_0(8 * n + f - 1))
                act.wait_ge(g_ready, 8 * n + f + 1)
                nc.scalar.activation(g_hi[f % 2][:, :], g[f % 2][:, :], ACT.Copy).then_inc(g_hi_ready, 1)

            def step(n, par, layer_of):
                for f in range(FT):
                    if f == AT_BIAS and layer_of(2) is not None:
                        m = n + 2
                        act.wait_ge(s_ready, m + 1)
                        act.wait_ge(sib_ready, m + 1)
                        for i in range(Q):
                            at = slice(i * P, (i + 1) * P)
                            nc.scalar.activation(s[:, at], s[:, at], ACT.Identity, bias=si_b[:, i:i + 1])\
                              .then_inc(s_biased, 1)
                    if f == AT_EXP and layer_of(2) is not None:
                        m = n + 2
                        act.wait_ge(lrelu_ready, m + 1)
                        act.wait_ge(shift_steps, 2 * m + 2)
                        act.wait_ge(eT_psum, at_least_0(m))
                        act.wait_ge(einv_ready, at_least_0(m))
                        for i in range(Q):
                            at = slice(i * P, (i + 1) * P)
                            nc.scalar.activation(e[:, at], s[:, at], ACT.Exp, bias=shift[:, i:i + 1],
                                                 accum_out=e_sum[:, i:i + 1]).then_inc(e_ready, 1)
                    if f == AT_YN and layer_of(-1) is not None:
                        m = n - 1
                        act.wait_ge(shift2_ready, m + 1)
                        act.wait_ge(rstd2_ready, m + 1)
                        act.wait_ge(gain_done, at_least_0(m))
                        for i in range(Q):
                            nc.scalar.activation(y_n[:, i, :], ps_r[i // 2][:, (i % 2) * D:(i % 2 + 1) * D], ACT.Identity,
                                                 bias=shift2[:, i:i + 1], scale=rstd2[:, i:i + 1]).then_inc(yn_ready, 1)
                    if f == AT_HT and layer_of(1) is not None:
                        m, layer = n + 1, layer_of(1)
                        act.wait_ge(yT_ready, at_least_0(2 * (m - 2) + 2))
                        for t in range(DT):
                            act.wait_ge(hT_psum, 2 * m + t + 1)
                            nc.scalar.activation(hT[1 - par][:, t, :], ps_h[t][:, :], ACT.Identity,
                                                 bias=mem["beta1"][:, layer, t:t + 1],
                                                 scale=mem["g1"][:, layer, t:t + 1]).then_inc(hT_ready, 1)
                    if f == 7 and layer_of(2) is not None:
                        m = n + 2
                        act.wait_ge(eT_psum, m + 1)
                        act.wait_ge(agg_psum, at_least_0(4 * m))
                        nc.scalar.activation(eT_hi[:, :], ps_s[:, :], ACT.Copy).then_inc(eT_hi_ready, 1)
                    if layer_of(0) is not None:
                        up(n, layer_of(0), f)
            run(act, step)

        @block.vector
        def _(dve):
            v = nc.vector

            def low(n, f):
                dve.wait_ge(g_hi_ready, 8 * n + f + 1)
                dve.wait_ge(y_psum, at_least_0(8 * n + f - 1))
                v.tensor_tensor(g_lo[f % 2][:, :], g[f % 2][:, :], g_hi[f % 2][:, :].bitcast(fp32), ALU.subtract)\
                 .then_inc(g_lo_ready, 1)

            def mean_and_variance(stats, mv, var, stats_ready, mv_ready, var_ready, m):
                stats_ready_count = worked_out(dve, 4 * m + 4)
                dve.wait_ge(begun, 1)
                dve.wait_ge(stats_ready, stats_ready_count)
                for i in range(Q):
                    v.bn_aggr(mv[:, i, :], stats[:, i, :]).then_inc(mv_ready, 1)
                dve.wait_ge(mv_ready, 4 * m + 4)
                v.tensor_scalar(var[:, :], mv[:, :, 1], EPS, None, ALU.add).then_inc(var_ready, 1)

            def node_scores(m, q, layer, graphs):
                for i in graphs:
                    for j, dst in enumerate((si, sj)):
                        v.tensor_tensor_reduce(
                            out=dump[:, 2 * i + j, :], in0=x[q][:, i, :],
                            in1=mem["attn_w"][:, layer, j * D:(j + 1) * D], scale=1.0, scalar=0.0,
                            op0=ALU.mult, op1=ALU.add, accum_out=dst[:, i:i + 1]).then_inc(sij_ready, 1)

            def step(n, par, layer_of):
                if layer_of(-1) is not None:
                    low(n - 1, 7)
                if layer_of(2) is not None:
                    m = n + 2
                    sj_spread_count, e_ready_count = worked_out(dve, m + 1), worked_out(dve, at_least_0(4 * m))
                    dve.wait_ge(begun, 1)
                    dve.wait_ge(sj_spread, sj_spread_count)
                    dve.wait_ge(e_ready, e_ready_count)
                    for i in range(Q):
                        at = slice(i * P, (i + 1) * P)
                        last = v.tensor_tensor_reduce(out=s[:, at], in0=ps_s[:, at], in1=mask[par][:, at], scale=1.0,
                                                      scalar=2 * MASKED, op0=ALU.add, op1=ALU.max,
                                                      accum_out=top[:, i:i + 1])
                    last.then_inc(s_ready, 1)
                    dve.wait_ge(s_ready, m + 1)
                    dve.wait_ge(sib_ready, m + 1)
                    v.scalar_tensor_tensor(out=top_n[:, :], in0=top[:, :], scalar=-1.0, in1=si_b[:, :],
                                           op0=ALU.mult, op1=ALU.subtract).then_inc(shift_steps, 1)
                    dve.wait_ge(shift_steps, 2 * m + 1)
                    v.scalar_tensor_tensor(out=shift[:, :], in0=top_n[:, :], scalar=0.2, in1=top_n[:, :],
                                           op0=ALU.mult, op1=ALU.min).then_inc(shift_steps, 1)
                if layer_of(0) is not None:
                    low(n, 0)
                if layer_of(-1) is not None:
                    m, layer = n - 1, layer_of(-1)
                    dve.wait_ge(y_psum, 8 * m + 8)
                    dve.wait_ge(rows_psum, at_least_0(2 * m))
                    for t in range(DT):
                        v.scalar_tensor_tensor(out=yT[:, t, :], in0=ps_y[t][:, :], scalar=mem["b2"][:, layer, t:t + 1],
                                               in1=hT[1 - par][:, t, :], op0=ALU.add, op1=ALU.add).then_inc(yT_ready, 1)
                if layer_of(2) is not None:
                    m = n + 2
                    dve.wait_ge(s_biased, 4 * m + 4)
                    v.scalar_tensor_tensor(out=s[:, :], in0=s[:, :], scalar=0.2, in1=s[:, :], op0=ALU.mult, op1=ALU.max)\
                     .then_inc(lrelu_ready, 1)
                if layer_of(0) is not None:
                    low(n, 1)
                if layer_of(1) is not None:
                    m = n + 1
                    for i in range(Q):
                        dve.wait_ge(agg_psum, 4 * m + 2 * (i // 2) + 2)
                        v.scalar_tensor_tensor(out=u[:, i, :], in0=ps_u[i // 2][:, (i % 2) * D:(i % 2 + 1) * D],
                                               scalar=e_inv[:, i:i + 1], in1=x[1 - par][:, i, :],
                                               op0=ALU.mult, op1=ALU.add).then_inc(u_ready, 1)
                if layer_of(1) is not None:
                    m = n + 1
                    dve.wait_ge(rstd1_ready, at_least_0(m))
                    for i in range(Q):
                        dve.wait_ge(u_ready, 4 * m + i + 1)
                        v.bn_stats(stats1[:, i, :], u[:, i, :]).then_inc(stats1_ready, 1)
                    mean_and_variance(stats1, mv1, var1, stats1_ready, mv1_ready, var1_ready, m)
                if layer_of(-1) is not None:
                    m = n - 1
                    dve.wait_ge(rstd2_ready, at_least_0(m))
                    for i in range(Q):
                        dve.wait_ge(rows_psum, 2 * m + i // 2 + 1)
                        v.bn_stats(stats2[:, i, :], ps_r[i // 2][:, (i % 2) * D:(i % 2 + 1) * D]).then_inc(stats2_ready, 1)
                if layer_of(0) is not None:
                    low(n, 2)
                if layer_of(-1) is not None:
                    mean_and_variance(stats2, mv2, var2, stats2_ready, mv2_ready, var2_ready, m)
                if layer_of(1) is not None:
                    m = n + 1
                    dve.wait_ge(rstd1_ready, m + 1)
                    dve.wait_ge(hT_psum, at_least_0(2 * m))
                    for i in range(Q):
                        v.tensor_scalar(u_n[:, i, :], u[:, i, :], mv1[:, i, 0:1], rstd1[:, i:i + 1],
                                        ALU.subtract, ALU.mult).then_inc(un_ready, 1)
                if layer_of(0) is not None:
                    low(n, 3)
                if layer_of(-1) is not None:
                    m = n - 1
                    dve.wait_ge(rstd2_ready, m + 1)
                    dve.wait_ge(yn_ready, at_least_0(4 * m))
                    v.scalar_tensor_tensor(out=shift2[:, :], in0=mv2[:, :, 0], scalar=-1.0, in1=rstd2[:, :],
                                           op0=ALU.mult, op1=ALU.mult).then_inc(shift2_ready, 1)
                if layer_of(0) is not None:
                    low(n, 4)
                if layer_of(3) is not None:
                    m, layer = n + 3, layer_of(3)
                    dve.wait_ge(x_in[1 - par], 16 * (m - 1 + par) + 32)
                    dve.wait_ge(sj_spread, at_least_0(m))
                    dve.wait_ge(s_biased, at_least_0(4 * m))
                    node_scores(m, 1 - par, layer, range(Q // 2))
                if layer_of(0) is not None:
                    low(n, 5)
                if layer_of(1) is not None:
                    m = n + 1
                    dve.wait_ge(ff_psum, at_least_0(8 * (m - 2) + 8))
                    for t in range(DT):
                        dve.wait_ge(hT_ready, 2 * m + t + 1)
                        v.tensor_copy(hT_hi[1 - par][:, t, :], hT[1 - par][:, t, :]).then_inc(hT_hi_ready, 1)
                        dve.wait_ge(hT_hi_ready, 2 * m + t + 1)
                        v.tensor_tensor(hT_lo[1 - par][:, t, :], hT[1 - par][:, t, :],
                                        hT_hi[1 - par][:, t, :].bitcast(fp32), ALU.subtract).then_inc(hT_lo_ready, 1)
                if layer_of(0) is not None:
                    low(n, 6)
                if layer_of(3) is not None:
                    m, layer = n + 3, layer_of(3)
                    node_scores(m, 1 - par, layer, range(Q // 2, Q))
                    dve.wait_ge(sij_ready, 2 * Q * (m + 1))
                    v.tensor_scalar(si_b[:, :], si[:, :], mem["attn_b"][:, layer:layer + 1], None, ALU.add)\
                     .then_inc(sib_ready, 1)
                if layer_of(2) is not None:
                    m = n + 2
                    dve.wait_ge(e_ready, 4 * m + 4)
                    v.reciprocal(e_inv[:, :], e_sum[:, :]).then_inc(einv_ready, 1)
                if layer_of(-2) == layers - 1:
                    k = n - 2 - (layers - 1) * groups
                    dve.wait_ge(z_ready, k + 1)
                    for i in range(Q):
                        v.bn_stats(stats3[:, i, :], x_first[:, i, :]).then_inc(stats3_ready, 1)
                    mean_and_variance(stats3, mv3, var3, stats3_ready, mv3_ready, var3_ready, k)
                    dve.wait_ge(rstd3_ready, k + 1)
                    dve.wait_ge(out_stored, at_least_0(16 * Q * k))
                    for i in range(Q):
                        v.tensor_scalar(x_out[:, i, :], x_first[:, i, :], mv3[:, i, 0:1], rstd3[:, i:i + 1],
                                        ALU.subtract, ALU.mult).then_inc(xout_ready, 1)
                if layer_of(2) is not None:
                    m = n + 2
                    dve.wait_ge(eT_hi_ready, m + 1)
                    v.tensor_tensor(eT_lo[:, :], ps_s[:, :], eT_hi[:, :].bitcast(fp32), ALU.subtract)\
                     .then_inc(eT_lo_ready, 1)
            run(dve, step)

        @block.tensor
        def _(pe):
            def up(n, par, layer, f):
                pe.wait_ge(g_ready, at_least_0(8 * n + f - 1))
                if f == 0:
                    pe.wait_ge(hT_lo_ready, 2 * n + 2)
                at = slice(f * P, (f + 1) * P)
                parts = [(w, t, h) for t in range(DT)
                         for w, h in ((mem["w1_hi"], hT_hi), (mem["w1_hi"], hT_lo), (mem["w1_lo"], hT_hi))]
                for c, (w, t, h) in enumerate(parts):
                    last = nc.tensor.matmul(ps_ff[f % 2][:, :], w[layer][:, t, at], h[par][:, t, :],
                                            start=(c == 0), stop=(c == len(parts) - 1))
                last.then_inc(ff_psum, 1)

            def down(n, layer, f):
                pe.wait_ge(g_hi_ready, 8 * n + f + 1)
                if f == 0:
                    pe.wait_ge(yT_ready, at_least_0(2 * n))
                last = None
                for t in range(DT):
                    at = slice(t * P, (t + 1) * P)
                    nc.tensor.matmul(ps_y[t][:, :], mem["w2_hi"][layer][:, f, at], g_hi[f % 2][:, :],
                                     start=(f == 0), stop=False)
                    nc.tensor.matmul(ps_y[t][:, :], mem["w2_lo"][layer][:, f, at], g_hi[f % 2][:, :],
                                     start=False, stop=False)
                pe.wait_ge(g_lo_ready, 8 * n + f + 1)
                for t in range(DT):
                    at = slice(t * P, (t + 1) * P)
                    last = nc.tensor.matmul(ps_y[t][:, :], mem["w2_hi"][layer][:, f, at], g_lo[f % 2][:, :],
                                            start=False, stop=(f == FT - 1))
                last.then_inc(y_psum, 1)

            def step(n, par, layer_of):
                for f in range(FT):
                    if f == AT_HT_PE and layer_of(1) is not None:
                        m = n + 1
                        for t in range(DT):
                            if t == 0:
                                pe.wait_ge(u_ready, 4 * m + 4)
                            else:
                                pe.wait_ge(yn_ready, at_least_0(4 * (n - 1) + 2))
                            for i in range(Q):
                                if t == 0:
                                    pe.wait_ge(un_ready, 4 * m + i + 1)
                                last = nc.tensor.transpose(ps_h[t][:, i * P:(i + 1) * P],
                                                           u_n[:, i, t * P:(t + 1) * P], ident[:, :])
                            last.then_inc(hT_psum, 1)
                    if f == AT_ROWS and layer_of(-1) is not None:
                        m = n - 1
                        pe.wait_ge(yT_ready, 2 * m + 2)
                        if layer_of(0) is not None:
                            pe.wait_ge(hT_ready, 2 * n + 2)
                        for b in range(2):
                            if b == 1 and layer_of(1) is not None:
                                pe.wait_ge(u_ready, 4 * (n + 1) + 2)
                            for i in (2 * b, 2 * b + 1):
                                for t in range(DT):
                                    last = nc.tensor.transpose(
                                        ps_r[b][:, (i % 2) * D + t * P:(i % 2) * D + (t + 1) * P],
                                        yT[:, t, i * P:(i + 1) * P], ident[:, :])
                            last.then_inc(rows_psum, 1)
                    if f < 2:
                        if layer_of(-1) is not None:
                            down(n - 1, layer_of(-1), FT - 2 + f)
                    elif layer_of(0) is not None:
                        down(n, layer_of(0), f - 2)
                    if layer_of(0) is not None:
                        up(n, par, layer_of(0), f)
                    if f == 1 and layer_of(1) is not None:
                        m = n + 1
                        pe.wait_ge(x_lo_ready, m + 1)
                        pe.wait_ge(eT_lo_ready, m + 1)
                        pe.wait_ge(yn_ready, at_least_0(4 * (n - 2) + 4))
                        pe.wait_ge(hT_ready, at_least_0(2 * n + 2))
                        for i in range(Q):
                            at = slice(i * P, (i + 1) * P)
                            dst = ps_u[i // 2][:, (i % 2) * D:(i % 2 + 1) * D]
                            nc.tensor.matmul(dst, eT_hi[:, at], x_hi[:, i, :], start=True, stop=False)
                            nc.tensor.matmul(dst, eT_hi[:, at], x_lo[:, i, :], start=False, stop=False)
                            nc.tensor.matmul(dst, eT_lo[:, at], x_hi[:, i, :], start=False, stop=True)\
                              .then_inc(agg_psum, 1)
                    if f == 0 and layer_of(2) is not None:
                        m = n + 2
                        pe.wait_ge(sij_ready, 2 * Q * (m + 1))
                        pe.wait_ge(eT_lo_ready, at_least_0(m))
                        for i in range(Q):
                            last = nc.tensor.transpose(ps_s[:, i * P:(i + 1) * P],
                                                       sj[:, i:i + 1].broadcast_to([P, P]), ident[:, :])
                        last.then_inc(sj_spread, 1)
                    if f == AT_ET and layer_of(2) is not None:
                        m = n + 2
                        pe.wait_ge(s_ready, m + 1)
                        for i in range(Q):
                            pe.wait_ge(e_ready, 4 * m + i + 1)
                            last = nc.tensor.transpose(ps_s[:, i * P:(i + 1) * P], e[:, i * P:(i + 1) * P], ident[:, :])
                        last.then_inc(eT_psum, 1)
            run(pe, step)
HEADS = 8
HD = D // HEADS
HALF = HEADS // 2
STACK = 3 * HD
STACKED = 3 * HALF * 16
SCALE = HD ** -0.5
LIFT = 2.0 ** 14


def first_layer(nc, mem, groups, x_in_dram, adj_dram, weights, x1, masks):
    ctx = ExitStack()
    with ctx:
        def sb(name, shape, dt=fp32):
            return ctx.enter_context(nc.sbuf_tensor("l0_" + name, shape, dt))

        def bank(name):
            return ctx.enter_context(nc.psum_tensor("l0_" + name, [P, R], fp32))

        def sem(name):
            return ctx.enter_context(nc.semaphore("l0_" + name))

        ident = mem["ident"]
        w_raw = sb("w_raw", [P, 4, DT, D])
        w_hi = sb("w_hi", [P, 4, DT, D], fp32r)
        w_lo = sb("w_lo", [P, 4, DT, D], fp32r)
        xp = sb("xp", [P, Q, D])
        adj = sb("adj", [P, Q, P], mybir.dt.int32)
        edges = sb("edges", [P, Q, P])
        reach = sb("reach", [P, Q, P])
        mask0 = [sb(f"mask0_{i}", [P, Q, P], bf16) for i in range(2)]
        mask1 = sb("mask1", [P, Q, P], bf16)
        xT_hi = sb("xT_hi", [P, DT, R], fp32r)
        xT_lo = sb("xT_lo", [P, DT, R], fp32r)
        qk = sb("qk", [P, 12, R], fp32r)
        qk_st = [sb(f"qk_st{i}", [STACK, 2, HALF, DT * R], fp32r) for i in range(2)]
        v_parts = [[sb(f"v_part{j}_{i}", [P, Q, D], bf16) for j in range(3)] for i in range(2)]
        v_rest = sb("v_rest", [P, Q, D])
        s = [sb(f"s0_{i}", [P, HEADS, P]) for i in range(2)]
        top = [sb(f"top0_{i}", [P, HEADS]) for i in range(2)]
        shift = [sb(f"shift0_{i}", [P, HEADS]) for i in range(2)]
        e = [sb(f"e0_{i}", [P, HEADS, P]) for i in range(2)]
        e_sum = [sb(f"e_sum0_{i}", [P, HEADS]) for i in range(2)]
        e_inv = [sb(f"e_inv0_{i}", [P, HEADS]) for i in range(2)]
        pT_hi = sb("pT_hi", [P, DT, R], mybir.dt.float16)
        pT_lo = sb("pT_lo", [P, DT, R], mybir.dt.float16)
        o = [sb(f"o{i}", [P, Q, D]) for i in range(2)]
        oT_hi = sb("oT_hi", [P, DT, R], fp32r)
        oT_lo = sb("oT_lo", [P, DT, R], fp32r)
        xo = sb("xo", [P, Q, D])
        y = sb("y0", [P, Q, D])
        stats = sb("stats0", [P, Q, 6])
        mv = sb("mv0", [P, Q, 2])
        var = sb("var0", [P, Q])
        rstd = sb("rstd0", [P, Q])
        yn = sb("yn0", [P, Q, D])
        half = sb("half0", [P, Q])

        ps_s = [bank(f"ps_s{i}") for i in range(DT)]
        ps_t = [bank(f"ps_t{i}") for i in range(DT)]
        ps_o = bank("ps_o")
        ps_r = [bank(f"ps_r{i}") for i in range(3)]

        w_in, w_hi_ready, w_lo_ready = sem("w_in"), sem("w_hi_ready"), sem("w_lo_ready")
        begun = sem("begun")
        edges_ready = sem("edges_ready")
        xp_in, adj_in, xo_in, stack_in = sem("xp_in"), sem("adj_in"), sem("xo_in"), sem("stack_in")
        mask0_ready, reach_ready, mask1_ready, mask1_stored = (
            sem("mask0_ready"), sem("reach_ready"), sem("mask1_ready"), sem("mask1_stored"))
        xT_psum, xT_hi_ready, xT_lo_ready = sem("xT_psum"), sem("xT_hi_ready"), sem("xT_lo_ready")
        qk_psum, qk_hi_ready, qk_lo_ready = sem("qk_psum"), sem("qk_hi_ready"), sem("qk_lo_ready")
        v_psum, v_first_ready, v_rest_ready = sem("v_psum"), sem("v_first_ready"), sem("v_rest_ready")
        v_second_ready, v_third_ready = sem("v_second_ready"), sem("v_third_ready")
        s_psum, s_ready, shift_ready = sem("s0_psum"), sem("s0_ready"), sem("shift0_ready")
        e_ready, e_inv_ready = sem("e0_ready"), sem("e_inv0_ready")
        pT_psum, pT_hi_ready, pT_lo_ready = sem("pT_psum"), sem("pT_hi_ready"), sem("pT_lo_ready")
        o_psum, o_ready = sem("o_psum"), sem("o_ready")
        oT_psum, oT_hi_ready, oT_lo_ready = sem("oT_psum"), sem("oT_hi_ready"), sem("oT_lo_ready")
        w_psum, y_ready = sem("w_psum"), sem("y_ready")
        stats_ready, mv_ready, var_ready = sem("stats0_ready"), sem("mv0_ready"), sem("var0_ready")
        rstd_ready, yn_ready, x1_stored = sem("rstd0_ready"), sem("yn0_ready"), sem("x1_stored")

        def run(eng, step):
            def peeled(n):
                step(n, n % 2, lambda k: 0 <= n + k < groups)

            for n in range(-2, 4):
                peeled(n)
            with eng.Fori(4, groups - 5, 2) as t:
                step(t, 0, lambda k: True)
                step(t + 1, 1, lambda k: True)
            for n in range(groups - 4, groups + 2):
                peeled(n)

        def upto(count, limit):
            return max(min(count, limit), 0) if isinstance(count, int) else count

        block = ctx.enter_context(nc.Block())

        @block.sync
        def _(sp):
            def load_x(m):
                sp.dma_start(xp[:, :, :], x_in_dram[bass.ds(Q * m, Q), :, :].rearrange("q p d -> p q d")).then_inc(xp_in, 16)

            def load_adj(m):
                sp.dma_start(adj[:, :, :], adj_dram[bass.ds(Q * m, Q), :, :].rearrange("q p n -> p q n")).then_inc(adj_in, 16)

            def stack(dst):
                for h in range(HALF):
                    rows = slice(h * HD, (h + 1) * HD)
                    high_high = qk[rows, :, :].rearrange("p (x t) r -> p x (t r)", t=4)[:, 0:2, 0:DT * R]
                    high_low = qk[rows, :, :].rearrange("p (x t) r -> p x (t r)", t=6)[:, :, 0:DT * R]
                    low_high = qk[rows, 2:6, :].rearrange("p (x t) r -> p x (t r)", t=2)
                    for b, src in enumerate((high_high, high_low, low_high)):
                        sp.dma_start(dst[b * HD:(b + 1) * HD, :, h, :].bitcast(fp32),
                                     src.bitcast(fp32)).then_inc(stack_in, 16)

            load_x(0)
            for j, w in enumerate(weights):
                sp.dma_start(w_raw[:, j, :, :], w.rearrange("(t p) n -> p t n", p=P)).then_inc(w_in, 16)
            load_adj(0)

            def step(n, par, has):
                if has(1):
                    m = n + 1
                    mask1_ready_count = worked_out(sp, m + 1)
                    sp.wait_ge(begun, 1)
                    sp.wait_ge(mask1_ready, mask1_ready_count)
                    sp.dma_start(masks[bass.ds(m, 1), :, :].rearrange("o p n -> (o p) n"),
                                 mask1[:, :, :].rearrange("p q n -> p (q n)")).then_inc(mask1_stored, 16)
                    if has(2):
                        load_adj(m + 1)
                if has(-1):
                    m = n - 1
                    y_ready_count = worked_out(sp, at_least_0(2 * m))
                    sp.wait_ge(begun, 1)
                    sp.wait_ge(y_ready, y_ready_count)
                    sp.dma_start(xo[:, :, :], x_in_dram[bass.ds(Q * m, Q), :, :].rearrange("q p d -> p q d")).then_inc(xo_in, 16)
                if has(1):
                    m = n + 1
                    qk_lo_count, s_psum_count = worked_out(sp, 4 * m + 4), worked_out(sp, at_least_0(4 * n))
                    sp.wait_ge(begun, 1)
                    sp.wait_ge(qk_lo_ready, qk_lo_count)
                    sp.wait_ge(s_psum, s_psum_count)
                    stack(qk_st[1 - par])
                if has(-2):
                    m = n - 2
                    yn_ready_count = worked_out(sp, 4 * m + 4)
                    sp.wait_ge(begun, 1)
                    sp.wait_ge(yn_ready, yn_ready_count)
                    sp.dma_start(x1[bass.ds(m, 1), :, :].rearrange("o p n -> (o p) n"),
                                 yn[:, :, :].rearrange("p q d -> p (q d)")).then_inc(x1_stored, 16)
                if has(3):
                    m = n + 2
                    xT_psum_count = worked_out(sp, at_least_0(2 * m + 2))
                    sp.wait_ge(begun, 1)
                    sp.wait_ge(xT_psum, xT_psum_count)
                    load_x(m + 1)
            run(sp, step)
            sp.wait_ge(x1_stored, 16 * groups)
            sp.wait_ge(mask1_stored, 16 * groups)

        @block.gpsimd
        def _(pool):
            pool.memset(half[:, :], -0.5).then_inc(begun, 1)
            pool.wait_ge(begun, 1)

            def step(n, par, has):
                if has(1):
                    m = n + 1
                    adj_in_count, s_ready_count = worked_out(pool, 16 * m + 16), worked_out(pool, at_least_0(4 * n))
                    pool.wait_ge(begun, 1)
                    pool.wait_ge(adj_in, adj_in_count)
                    pool.wait_ge(s_ready, s_ready_count)
                    nc.gpsimd.tensor_scalar(mask0[1 - par][:, :, :], adj[:, :, :], 0.0, MASKED, ALU.is_equal, ALU.mult)\
                      .then_inc(mask0_ready, 1)
                    nc.gpsimd.tensor_scalar(edges[:, :, :], adj[:, :, :], 1.0, 0.0, ALU.mult, ALU.add).then_inc(edges_ready, 1)
                    pool.wait_ge(edges_ready, m + 1)
                    nc.gpsimd.tensor_tensor(reach[:, :, :], edges[:, :, :], ident[:, :].unsqueeze(1).broadcast_to([P, Q, P]),
                                            ALU.add).then_inc(reach_ready, 1)
                    reach_ready_count, mask1_stored_count = worked_out(pool, m + 1), worked_out(pool, at_least_0(16 * m))
                    pool.wait_ge(begun, 1)
                    pool.wait_ge(reach_ready, reach_ready_count)
                    pool.wait_ge(mask1_stored, mask1_stored_count)
                    nc.gpsimd.tensor_scalar(mask1[:, :, :], reach[:, :, :], 0.0, MASKED, ALU.is_le, ALU.mult)\
                      .then_inc(mask1_ready, 1)
                if has(-2):
                    m = n - 2
                    pool.wait_ge(var_ready, m + 1)
                    nc.gpsimd.tensor_tensor(rstd[:, :], var[:, :], half[:, :], ALU.pow).then_inc(rstd_ready, 1)
                    rstd_ready_count, x1_stored_count = worked_out(pool, m + 1), worked_out(pool, at_least_0(16 * m))
                    pool.wait_ge(begun, 1)
                    pool.wait_ge(rstd_ready, rstd_ready_count)
                    pool.wait_ge(x1_stored, x1_stored_count)
                    for q in range(Q):
                        nc.gpsimd.tensor_scalar(yn[:, q, :], y[:, q, :], mv[:, q, 0:1], rstd[:, q:q + 1],
                                                ALU.subtract, ALU.mult).then_inc(yn_ready, 1)
                if has(1):
                    m = n + 1
                    for b in range(2):
                        at = slice(2 * b, 2 * b + 2)
                        v_rest_count = worked_out(pool, 2 * m + b + 1)
                        pool.wait_ge(begun, 1)
                        pool.wait_ge(v_rest_ready, v_rest_count)
                        nc.gpsimd.tensor_scalar(v_parts[1 - par][1][:, at, :], v_rest[:, at, :], 1.0, 0.0, ALU.mult, ALU.add)\
                          .then_inc(v_second_ready, 1)
                        pool.wait_ge(v_second_ready, 2 * m + b + 1)
                        nc.gpsimd.tensor_tensor(v_parts[1 - par][2][:, at, :], v_rest[:, at, :],
                                                v_parts[1 - par][1][:, at, :], ALU.subtract).then_inc(v_third_ready, 1)
            run(pool, step)

        @block.scalar
        def _(act):
            def copy(dst, src, ready, scale=1.0):
                nc.scalar.activation(dst, src, ACT.Copy, scale=scale).then_inc(ready, 1)

            def first_part_of_v(m, q, b):
                act.wait_ge(v_psum, 2 * m + b + 1)
                copy(v_parts[q][0][:, 2 * b:2 * b + 2, :], ps_r[b][:, :].rearrange("p (q d) -> p q d", q=2), v_first_ready)

            def exponentials(i, heads):
                for h in heads:
                    nc.scalar.activation(e[i % 2][:, h, :], s[i % 2][:, h, :], ACT.Exp, bias=shift[i % 2][:, h:h + 1],
                                         scale=SCALE, accum_out=e_sum[i % 2][:, h:h + 1]).then_inc(e_ready, 1)

            def step(n, par, has):
                for i in range(Q):
                    gi = 4 * n + i
                    if has(-1) if i == 0 else has(0):
                        act.wait_ge(o_psum, at_least_0(gi - 1))
                        for t in range(DT):
                            act.wait_ge(pT_psum, 2 * (gi - 1) + t + 1)
                            copy(pT_hi[:, t, :], ps_t[t][:, :], pT_hi_ready, LIFT)
                    if i == 2 and has(-1):
                        m = n - 1
                        act.wait_ge(w_psum, at_least_0(2 * m))
                        for t in range(DT):
                            act.wait_ge(oT_psum, 2 * m + t + 1)
                            copy(oT_hi[:, t, :], ps_r[1 + t][:, :], oT_hi_ready)
                    if i == 3 and has(2):
                        m = n + 2
                        act.wait_ge(v_psum, at_least_0(2 * m))
                        for t in range(DT):
                            act.wait_ge(xT_psum, 2 * m + t + 1)
                            copy(xT_hi[:, t, :], ps_r[2 * (1 - t)][:, :], xT_hi_ready)
                    if has(0):
                        act.wait_ge(shift_ready, gi + 1)
                        act.wait_ge(pT_psum, at_least_0(2 * (gi - 1)))
                        act.wait_ge(e_inv_ready, at_least_0(gi - 1))
                        exponentials(i, range(HALF))
                    if i < 2 and has(1):
                        m = n + 1
                        act.wait_ge(stack_in, at_least_0(STACKED * m))
                        act.wait_ge(qk_psum, 4 * m + 2 * i + 1)
                        copy(qk[:, 4 * i, :], ps_r[2 * i][:, :], qk_hi_ready)
                        if i == 1:
                            act.wait_ge(qk_psum, 4 * m + 4)
                            copy(qk[:, 5, :], ps_r[0][:, :], qk_hi_ready)
                    if i == 2 and has(1):
                        act.wait_ge(o_psum, at_least_0(4 * n))
                        first_part_of_v(n + 1, 1 - par, 0)
                    if has(0):
                        exponentials(i, range(HALF, HEADS))
                    if i == 0 and has(1):
                        m = n + 1
                        act.wait_ge(qk_psum, 4 * m + 2)
                        copy(qk[:, 1, :], ps_r[1][:, :], qk_hi_ready)
                    if i == 2 and has(1):
                        first_part_of_v(n + 1, 1 - par, 1)
            run(act, step)

        @block.vector
        def _(dve):
            v = nc.vector
            dve.wait_ge(w_in, 64)
            v.tensor_scalar(w_raw[:, 3, :, :], w_raw[:, 3, :, :], 1.0 / LIFT, None, ALU.mult).then_inc(w_hi_ready, 1)
            dve.wait_ge(w_hi_ready, 1)
            for j in range(4):
                v.tensor_copy(w_hi[:, j, :, :], w_raw[:, j, :, :]).then_inc(w_hi_ready, 1)
            for j in range(4):
                dve.wait_ge(w_hi_ready, j + 2)
                v.tensor_tensor(w_lo[:, j, :, :], w_raw[:, j, :, :], w_hi[:, j, :, :].bitcast(fp32), ALU.subtract)\
                 .then_inc(w_lo_ready, 1)

            def low(dst, src, hi, ready):
                v.tensor_tensor(dst, src, hi.bitcast(fp32), ALU.subtract).then_inc(ready, 1)

            def low_of_q_or_k(m, c):
                dve.wait_ge(qk_hi_ready, 4 * m + c + 1)
                plane = 4 * (c // 2) + c % 2
                low(qk[:, plane + 2, :], ps_r[c % 3][:, :], qk[:, plane, :], qk_lo_ready)

            def rest_of_v(m, q, b):
                at = slice(2 * b, 2 * b + 2)
                dve.wait_ge(v_first_ready, 2 * m + b + 1)
                v.tensor_tensor(v_rest[:, at, :], ps_r[b][:, :].rearrange("p (q d) -> p q d", q=2),
                                v_parts[q][0][:, at, :], ALU.subtract).then_inc(v_rest_ready, 1)

            def residual(m, b):
                at = slice(2 * b, 2 * b + 2)
                dve.wait_ge(w_psum, 2 * m + b + 1)
                v.tensor_tensor(y[:, at, :], ps_r[1 + b][:, :].rearrange("p (q d) -> p q d", q=2),
                                xo[:, at, :], ALU.add).then_inc(y_ready, 1)

            def step(n, par, has):
                for i in range(Q):
                    gi = 4 * n + i
                    if has(0):
                        s_psum_count, e_ready_count = worked_out(dve, gi + 1), worked_out(dve, at_least_0(8 * (gi - 1)))
                        mask0_count = worked_out(dve, n + 1)
                        dve.wait_ge(begun, 1)
                        dve.wait_ge(mask0_ready, mask0_count)
                        dve.wait_ge(s_psum, s_psum_count)
                        dve.wait_ge(e_ready, e_ready_count)
                        for h in range(HEADS):
                            last = v.tensor_tensor_reduce(
                                out=s[i % 2][:, h, :], in0=ps_s[h // HALF][:, (h % HALF) * P:(h % HALF + 1) * P],
                                in1=mask0[par][:, i, :], scale=1.0, scalar=2 * MASKED, op0=ALU.add, op1=ALU.max,
                                accum_out=top[i % 2][:, h:h + 1])
                        last.then_inc(s_ready, 1)
                    if has(-1) if i == 0 else has(0):
                        dve.wait_ge(e_ready, 8 * gi)
                        dve.wait_ge(o_ready, at_least_0(gi - 2))
                        v.reciprocal(e_inv[1 - i % 2][:, :], e_sum[1 - i % 2][:, :]).then_inc(e_inv_ready, 1)
                    if has(0):
                        dve.wait_ge(s_ready, gi + 1)
                        v.tensor_scalar(shift[i % 2][:, :], top[i % 2][:, :], -SCALE, None, ALU.mult).then_inc(shift_ready, 1)
                    if i == 0 and has(-2):
                        residual(n - 2, 1)
                    if i == 1 and has(1):
                        low_of_q_or_k(n + 1, 1)
                    if i == 3 and has(1):
                        rest_of_v(n + 1, 1 - par, 1)
                    if has(-1) if i < 2 else has(0):
                        k = (i - 2) % Q
                        q = par if i >= 2 else 1 - par
                        dve.wait_ge(o_psum, gi - 1)
                        dve.wait_ge(e_inv_ready, gi - 1)
                        v.scalar_tensor_tensor(
                            out=o[q][:, k, :].rearrange("p (h c) -> p h c", h=HEADS),
                            in0=ps_o[:, 0:D].rearrange("p (h c) -> p h c", h=HEADS), scalar=0.0,
                            in1=e_inv[i % 2][:, :].unsqueeze(2).broadcast_to([P, HEADS, HD]), op0=ALU.max, op1=ALU.mult)\
                         .then_inc(o_ready, 1)
                    if has(-1) if i == 0 else has(0):
                        for t in range(DT):
                            dve.wait_ge(pT_hi_ready, 2 * (gi - 1) + t + 1)
                            v.scalar_tensor_tensor(out=pT_lo[:, t, :], in0=ps_t[t][:, :], scalar=LIFT, in1=pT_hi[:, t, :],
                                                   op0=ALU.mult, op1=ALU.subtract).then_inc(pT_lo_ready, 1)
                    if i == 0 and has(-2):
                        m = n - 2
                        dve.wait_ge(yn_ready, at_least_0(4 * m))
                        for q in range(Q):
                            dve.wait_ge(y_ready, 2 * m + q // 2 + 1)
                            v.bn_stats(stats[:, q, :], y[:, q, :]).then_inc(stats_ready, 1)
                        stats_ready_count = worked_out(dve, 4 * m + 4)
                        dve.wait_ge(begun, 1)
                        dve.wait_ge(stats_ready, stats_ready_count)
                        for q in range(Q):
                            v.bn_aggr(mv[:, q, :], stats[:, q, :]).then_inc(mv_ready, 1)
                        dve.wait_ge(mv_ready, 4 * m + 4)
                        v.tensor_scalar(var[:, :], mv[:, :, 1], EPS, None, ALU.add).then_inc(var_ready, 1)
                    if i < 2 and has(1):
                        m = n + 1
                        low_of_q_or_k(m, 2 * i)
                        if i == 1:
                            low_of_q_or_k(m, 3)
                    if i == 2 and has(-1):
                        m = n - 1
                        for t in range(DT):
                            dve.wait_ge(oT_hi_ready, 2 * m + t + 1)
                            low(oT_lo[:, t, :], ps_r[1 + t][:, :], oT_hi[:, t, :], oT_lo_ready)
                    if i == 2 and has(1):
                        m = n + 1
                        dve.wait_ge(v_third_ready, at_least_0(2 * m))
                        rest_of_v(m, 1 - par, 0)
                    if i == 3 and has(2):
                        m = n + 2
                        for t in range(DT):
                            dve.wait_ge(xT_hi_ready, 2 * m + t + 1)
                            low(xT_lo[:, t, :], ps_r[2 * (1 - t)][:, :], xT_hi[:, t, :], xT_lo_ready)
                    if i == 3 and has(-1):
                        m = n - 1
                        dve.wait_ge(xo_in, 16 * m + 16)
                        dve.wait_ge(yn_ready, at_least_0(4 * m))
                        residual(m, 0)
            run(dve, step)

        @block.tensor
        def _(pe):
            def split_product(dst, pairs, signal):
                n = 3 * len(pairs)
                c = 0
                for (l_hi, l_lo), (r_hi, r_lo) in pairs:
                    for left, right in ((l_hi, r_hi), (l_hi, r_lo), (l_lo, r_hi)):
                        last = nc.tensor.matmul(dst, left, right, start=(c == 0), stop=(c == n - 1))
                        c += 1
                if signal is not None:
                    last.then_inc(signal, 1)

            def transposes(dst, srcs, signal):
                for j, src in enumerate(srcs):
                    last = nc.tensor.transpose(dst[:, j * P:(j + 1) * P], src, ident[:, :])
                last.then_inc(signal, 1)

            def q_or_k(c):
                at = slice((c % 2) * P, (c % 2 + 1) * P)
                split_product(ps_r[c % 3][:, :],
                              [((w_hi[:, c // 2, t, at], w_lo[:, c // 2, t, at]),
                                (xT_hi[:, t, :], xT_lo[:, t, :])) for t in range(DT)], qk_psum)

            def rows_times(dst, lhs_hi, lhs_lo, j, b, signal):
                for q in (2 * b, 2 * b + 1):
                    rows = slice(q * P, (q + 1) * P)
                    split_product(dst[:, (q % 2) * D:(q % 2 + 1) * D],
                                  [((lhs_hi[:, t, rows], lhs_lo[:, t, rows]),
                                    (w_hi[:, j, t, :], w_lo[:, j, t, :])) for t in range(DT)],
                                  signal if q % 2 else None)

            def step(n, par, has):
                for i in range(Q):
                    gi = 4 * n + i
                    if has(0):
                        pe.wait_ge(stack_in, STACKED * n + STACKED)
                        pe.wait_ge(s_ready, at_least_0(gi))
                        for h in range(HEADS):
                            at = slice((h // HALF) * R + i * P, (h // HALF) * R + (i + 1) * P)
                            last = nc.tensor.matmul(ps_s[h // HALF][:, (h % HALF) * P:(h % HALF + 1) * P],
                                                    qk_st[par][:, 0, h % HALF, at], qk_st[par][:, 1, h % HALF, at],
                                                    start=True, stop=True)
                        last.then_inc(s_psum, 1)
                    if has(-1) if i < 2 else has(0):
                        k = (i - 2) % Q
                        q = par if i >= 2 else 1 - par
                        pe.wait_ge(pT_lo_ready, 2 * (gi - 2) + 2)
                        pe.wait_ge(o_ready, at_least_0(gi - 2))
                        if i == 2:
                            pe.wait_ge(v_third_ready, 2 * n + 2)
                        for h in range(HEADS):
                            at = slice((h % HALF) * P, (h % HALF + 1) * P)
                            cols = slice(h * HD, (h + 1) * HD)
                            parts = [(pT_hi, 0), (pT_hi, 1), (pT_hi, 2), (pT_lo, 0), (pT_lo, 1)]
                            for c, (p, j) in enumerate(parts):
                                last = nc.tensor.matmul(ps_o[:, cols],
                                                        p[:, h // HALF, at], v_parts[q][j][:, k, cols],
                                                        start=(c == 0), stop=(c == len(parts) - 1))
                        last.then_inc(o_psum, 1)
                    if has(-1) if i == 0 else has(0):
                        pe.wait_ge(pT_lo_ready, at_least_0(2 * (gi - 1)))
                        for t in range(DT):
                            pe.wait_ge(e_ready, 8 * (gi - 1) + HALF * (t + 1))
                            transposes(ps_t[t], [e[1 - i % 2][:, HALF * t + j, :] for j in range(HALF)], pT_psum)
                    if i == 0 and has(1):
                        m = n + 1
                        if isinstance(n, int):
                            pe.wait_ge(w_lo_ready, 4)
                        pe.wait_ge(xT_lo_ready, 2 * m + 2)
                        q_or_k(0)
                        pe.wait_ge(y_ready, at_least_0(2 * (n - 2) + 1))
                        q_or_k(1)
                    if i == 1 and has(1):
                        pe.wait_ge(y_ready, at_least_0(2 * (n - 2) + 2))
                        q_or_k(2)
                        pe.wait_ge(qk_lo_ready, 4 * (n + 1) + 1)
                        q_or_k(3)
                    if i == 2 and has(-1):
                        m = n - 1
                        pe.wait_ge(o_ready, 4 * m + 4)
                        for t in range(DT):
                            pe.wait_ge(qk_lo_ready, upto(4 * (n + 1) + 2 + t, 4 * groups))
                            if not has(1):
                                pe.wait_ge(y_ready, at_least_0(2 * (n - 2) + 1 + t))
                            transposes(ps_r[1 + t], [o[1 - par][:, q, t * P:(t + 1) * P] for q in range(Q)], oT_psum)
                    if i == 2 and has(1):
                        pe.wait_ge(qk_lo_ready, 4 * (n + 1) + 4)
                        rows_times(ps_r[0], xT_hi, xT_lo, 2, 0, v_psum)
                        pe.wait_ge(oT_lo_ready, at_least_0(2 * (n - 1) + 1))
                        rows_times(ps_r[1], xT_hi, xT_lo, 2, 1, v_psum)
                    if i == 3 and has(2):
                        m = n + 2
                        pe.wait_ge(xp_in, 16 * m + 16)
                        pe.wait_ge(oT_lo_ready, at_least_0(2 * (n - 1) + 2))
                        transposes(ps_r[2], [xp[:, q, 0:P] for q in range(Q)], xT_psum)
                        pe.wait_ge(v_rest_ready, at_least_0(2 * (n + 1) + 1))
                        transposes(ps_r[0], [xp[:, q, P:2 * P] for q in range(Q)], xT_psum)
                    if i == 3 and has(-1):
                        m = n - 1
                        pe.wait_ge(oT_lo_ready, 2 * m + 2)
                        pe.wait_ge(v_rest_ready, upto(2 * (n + 1) + 2, 2 * groups))
                        rows_times(ps_r[1], oT_hi, oT_lo, 3, 0, w_psum)
                        pe.wait_ge(xT_lo_ready, upto(2 * (n + 2) + 1, 2 * groups))
                        rows_times(ps_r[2], oT_hi, oT_lo, 3, 1, w_psum)
            run(pe, step)
def load_constants(nc, mem, layers, raw):
    with ExitStack() as ctx:
        def sem(name):
            return ctx.enter_context(nc.semaphore(name))

        stage = [ctx.enter_context(nc.sbuf_tensor(f"stage{i}", [P, DT * FF], fp32)) for i in range(2)]
        stage_in = [sem(f"stage_in{i}") for i in range(2)]
        consts_in, hi_ready, lo_ready = sem("consts_in"), sem("hi_ready"), sem("lo_ready")
        pieces = []
        for l in range(layers):
            pieces.append((raw["W1"][l, :, :].rearrange("(t p) n -> p t n", p=P), mem["w1_hi"][l], mem["w1_lo"][l], DT))
            pieces.append((raw["W2"][l, :, :].rearrange("(t p) n -> p t n", p=P), mem["w2_hi"][l], mem["w2_lo"][l], FT))
        block = ctx.enter_context(nc.Block())

        @block.sync
        def _(sp):
            for i, (src, _, _, t) in enumerate(pieces):
                if i >= 2:
                    sp.wait_ge(lo_ready, i - 1)
                sp.dma_start(stage[i % 2][:, :].rearrange("p (t n) -> p t n", t=t), src).then_inc(stage_in[i % 2], 16)

        @block.scalar
        def _(act):
            count = 0
            for dst, src in ((mem["attn_w"][:, :, :], raw["attn_w"]), (mem["attn_b"][:, :], raw["attn_b"]),
                             (mem["g2_row"][:, :, :], raw["g2"]), (mem["beta2_row"][:, :, :], raw["beta2"])):
                act.dma_start(dst, src.partition_broadcast(P)).then_inc(consts_in, 16)
                count += 16
            for name in ("g1", "beta1", "b1", "b2"):
                for l in range(layers):
                    act.dma_start(mem[name][:, l, :], raw[name][l, :].rearrange("(t p) -> p t", p=P),
                                  allow_slow_non_contiguous=True).then_inc(consts_in, 16)
                    count += 16
            act.wait_ge(consts_in, count)

        @block.vector
        def _(dve):
            for i, (_, hi, lo, t) in enumerate(pieces):
                src = stage[i % 2][:, :].rearrange("p (t n) -> p t n", t=t)
                dve.wait_ge(stage_in[i % 2], 16 * (i // 2 + 1))
                nc.vector.tensor_copy(hi[:, :, :], src).then_inc(hi_ready, 1)
                dve.wait_ge(hi_ready, i + 1)
                nc.vector.tensor_tensor(lo[:, :, :], src, hi[:, :, :].bitcast(fp32), ALU.subtract).then_inc(lo_ready, 1)


def program(nc, x, adj, Wq, Wk, Wv, Wo, attn_w, attn_b, W1, b1, W2, b2, g1, beta1, g2, beta2, out):
    graphs = x.shape[0]
    groups = graphs // Q
    layers = attn_w.shape[0]
    x1 = nc.dram_tensor("x1_kept", (groups, P, Q * D), fp32, kind="Internal").ap()
    masks = nc.dram_tensor("masks_kept", (groups, P, Q * P), bf16, kind="Internal").ap()
    x_mid = [nc.dram_tensor(f"x_kept{i}", (groups, P, Q * D), fp32, kind="Internal").ap() for i in range(layers - 1)]
    raw = dict(W1=W1, W2=W2, attn_w=attn_w, attn_b=attn_b, g1=g1, beta1=beta1, g2=g2, beta2=beta2, b1=b1, b2=b2)
    with ExitStack() as ctx:
        def sb(name, shape, dt=fp32):
            return ctx.enter_context(nc.sbuf_tensor(name, shape, dt))

        mem = {"ident": sb("ident", [P, P])}
        ident_ready = ctx.enter_context(nc.semaphore("ident_ready"))
        with nc.Block() as block:
            @block.gpsimd
            def _(pool):
                pool.memset(mem["ident"][:, :], 0.0).then_inc(ident_ready, 1)
                pool.wait_ge(ident_ready, 1)
                pool.affine_select(out=mem["ident"][:, :], in_=mem["ident"][:, :], compare_op=ALU.not_equal, fill=1.0,
                                   base=0, pattern=[[-1, P]], channel_multiplier=1).then_inc(ident_ready, 1)
        first_layer(nc, mem, groups, x, adj, (Wq, Wk, Wv, Wo), x1, masks)
        mem["attn_w"] = sb("attn_w_row", [P, layers, 2 * D])
        mem["attn_b"] = sb("attn_b_row", [P, layers])
        mem["g2_row"] = sb("g2_row", [P, layers, D])
        mem["beta2_row"] = sb("beta2_row", [P, layers, D])
        for name, tiles in (("g1", DT), ("beta1", DT), ("b2", DT), ("b1", FT)):
            mem[name] = sb(f"{name}_col", [P, layers, tiles])
        for part in ("hi", "lo"):
            mem[f"w1_{part}"] = [sb(f"w1_{part}{l}", [P, DT, FF], fp32r) for l in range(layers)]
            mem[f"w2_{part}"] = [sb(f"w2_{part}{l}", [P, FT, D], fp32r) for l in range(layers)]
        load_constants(nc, mem, layers, raw)
        gnn_layers(nc, mem, layers, groups, x1, masks, x_mid, out)


_INS = ["x", "adj", "L0_gnn_Wq", "L0_gnn_Wk", "L0_gnn_Wv", "L0_gnn_Wo", "L1_gnn_attn_w", "L1_gnn_attn_b",
        "L1_gnn_W1", "L1_gnn_b1", "L1_gnn_W2", "L1_gnn_b2", "L1_gnn_g1", "L1_gnn_beta1", "L1_gnn_g2", "L1_gnn_beta2"]


def kernel(**inputs):
    import numpy as _np
    import concourse.bacc as _bacc
    from concourse import mybir as _mybir
    from concourse.bass_utils import run_bass_kernel_spmd as _run

    nc = _bacc.Bacc("TRN2", target_bir_lowering=False, num_devices=1)
    arrays, args = {}, []
    for name in _INS:
        a = _np.ascontiguousarray(inputs[name])
        arrays[f"in_{name}"] = a
        args.append(nc.dram_tensor(f"in_{name}", a.shape, _mybir.dt.from_np(a.dtype), kind="ExternalInput").ap())
    shape = tuple(inputs["x"].shape)
    args.append(nc.dram_tensor("result", shape, _mybir.dt.float32, kind="ExternalOutput").ap())
    program(nc, *args)
    r = _run(nc, [arrays], core_ids=[0])
    return r.results[0]["result"]
```

```python
import concourse.bass as bass
from concourse import mybir
from contextlib import ExitStack

fp32 = mybir.dt.float32
fp32r = mybir.dt.float32r
bf16 = mybir.dt.bfloat16
ALU = mybir.AluOpType
ACT = mybir.ActivationFunctionType

P = 128
Q = 4
R = Q * P
D = 256
DT = D // P
FF = 1024
FT = FF // P
EPS = 1e-5
MASKED = -1e30
WEIGHTS = (("W1", DT), ("W2", FT))

AT_BIAS, AT_EXP, AT_YN, AT_HT = 1, 2, 5, 6
AT_ROWS, AT_ET, AT_HT_PE = 3, 4, 6


def at_least_0(count):
    return max(count, 0) if isinstance(count, int) else count


def worked_out(eng, count):
    return count if isinstance(count, int) else eng.to_reg(count)


def gnn_layers(nc, mem, layers, groups, raw, x1, masks, x_mid, out):
    total = layers * groups
    ctx = ExitStack()
    with ctx:
        def sb(name, shape, dt=fp32):
            return ctx.enter_context(nc.sbuf_tensor(name, shape, dt))

        def bank(name, dt=fp32):
            return ctx.enter_context(nc.psum_tensor(name, [P, R], dt))

        def sem(name):
            return ctx.enter_context(nc.semaphore(name))

        ident = mem["ident"]
        x = [sb(f"x{i}", [P, Q, D]) for i in range(2)]
        mask = [sb(f"mask{i}", [P, R], bf16) for i in range(2)]
        x_hi = sb("x_hi", [P, Q, D], fp32r)
        x_lo = sb("x_lo", [P, Q, D], fp32r)
        dump = sb("dump", [P, 2 * Q, D], bf16)
        si = sb("si", [P, Q])
        sj = sb("sj", [P, Q])
        si_b = sb("si_b", [P, Q])
        top = sb("top", [P, Q])
        top_n = sb("top_n", [P, Q])
        shift = sb("shift", [P, Q])
        s = sb("s", [P, R])
        e = sb("e", [P, R])
        e_sum = sb("e_sum", [P, Q])
        e_inv = sb("e_inv", [P, Q])
        eT_hi = sb("eT_hi", [P, R], fp32r)
        eT_lo = sb("eT_lo", [P, R], fp32r)
        u = sb("u", [P, Q, D])
        stats1 = sb("stats1", [P, Q, 6])
        mv1 = sb("mv1", [P, Q, 2])
        var1 = sb("var1", [P, Q])
        rstd1 = sb("rstd1", [P, Q])
        hT = [sb(f"hT{i}", [P, DT, R]) for i in range(2)]
        hT_hi = [sb(f"hT_hi{i}", [P, DT, R], fp32r) for i in range(2)]
        hT_lo = [sb(f"hT_lo{i}", [P, DT, R], fp32r) for i in range(2)]
        g = [sb(f"g{i}", [P, R]) for i in range(2)]
        g_hi = [sb(f"g_hi{i}", [P, R], fp32r) for i in range(2)]
        g_lo = [sb(f"g_lo{i}", [P, R], fp32r) for i in range(2)]
        yT = sb("yT", [P, DT, R])
        stats2 = sb("stats2", [P, Q, 6])
        mv2 = sb("mv2", [P, Q, 2])
        var2 = sb("var2", [P, Q])
        rstd2 = sb("rstd2", [P, Q])
        shift2 = sb("shift2", [P, Q])
        y_n = sb("y_n", [P, Q, D])
        x_first = sb("x_first", [P, Q, D])
        stats3 = sb("stats3", [P, Q, 6])
        mv3 = sb("mv3", [P, Q, 2])
        var3 = sb("var3", [P, Q])
        rstd3 = sb("rstd3", [P, Q])
        half = sb("half", [P, Q])
        stage = mem["stage"]
        x_out = stage[0][:, 0:Q * D].rearrange("p (q d) -> p q d", q=Q)

        ps_ff = [bank(f"ps_ff{i}") for i in range(2)]
        ps_y = [bank(f"ps_y{i}") for i in range(DT)]
        ps_s = bank("ps_s")
        ps_a = bank("ps_a")
        ps_b = bank("ps_b")
        ps_c = bank("ps_c")
        ps_u = [ps_a, ps_b]
        ps_h = [ps_b, ps_c]
        ps_r = [ps_c, ps_a]

        x_in = [sem(f"x_in{i}") for i in range(2)]
        x_hi_ready, x_lo_ready = sem("x_hi_ready"), sem("x_lo_ready")
        sij_ready, sib_ready = sem("sij_ready"), sem("sib_ready")
        sj_spread = sem("sj_spread")
        s_ready = sem("s_ready")
        shift_steps = sem("shift_steps")
        s_biased, lrelu_ready, e_ready = sem("s_biased"), sem("lrelu_ready"), sem("e_ready")
        einv_ready = sem("einv_ready")
        eT_psum, eT_hi_ready, eT_lo_ready = sem("eT_psum"), sem("eT_hi_ready"), sem("eT_lo_ready")
        agg_psum = sem("agg_psum")
        u_ready, stats1_ready, mv1_ready = sem("u_ready"), sem("stats1_ready"), sem("mv1_ready")
        rstd1_ready, un_ready = sem("rstd1_ready"), sem("un_ready")
        hT_psum, hT_ready = sem("hT_psum"), sem("hT_ready")
        hT_hi_ready, hT_lo_ready = sem("hT_hi_ready"), sem("hT_lo_ready")
        ff_psum = sem("ff_psum")
        g_ready, g_hi_ready, g_lo_ready = sem("g_ready"), sem("g_hi_ready"), sem("g_lo_ready")
        y_psum, yT_ready = sem("y_psum"), sem("yT_ready")
        rows_psum = sem("rows_psum")
        stats2_ready, mv2_ready = sem("stats2_ready"), sem("mv2_ready")
        var1_ready, var2_ready, var3_ready = sem("var1_ready"), sem("var2_ready"), sem("var3_ready")
        rstd2_ready, shift2_ready, yn_ready = sem("rstd2_ready"), sem("shift2_ready"), sem("yn_ready")
        gain_done, xnew_ready = sem("gain_done"), sem("xnew_ready")
        x_stored = sem("x_stored")
        begun = sem("begun")
        attn_w_in, attn_w_rest_in, attn_b_in = sem("attn_w_in"), sem("attn_w_rest_in"), sem("attn_b_in")
        norm_rows_in = sem("norm_rows_in")
        stage_in, w_hi_ready, w_lo_ready = sem("stage_in"), sem("w_hi_ready"), sem("w_lo_ready")
        first_in = sem("first_in")
        z_ready, stats3_ready, mv3_ready = sem("z_ready"), sem("stats3_ready"), sem("mv3_ready")
        rstd3_ready, xout_ready = sem("rstd3_ready"), sem("xout_ready")
        out_stored = sem("out_stored")

        def run(eng, step):
            def peeled(n):
                step(n, n % 2, lambda k: (n + k) // groups if 0 <= n + k < total else None)

            for n in range(-3, 0):
                peeled(n)
            for layer in range(layers):
                base = layer * groups
                first = base + (4 if layer == layers - 1 else 2)
                end = base + groups - 4
                for n in range(base, first):
                    peeled(n)
                with eng.Fori(first, end - 1, 2) as t:
                    step(t, 0, lambda k: layer)
                    step(t + 1, 1, lambda k: layer)
                for n in range(end, base + groups):
                    peeled(n)
            peeled(total)
            peeled(total + 1)

        block = ctx.enter_context(nc.Block())

        @block.sync
        def _(sp):
            def step(n, par, layer_of):
                if isinstance(n, int) and n % groups == 0 and 0 <= n // groups < layers - 1:
                    sp.wait_ge(w_lo_ready, 2 * (n // groups + 1))
                    for j, (name, t) in enumerate(WEIGHTS):
                        sp.dma_start(stage[j][:, :].rearrange("p (t n) -> p t n", t=t),
                                     raw[name][n // groups + 1, :, :].rearrange("(t p) n -> p t n", p=P)).then_inc(stage_in, 16)
                m = n + 3
                layer = layer_of(3)
                if layer is not None:
                    q = m % 2 if isinstance(m, int) else 1 - par
                    src = x1 if layer == 0 else x_mid[layer - 1]
                    row = m - layer * groups
                    u_ready_count = worked_out(sp, at_least_0(4 * (m - 2) + 4))
                    x_stored_count = worked_out(sp, at_least_0(16 * (m - groups) + 16)) if layer > 0 else 0
                    sp.wait_ge(begun, 1)
                    sp.wait_ge(u_ready, u_ready_count)
                    if layer > 0:
                        sp.wait_ge(x_stored, x_stored_count)
                    sp.dma_start(x[q][:, :, :], src[bass.ds(row, 1), :, :].rearrange("o p (q d) -> (o p) q d", q=Q))\
                      .then_inc(x_in[q], 16)
                    sp.dma_start(mask[q][:, :], masks[bass.ds(row, 1), :, :].rearrange("o p n -> (o p) n"))\
                      .then_inc(x_in[q], 16)
                if layer_of(-2) == layers - 1:
                    k = n - 2 - (layers - 1) * groups
                    xout_ready_count = worked_out(sp, 4 * k + 4)
                    sp.wait_ge(begun, 1)
                    sp.wait_ge(xout_ready, xout_ready_count)
                    for i in range(Q):
                        sp.dma_start(out[bass.ds(Q * k + i, 1), :, :].rearrange("o p d -> (o p) d"),
                                     x_out[:, i, :]).then_inc(out_stored, 16)
                if layer_of(-1) is not None:
                    m, layer = n - 1, layer_of(-1)
                    if layer < layers - 1:
                        xnew_ready_count = worked_out(sp, m + 1)
                        sp.wait_ge(begun, 1)
                        sp.wait_ge(xnew_ready, xnew_ready_count)
                        sp.dma_start(x_mid[layer][bass.ds(m - layer * groups, 1), :, :].rearrange("o p (q d) -> (o p) q d", q=Q),
                                     y_n[:, :, :]).then_inc(x_stored, 16)
                    else:
                        k = m - layer * groups
                        xout_ready_count = worked_out(sp, at_least_0(4 * k))
                        sp.wait_ge(begun, 1)
                        sp.wait_ge(xout_ready, xout_ready_count)
                        sp.dma_start(x_first[:, :, :], x1[bass.ds(k, 1), :, :].rearrange("o p (q d) -> (o p) q d", q=Q))\
                          .then_inc(first_in, 16)
            run(sp, step)
            sp.wait_ge(out_stored, 16 * Q * groups)
            sp.wait_ge(x_stored, 16 * (layers - 1) * groups)

        @block.gpsimd
        def _(pool):
            pool.memset(half[:, :], -0.5).then_inc(begun, 1)
            pool.wait_ge(begun, 1)

            def inverse_deviation(rstd, var, ready):
                nc.gpsimd.tensor_tensor(rstd[:, :], var[:, :], half[:, :], ALU.pow).then_inc(ready, 1)

            def step(n, par, layer_of):
                if isinstance(n, int) and (n + 3) % groups < 2 and (n + 3) // groups < layers:
                    layer, j = (n + 3) // groups, (n + 3) % groups
                    name, t = WEIGHTS[j]
                    src = stage[j][:, :].rearrange("p (t n) -> p t n", t=t)
                    hi, lo = mem[name + "_hi"][layer], mem[name + "_lo"][layer]
                    if layer > 0:
                        pool.wait_ge(stage_in, 16 * 2 * layer)
                    nc.gpsimd.tensor_scalar(hi[:, :, :], src, 1.0, 0.0, ALU.mult, ALU.add).then_inc(w_hi_ready, 1)
                    pool.wait_ge(w_hi_ready, 2 * layer + j + 1)
                    nc.gpsimd.tensor_tensor(lo[:, :, :], src, hi[:, :, :].bitcast(fp32), ALU.subtract).then_inc(w_lo_ready, 1)
                if layer_of(2) is not None:
                    m = n + 2
                    x_in_count = worked_out(pool, 16 * (m - par) + 32)
                    agg_psum_count = worked_out(pool, at_least_0(4 * (m - 1) + 4))
                    pool.wait_ge(begun, 1)
                    pool.wait_ge(x_in[par], x_in_count)
                    pool.wait_ge(agg_psum, agg_psum_count)
                    nc.gpsimd.tensor_scalar(x_hi[:, :, :], x[par][:, :, :], 1.0, 0.0, ALU.mult, ALU.add)\
                      .then_inc(x_hi_ready, 1)
                    pool.wait_ge(x_hi_ready, m + 1)
                    nc.gpsimd.tensor_tensor(x_lo[:, :, :], x[par][:, :, :], x_hi[:, :, :].bitcast(fp32), ALU.subtract)\
                      .then_inc(x_lo_ready, 1)
                if layer_of(1) is not None:
                    m = n + 1
                    pool.wait_ge(var1_ready, m + 1)
                    pool.wait_ge(un_ready, at_least_0(4 * (m - 1) + 4))
                    inverse_deviation(rstd1, var1, rstd1_ready)
                if layer_of(-1) is not None:
                    m = n - 1
                    pool.wait_ge(var2_ready, m + 1)
                    pool.wait_ge(yn_ready, at_least_0(4 * (m - 1) + 4))
                    inverse_deviation(rstd2, var2, rstd2_ready)
                if layer_of(-2) == layers - 1:
                    k = n - 2 - (layers - 1) * groups
                    pool.wait_ge(var3_ready, k + 1)
                    pool.wait_ge(xout_ready, at_least_0(4 * k))
                    inverse_deviation(rstd3, var3, rstd3_ready)
                    if layer_of(0) is not None:
                        rstd3_count, out_stored_count = worked_out(pool, k + 1), worked_out(pool, at_least_0(16 * Q * k))
                        pool.wait_ge(begun, 1)
                        pool.wait_ge(rstd3_ready, rstd3_count)
                        pool.wait_ge(out_stored, out_stored_count)
                        for i in range(Q):
                            nc.gpsimd.tensor_scalar(x_out[:, i, :], x_first[:, i, :], mv3[:, i, 0:1], rstd3[:, i:i + 1],
                                                    ALU.subtract, ALU.mult).then_inc(xout_ready, 1)
                if layer_of(-1) is not None:
                    m, layer = n - 1, layer_of(-1)
                    gain = mem["g2"][:, layer, :].unsqueeze(1).broadcast_to([P, Q, D])
                    beta = mem["beta2"][:, layer, :].unsqueeze(1).broadcast_to([P, Q, D])
                    if isinstance(m, int) and m == 0:
                        pool.wait_ge(norm_rows_in, 32)
                    pool.wait_ge(yn_ready, 4 * m + 4)
                    nc.gpsimd.tensor_tensor(y_n[:, :, :], y_n[:, :, :], gain, ALU.mult).then_inc(gain_done, 1)
                    pool.wait_ge(gain_done, m + 1)
                    nc.gpsimd.tensor_tensor(y_n[:, :, :], y_n[:, :, :], beta, ALU.add).then_inc(xnew_ready, 1)
                    if layer == layers - 1:
                        pool.wait_ge(xnew_ready, m + 1)
                        pool.wait_ge(first_in, 16 * (m - layer * groups) + 16)
                        nc.gpsimd.tensor_tensor(x_first[:, :, :], x_first[:, :, :], y_n[:, :, :], ALU.add)\
                          .then_inc(z_ready, 1)
            run(pool, step)

        @block.scalar
        def _(act):
            act.dma_start(mem["attn_w"][:, 0, :], raw["attn_w"][0, :].partition_broadcast(P)).then_inc(attn_w_in, 16)
            act.dma_start(mem["attn_b"][:, :], raw["attn_b"].partition_broadcast(P)).then_inc(attn_b_in, 16)
            for name in ("g2", "beta2"):
                act.dma_start(mem[name][:, :, :], raw[name].partition_broadcast(P)).then_inc(norm_rows_in, 16)
            for l in range(1, layers):
                act.dma_start(mem["attn_w"][:, l, :], raw["attn_w"][l, :].partition_broadcast(P))\
                  .then_inc(attn_w_rest_in, 16)

            def up(n, layer, f):
                act.wait_ge(ff_psum, 8 * n + f + 1)
                act.wait_ge(g_lo_ready, at_least_0(8 * n + f - 1))
                nc.scalar.activation(g[f % 2][:, :], ps_ff[f % 2][:, :], ACT.Gelu,
                                     bias=mem["b1"][:, layer, f:f + 1]).then_inc(g_ready, 1)
                act.wait_ge(y_psum, at_least_0(8 * n + f - 1))
                act.wait_ge(g_ready, 8 * n + f + 1)
                nc.scalar.activation(g_hi[f % 2][:, :], g[f % 2][:, :], ACT.Copy).then_inc(g_hi_ready, 1)

            def step(n, par, layer_of):
                for f in range(FT):
                    if f == AT_BIAS and layer_of(2) is not None:
                        m = n + 2
                        act.wait_ge(s_ready, m + 1)
                        act.wait_ge(sib_ready, m + 1)
                        for i in range(Q):
                            at = slice(i * P, (i + 1) * P)
                            nc.scalar.activation(s[:, at], s[:, at], ACT.Identity, bias=si_b[:, i:i + 1])\
                              .then_inc(s_biased, 1)
                    if f == AT_EXP and layer_of(2) is not None:
                        m = n + 2
                        act.wait_ge(lrelu_ready, m + 1)
                        act.wait_ge(shift_steps, 2 * m + 2)
                        act.wait_ge(eT_psum, at_least_0(m))
                        act.wait_ge(einv_ready, at_least_0(m))
                        for i in range(Q):
                            at = slice(i * P, (i + 1) * P)
                            nc.scalar.activation(e[:, at], s[:, at], ACT.Exp, bias=shift[:, i:i + 1],
                                                 accum_out=e_sum[:, i:i + 1]).then_inc(e_ready, 1)
                    if f == AT_YN and layer_of(-1) is not None:
                        m = n - 1
                        act.wait_ge(shift2_ready, m + 1)
                        act.wait_ge(rstd2_ready, m + 1)
                        k = m - (layers - 1) * groups
                        if layer_of(-1) < layers - 1 or isinstance(k, int) and k == 0:
                            act.wait_ge(x_stored, at_least_0(16 * m))
                        else:
                            act.wait_ge(z_ready, k)
                        for i in range(Q):
                            nc.scalar.activation(y_n[:, i, :], ps_r[i // 2][:, (i % 2) * D:(i % 2 + 1) * D], ACT.Identity,
                                                 bias=shift2[:, i:i + 1], scale=rstd2[:, i:i + 1]).then_inc(yn_ready, 1)
                    if f == AT_HT and layer_of(1) is not None:
                        m, layer = n + 1, layer_of(1)
                        act.wait_ge(yT_ready, at_least_0(2 * (m - 2) + 2))
                        for t in range(DT):
                            act.wait_ge(hT_psum, 2 * m + t + 1)
                            nc.scalar.activation(hT[1 - par][:, t, :], ps_h[t][:, :], ACT.Identity,
                                                 bias=mem["beta1"][:, layer, t:t + 1],
                                                 scale=mem["g1"][:, layer, t:t + 1]).then_inc(hT_ready, 1)
                    if f == 7 and layer_of(2) is not None:
                        m = n + 2
                        act.wait_ge(eT_psum, m + 1)
                        act.wait_ge(agg_psum, at_least_0(4 * m))
                        nc.scalar.activation(eT_hi[:, :], ps_s[:, :], ACT.Copy).then_inc(eT_hi_ready, 1)
                    if layer_of(0) is not None:
                        up(n, layer_of(0), f)
            run(act, step)

        @block.vector
        def _(dve):
            v = nc.vector

            def low(n, f):
                dve.wait_ge(g_hi_ready, 8 * n + f + 1)
                dve.wait_ge(y_psum, at_least_0(8 * n + f - 1))
                v.tensor_tensor(g_lo[f % 2][:, :], g[f % 2][:, :], g_hi[f % 2][:, :].bitcast(fp32), ALU.subtract)\
                 .then_inc(g_lo_ready, 1)

            def mean_and_variance(stats, mv, var, stats_ready, mv_ready, var_ready, m):
                stats_ready_count = worked_out(dve, 4 * m + 4)
                dve.wait_ge(begun, 1)
                dve.wait_ge(stats_ready, stats_ready_count)
                for i in range(Q):
                    v.bn_aggr(mv[:, i, :], stats[:, i, :]).then_inc(mv_ready, 1)
                dve.wait_ge(mv_ready, 4 * m + 4)
                v.tensor_scalar(var[:, :], mv[:, :, 1], EPS, None, ALU.add).then_inc(var_ready, 1)

            def node_scores(m, q, layer, graphs):
                for i in graphs:
                    for j, dst in enumerate((si, sj)):
                        v.tensor_tensor_reduce(
                            out=dump[:, 2 * i + j, :], in0=x[q][:, i, :],
                            in1=mem["attn_w"][:, layer, j * D:(j + 1) * D], scale=1.0, scalar=0.0,
                            op0=ALU.mult, op1=ALU.add, accum_out=dst[:, i:i + 1]).then_inc(sij_ready, 1)

            def step(n, par, layer_of):
                if layer_of(-1) is not None:
                    low(n - 1, 7)
                if layer_of(2) is not None:
                    m = n + 2
                    sj_spread_count, e_ready_count = worked_out(dve, m + 1), worked_out(dve, at_least_0(4 * m))
                    dve.wait_ge(begun, 1)
                    dve.wait_ge(sj_spread, sj_spread_count)
                    dve.wait_ge(e_ready, e_ready_count)
                    for i in range(Q):
                        at = slice(i * P, (i + 1) * P)
                        last = v.tensor_tensor_reduce(out=s[:, at], in0=ps_s[:, at], in1=mask[par][:, at], scale=1.0,
                                                      scalar=2 * MASKED, op0=ALU.add, op1=ALU.max,
                                                      accum_out=top[:, i:i + 1])
                    last.then_inc(s_ready, 1)
                    dve.wait_ge(s_ready, m + 1)
                    dve.wait_ge(sib_ready, m + 1)
                    v.scalar_tensor_tensor(out=top_n[:, :], in0=top[:, :], scalar=-1.0, in1=si_b[:, :],
                                           op0=ALU.mult, op1=ALU.subtract).then_inc(shift_steps, 1)
                    dve.wait_ge(shift_steps, 2 * m + 1)
                    v.scalar_tensor_tensor(out=shift[:, :], in0=top_n[:, :], scalar=0.2, in1=top_n[:, :],
                                           op0=ALU.mult, op1=ALU.min).then_inc(shift_steps, 1)
                if layer_of(0) is not None:
                    low(n, 0)
                if layer_of(-1) is not None:
                    m, layer = n - 1, layer_of(-1)
                    dve.wait_ge(y_psum, 8 * m + 8)
                    dve.wait_ge(rows_psum, at_least_0(2 * m))
                    for t in range(DT):
                        v.scalar_tensor_tensor(out=yT[:, t, :], in0=ps_y[t][:, :], scalar=mem["b2"][:, layer, t:t + 1],
                                               in1=hT[1 - par][:, t, :], op0=ALU.add, op1=ALU.add).then_inc(yT_ready, 1)
                if layer_of(2) is not None:
                    m = n + 2
                    dve.wait_ge(s_biased, 4 * m + 4)
                    v.scalar_tensor_tensor(out=s[:, :], in0=s[:, :], scalar=0.2, in1=s[:, :], op0=ALU.mult, op1=ALU.max)\
                     .then_inc(lrelu_ready, 1)
                if layer_of(0) is not None:
                    low(n, 1)
                if layer_of(1) is not None:
                    m = n + 1
                    dve.wait_ge(hT_psum, at_least_0(2 * m))
                    for i in range(Q):
                        dve.wait_ge(agg_psum, 4 * m + 2 * (i // 2) + 2)
                        v.scalar_tensor_tensor(out=u[:, i, :], in0=ps_u[i // 2][:, (i % 2) * D:(i % 2 + 1) * D],
                                               scalar=e_inv[:, i:i + 1], in1=x[1 - par][:, i, :],
                                               op0=ALU.mult, op1=ALU.add).then_inc(u_ready, 1)
                if layer_of(1) is not None:
                    m = n + 1
                    dve.wait_ge(rstd1_ready, at_least_0(m))
                    for i in range(Q):
                        dve.wait_ge(u_ready, 4 * m + i + 1)
                        v.bn_stats(stats1[:, i, :], u[:, i, :]).then_inc(stats1_ready, 1)
                    mean_and_variance(stats1, mv1, var1, stats1_ready, mv1_ready, var1_ready, m)
                if layer_of(-1) is not None:
                    m = n - 1
                    dve.wait_ge(rstd2_ready, at_least_0(m))
                    for i in range(Q):
                        dve.wait_ge(rows_psum, 2 * m + i // 2 + 1)
                        v.bn_stats(stats2[:, i, :], ps_r[i // 2][:, (i % 2) * D:(i % 2 + 1) * D]).then_inc(stats2_ready, 1)
                if layer_of(0) is not None:
                    low(n, 2)
                if layer_of(-1) is not None:
                    mean_and_variance(stats2, mv2, var2, stats2_ready, mv2_ready, var2_ready, m)
                if layer_of(1) is not None:
                    m = n + 1
                    dve.wait_ge(rstd1_ready, m + 1)
                    for i in range(Q):
                        v.tensor_scalar(u[:, i, :], u[:, i, :], mv1[:, i, 0:1], rstd1[:, i:i + 1],
                                        ALU.subtract, ALU.mult).then_inc(un_ready, 1)
                if layer_of(0) is not None:
                    low(n, 3)
                if layer_of(-1) is not None:
                    m = n - 1
                    dve.wait_ge(rstd2_ready, m + 1)
                    dve.wait_ge(yn_ready, at_least_0(4 * m))
                    v.scalar_tensor_tensor(out=shift2[:, :], in0=mv2[:, :, 0], scalar=-1.0, in1=rstd2[:, :],
                                           op0=ALU.mult, op1=ALU.mult).then_inc(shift2_ready, 1)
                if layer_of(-2) == layers - 1:
                    k = n - 2 - (layers - 1) * groups
                    dve.wait_ge(xout_ready, at_least_0(4 * k))
                    dve.wait_ge(z_ready, k + 1)
                    for i in range(Q):
                        v.bn_stats(stats3[:, i, :], x_first[:, i, :]).then_inc(stats3_ready, 1)
                    mean_and_variance(stats3, mv3, var3, stats3_ready, mv3_ready, var3_ready, k)
                    if layer_of(0) is None:
                        dve.wait_ge(rstd3_ready, k + 1)
                        dve.wait_ge(out_stored, at_least_0(16 * Q * k))
                        for i in range(Q):
                            v.tensor_scalar(x_out[:, i, :], x_first[:, i, :], mv3[:, i, 0:1], rstd3[:, i:i + 1],
                                            ALU.subtract, ALU.mult).then_inc(xout_ready, 1)
                if layer_of(0) is not None:
                    low(n, 4)
                if layer_of(3) is not None:
                    m, layer = n + 3, layer_of(3)
                    if isinstance(m, int) and m == 0:
                        dve.wait_ge(attn_w_in, 16)
                    elif isinstance(m, int) and m == groups:
                        dve.wait_ge(attn_w_rest_in, 16 * (layers - 1))
                    dve.wait_ge(x_in[1 - par], 16 * (m - 1 + par) + 32)
                    dve.wait_ge(sj_spread, at_least_0(m))
                    dve.wait_ge(s_biased, at_least_0(4 * m))
                    node_scores(m, 1 - par, layer, range(Q // 2))
                if layer_of(0) is not None:
                    low(n, 5)
                if layer_of(1) is not None:
                    m = n + 1
                    dve.wait_ge(ff_psum, at_least_0(8 * (m - 2) + 8))
                    for t in range(DT):
                        dve.wait_ge(hT_ready, 2 * m + t + 1)
                        v.tensor_copy(hT_hi[1 - par][:, t, :], hT[1 - par][:, t, :]).then_inc(hT_hi_ready, 1)
                        dve.wait_ge(hT_hi_ready, 2 * m + t + 1)
                        v.tensor_tensor(hT_lo[1 - par][:, t, :], hT[1 - par][:, t, :],
                                        hT_hi[1 - par][:, t, :].bitcast(fp32), ALU.subtract).then_inc(hT_lo_ready, 1)
                if layer_of(0) is not None:
                    low(n, 6)
                if layer_of(3) is not None:
                    m, layer = n + 3, layer_of(3)
                    node_scores(m, 1 - par, layer, range(Q // 2, Q))
                    if isinstance(m, int) and m == 0:
                        dve.wait_ge(attn_b_in, 16)
                    dve.wait_ge(sij_ready, 2 * Q * (m + 1))
                    v.tensor_scalar(si_b[:, :], si[:, :], mem["attn_b"][:, layer:layer + 1], None, ALU.add)\
                     .then_inc(sib_ready, 1)
                if layer_of(2) is not None:
                    m = n + 2
                    dve.wait_ge(e_ready, 4 * m + 4)
                    v.reciprocal(e_inv[:, :], e_sum[:, :]).then_inc(einv_ready, 1)
                if layer_of(2) is not None:
                    m = n + 2
                    dve.wait_ge(eT_hi_ready, m + 1)
                    v.tensor_tensor(eT_lo[:, :], ps_s[:, :], eT_hi[:, :].bitcast(fp32), ALU.subtract)\
                     .then_inc(eT_lo_ready, 1)
            run(dve, step)

        @block.tensor
        def _(pe):
            def up(n, par, layer, f):
                pe.wait_ge(g_ready, at_least_0(8 * n + f - 1))
                if f == 0:
                    pe.wait_ge(hT_lo_ready, 2 * n + 2)
                    if isinstance(n, int) and n % groups == 0:
                        pe.wait_ge(w_lo_ready, 2 * layer + 2)
                at = slice(f * P, (f + 1) * P)
                parts = [(w, t, h) for t in range(DT)
                         for w, h in ((mem["W1_hi"], hT_hi), (mem["W1_hi"], hT_lo), (mem["W1_lo"], hT_hi))]
                for c, (w, t, h) in enumerate(parts):
                    last = nc.tensor.matmul(ps_ff[f % 2][:, :], w[layer][:, t, at], h[par][:, t, :],
                                            start=(c == 0), stop=(c == len(parts) - 1))
                last.then_inc(ff_psum, 1)

            def down(n, layer, f):
                pe.wait_ge(g_hi_ready, 8 * n + f + 1)
                if f == 0:
                    pe.wait_ge(yT_ready, at_least_0(2 * n))
                last = None
                for t in range(DT):
                    at = slice(t * P, (t + 1) * P)
                    nc.tensor.matmul(ps_y[t][:, :], mem["W2_hi"][layer][:, f, at], g_hi[f % 2][:, :],
                                     start=(f == 0), stop=False)
                    nc.tensor.matmul(ps_y[t][:, :], mem["W2_lo"][layer][:, f, at], g_hi[f % 2][:, :],
                                     start=False, stop=False)
                pe.wait_ge(g_lo_ready, 8 * n + f + 1)
                for t in range(DT):
                    at = slice(t * P, (t + 1) * P)
                    last = nc.tensor.matmul(ps_y[t][:, :], mem["W2_hi"][layer][:, f, at], g_lo[f % 2][:, :],
                                            start=False, stop=(f == FT - 1))
                last.then_inc(y_psum, 1)

            def step(n, par, layer_of):
                for f in range(FT):
                    if f == AT_HT_PE and layer_of(1) is not None:
                        m = n + 1
                        for t in range(DT):
                            if t == 0:
                                pe.wait_ge(u_ready, 4 * m + 4)
                            else:
                                pe.wait_ge(yn_ready, at_least_0(4 * (n - 1) + 2))
                            for i in range(Q):
                                if t == 0:
                                    pe.wait_ge(un_ready, 4 * m + i + 1)
                                last = nc.tensor.transpose(ps_h[t][:, i * P:(i + 1) * P],
                                                           u[:, i, t * P:(t + 1) * P], ident[:, :])
                            last.then_inc(hT_psum, 1)
                    if f == AT_ROWS and layer_of(-1) is not None:
                        m = n - 1
                        pe.wait_ge(yT_ready, 2 * m + 2)
                        if layer_of(0) is not None:
                            pe.wait_ge(hT_ready, 2 * n + 2)
                        for b in range(2):
                            if b == 1 and layer_of(1) is not None:
                                pe.wait_ge(u_ready, 4 * (n + 1) + 2)
                            for i in (2 * b, 2 * b + 1):
                                for t in range(DT):
                                    last = nc.tensor.transpose(
                                        ps_r[b][:, (i % 2) * D + t * P:(i % 2) * D + (t + 1) * P],
                                        yT[:, t, i * P:(i + 1) * P], ident[:, :])
                            last.then_inc(rows_psum, 1)
                    if f < 2:
                        if layer_of(-1) is not None:
                            down(n - 1, layer_of(-1), FT - 2 + f)
                    elif layer_of(0) is not None:
                        down(n, layer_of(0), f - 2)
                    if layer_of(0) is not None:
                        up(n, par, layer_of(0), f)
                    if f == 1 and layer_of(1) is not None:
                        m = n + 1
                        pe.wait_ge(x_lo_ready, m + 1)
                        pe.wait_ge(eT_lo_ready, m + 1)
                        pe.wait_ge(yn_ready, at_least_0(4 * (n - 2) + 4))
                        pe.wait_ge(hT_ready, at_least_0(2 * n + 2))
                        for i in range(Q):
                            at = slice(i * P, (i + 1) * P)
                            dst = ps_u[i // 2][:, (i % 2) * D:(i % 2 + 1) * D]
                            nc.tensor.matmul(dst, eT_hi[:, at], x_hi[:, i, :], start=True, stop=False)
                            nc.tensor.matmul(dst, eT_hi[:, at], x_lo[:, i, :], start=False, stop=False)
                            nc.tensor.matmul(dst, eT_lo[:, at], x_hi[:, i, :], start=False, stop=True)\
                              .then_inc(agg_psum, 1)
                    if f == 0 and layer_of(2) is not None:
                        m = n + 2
                        pe.wait_ge(sij_ready, 2 * Q * (m + 1))
                        pe.wait_ge(eT_lo_ready, at_least_0(m))
                        for i in range(Q):
                            last = nc.tensor.transpose(ps_s[:, i * P:(i + 1) * P],
                                                       sj[:, i:i + 1].broadcast_to([P, P]), ident[:, :])
                        last.then_inc(sj_spread, 1)
                    if f == AT_ET and layer_of(2) is not None:
                        m = n + 2
                        pe.wait_ge(s_ready, m + 1)
                        for i in range(Q):
                            pe.wait_ge(e_ready, 4 * m + i + 1)
                            last = nc.tensor.transpose(ps_s[:, i * P:(i + 1) * P], e[:, i * P:(i + 1) * P], ident[:, :])
                        last.then_inc(eT_psum, 1)
            run(pe, step)
HEADS = 8
HD = D // HEADS
HALF = HEADS // 2
STACK = 3 * HD
STACKED = 3 * HALF * 16
SCALE = HD ** -0.5
LIFT = 2.0 ** 14


def first_layer(nc, mem, groups, x_in_dram, adj_dram, weights, raw, columns, x1, masks):
    ctx = ExitStack()
    with ctx:
        def sb(name, shape, dt=fp32):
            return ctx.enter_context(nc.sbuf_tensor("l0_" + name, shape, dt))

        def bank(name):
            return ctx.enter_context(nc.psum_tensor("l0_" + name, [P, R], fp32))

        def sem(name):
            return ctx.enter_context(nc.semaphore("l0_" + name))

        ident = mem["ident"]
        stage = mem["stage"]
        w_raw = stage[0][:, :].rearrange("p (j t d) -> p j t d", j=4, t=DT)
        w_hi = sb("w_hi", [P, 4, DT, D], fp32r)
        w_lo = sb("w_lo", [P, 4, DT, D], fp32r)
        xp = sb("xp", [P, Q, D])
        adj = sb("adj", [P, Q, P], mybir.dt.int32)
        reach = sb("reach", [P, Q, P])
        mask0 = [sb(f"mask0_{i}", [P, Q, P], bf16) for i in range(2)]
        mask1 = sb("mask1", [P, Q, P], bf16)
        xT_hi = sb("xT_hi", [P, DT, R], fp32r)
        xT_lo = sb("xT_lo", [P, DT, R], fp32r)
        qk = sb("qk", [P, 12, R], fp32r)
        q_whole = sb("q_whole", [P, R])
        qk_st = [sb(f"qk_st{i}", [STACK, 2, HALF, DT * R], fp32r) for i in range(2)]
        v_parts = [[sb(f"v_part{j}_{i}", [P, Q, D], bf16) for j in range(3)] for i in range(2)]
        v_whole = sb("v_whole", [P, Q, D])
        s = [sb(f"s0_{i}", [P, HEADS, P]) for i in range(2)]
        top = [sb(f"top0_{i}", [P, HEADS]) for i in range(2)]
        shift = [sb(f"shift0_{i}", [P, HEADS]) for i in range(2)]
        e = [sb(f"e0_{i}", [P, HEADS, P]) for i in range(2)]
        e_sum = [sb(f"e_sum0_{i}", [P, HEADS]) for i in range(2)]
        e_inv = [sb(f"e_inv0_{i}", [P, HEADS]) for i in range(2)]
        pT_hi = sb("pT_hi", [P, DT, R], mybir.dt.float16)
        pT_lo = sb("pT_lo", [P, DT, R], mybir.dt.float16)
        o = [sb(f"o{i}", [P, Q, D]) for i in range(2)]
        oT_hi = sb("oT_hi", [P, DT, R], fp32r)
        oT_lo = sb("oT_lo", [P, DT, R], fp32r)
        xo = sb("xo", [P, Q, D])
        y = sb("y0", [P, Q, D])
        stats = sb("stats0", [P, Q, 6])
        mv = sb("mv0", [P, Q, 2])
        var = sb("var0", [P, Q])
        rstd = sb("rstd0", [P, Q])
        yn = sb("yn0", [P, Q, D])
        half = sb("half0", [P, Q])

        ps_s = [bank(f"ps_s{i}") for i in range(DT)]
        ps_t = [bank(f"ps_t{i}") for i in range(DT)]
        ps_o = bank("ps_o")
        ps_r = [bank(f"ps_r{i}") for i in range(3)]

        w_in, w_hi_ready, w_lo_ready = sem("w_in"), sem("w_hi_ready"), sem("w_lo_ready")
        begun, stage_in, columns_in = sem("begun"), sem("stage_in"), sem("columns_in")
        edges_ready = sem("edges_ready")
        xp_in, adj_in, xo_in, stack_in = sem("xp_in"), sem("adj_in"), sem("xo_in"), sem("stack_in")
        mask0_ready, reach_ready, mask1_ready, mask1_stored = (
            sem("mask0_ready"), sem("reach_ready"), sem("mask1_ready"), sem("mask1_stored"))
        xT_psum, xT_hi_ready, xT_lo_ready = sem("xT_psum"), sem("xT_hi_ready"), sem("xT_lo_ready")
        qk_psum, qk_hi_ready, qk_lo_ready = sem("qk_psum"), sem("qk_hi_ready"), sem("qk_lo_ready")
        q_whole_ready, q_part_hi_ready, q_part_lo_ready = (
            sem("q_whole_ready"), sem("q_part_hi_ready"), sem("q_part_lo_ready"))
        v_psum, v_whole_ready = sem("v_psum"), sem("v_whole_ready")
        v_first_ready, v_rest_ready = sem("v_first_ready"), sem("v_rest_ready")
        v_second_ready, v_third_ready = sem("v_second_ready"), sem("v_third_ready")
        s_psum, s_ready, shift_ready = sem("s0_psum"), sem("s0_ready"), sem("shift0_ready")
        e_ready, e_inv_ready = sem("e0_ready"), sem("e_inv0_ready")
        pT_psum, pT_hi_ready, pT_lo_ready = sem("pT_psum"), sem("pT_hi_ready"), sem("pT_lo_ready")
        o_psum, o_ready = sem("o_psum"), sem("o_ready")
        oT_psum, oT_hi_ready, oT_lo_ready = sem("oT_psum"), sem("oT_hi_ready"), sem("oT_lo_ready")
        w_psum, y_ready = sem("w_psum"), sem("y_ready")
        stats_ready, mv_ready, var_ready = sem("stats0_ready"), sem("mv0_ready"), sem("var0_ready")
        centred = sem("centred")
        rstd_ready, yn_ready, x1_stored = sem("rstd0_ready"), sem("yn0_ready"), sem("x1_stored")

        def run(eng, step):
            def peeled(n):
                step(n, n % 2, lambda k: 0 <= n + k < groups)

            for n in range(-2, 4):
                peeled(n)
            with eng.Fori(4, groups - 5, 2) as t:
                step(t, 0, lambda k: True)
                step(t + 1, 1, lambda k: True)
            for n in range(groups - 4, groups + 2):
                peeled(n)

        def upto(count, limit):
            return max(min(count, limit), 0) if isinstance(count, int) else count

        block = ctx.enter_context(nc.Block())

        @block.sync
        def _(sp):
            def load_x(m):
                sp.dma_start(xp[:, :, :], x_in_dram[bass.ds(Q * m, Q), :, :].rearrange("q p d -> p q d")).then_inc(xp_in, 16)

            def load_adj(m):
                sp.dma_start(adj[:, :, :], adj_dram[bass.ds(Q * m, Q), :, :].rearrange("q p n -> p q n")).then_inc(adj_in, 16)

            def stack(dst, blocks):
                for b in blocks:
                    for h in range(HALF):
                        rows = slice(h * HD, (h + 1) * HD)
                        high_high = qk[rows, :, :].rearrange("p (x t) r -> p x (t r)", t=4)[:, 0:2, 0:DT * R]
                        high_low = qk[rows, :, :].rearrange("p (x t) r -> p x (t r)", t=6)[:, :, 0:DT * R]
                        low_high = qk[rows, 2:6, :].rearrange("p (x t) r -> p x (t r)", t=2)
                        src = (high_high, high_low, low_high)[b]
                        sp.dma_start(dst[b * HD:(b + 1) * HD, :, h, :].bitcast(fp32),
                                     src.bitcast(fp32)).then_inc(stack_in, 16)

            load_x(0)
            for j, w in enumerate(weights):
                sp.dma_start(w_raw[:, j, :, :], w.rearrange("(t p) n -> p t n", p=P)).then_inc(w_in, 16)
            load_adj(0)

            def step(n, par, has):
                if isinstance(n, int) and n in (2, 3):
                    sp.wait_ge(w_lo_ready, 4)
                    name, t = WEIGHTS[n - 2]
                    sp.dma_start(stage[n - 2][:, :].rearrange("p (t n) -> p t n", t=t),
                                 raw[name][0, :, :].rearrange("(t p) n -> p t n", p=P)).then_inc(stage_in, 16)
                    for name in columns[2 * (n - 2):2 * (n - 2) + 2]:
                        for l in range(raw[name].shape[0]):
                            sp.dma_start(mem[name][:, l, :], raw[name][l, :].rearrange("(t p) -> p t", p=P),
                                         allow_slow_non_contiguous=True).then_inc(columns_in, 16)
                if has(1):
                    m = n + 1
                    mask1_ready_count = worked_out(sp, m + 1)
                    sp.wait_ge(begun, 1)
                    sp.wait_ge(mask1_ready, mask1_ready_count)
                    sp.dma_start(masks[bass.ds(m, 1), :, :].rearrange("o p n -> (o p) n"),
                                 mask1[:, :, :].rearrange("p q n -> p (q n)")).then_inc(mask1_stored, 16)
                    if has(2):
                        load_adj(m + 1)
                if has(-1):
                    m = n - 1
                    y_ready_count = worked_out(sp, at_least_0(2 * m))
                    sp.wait_ge(begun, 1)
                    sp.wait_ge(y_ready, y_ready_count)
                    sp.dma_start(xo[:, :, :], x_in_dram[bass.ds(Q * m, Q), :, :].rearrange("q p d -> p q d")).then_inc(xo_in, 16)
                if has(1):
                    m = n + 1
                    qk_count, s_psum_count = worked_out(sp, 3 * m + 3), worked_out(sp, at_least_0(4 * n))
                    q_part_count = worked_out(sp, m + 1)
                    sp.wait_ge(begun, 1)
                    sp.wait_ge(qk_hi_ready, qk_count)
                    sp.wait_ge(q_part_hi_ready, q_part_count)
                    sp.wait_ge(s_psum, s_psum_count)
                    stack(qk_st[1 - par], (0,))
                    sp.wait_ge(qk_lo_ready, qk_count)
                    sp.wait_ge(q_part_lo_ready, q_part_count)
                    stack(qk_st[1 - par], (1, 2))
                if has(-2):
                    m = n - 2
                    yn_ready_count = worked_out(sp, 4 * m + 4)
                    sp.wait_ge(begun, 1)
                    sp.wait_ge(yn_ready, yn_ready_count)
                    sp.dma_start(x1[bass.ds(m, 1), :, :].rearrange("o p n -> (o p) n"),
                                 yn[:, :, :].rearrange("p q d -> p (q d)")).then_inc(x1_stored, 16)
                if has(3):
                    m = n + 2
                    xT_psum_count = worked_out(sp, at_least_0(2 * m + 2))
                    sp.wait_ge(begun, 1)
                    sp.wait_ge(xT_psum, xT_psum_count)
                    load_x(m + 1)
            run(sp, step)
            sp.wait_ge(x1_stored, 16 * groups)
            sp.wait_ge(mask1_stored, 16 * groups)
            sp.wait_ge(stage_in, 32)
            sp.wait_ge(columns_in, 16 * len(columns) * raw["b1"].shape[0])

        @block.gpsimd
        def _(pool):
            pool.memset(half[:, :], -0.5).then_inc(begun, 1)
            pool.wait_ge(begun, 1)

            def step(n, par, has):
                if has(1):
                    m = n + 1
                    adj_in_count, s_ready_count = worked_out(pool, 16 * m + 16), worked_out(pool, at_least_0(4 * n))
                    mask1_ready_count = worked_out(pool, at_least_0(m))
                    pool.wait_ge(begun, 1)
                    pool.wait_ge(adj_in, adj_in_count)
                    pool.wait_ge(mask1_ready, mask1_ready_count)
                    pool.wait_ge(s_ready, s_ready_count)
                    nc.gpsimd.tensor_scalar(mask0[1 - par][:, :, :], adj[:, :, :], 0.0, MASKED, ALU.is_equal, ALU.mult)\
                      .then_inc(mask0_ready, 1)
                    nc.gpsimd.tensor_scalar(reach[:, :, :], adj[:, :, :], 1.0, 0.0, ALU.mult, ALU.add).then_inc(edges_ready, 1)
                    pool.wait_ge(edges_ready, m + 1)
                    nc.gpsimd.tensor_tensor(reach[:, :, :], reach[:, :, :], ident[:, :].unsqueeze(1).broadcast_to([P, Q, P]),
                                            ALU.add).then_inc(reach_ready, 1)
                    reach_ready_count, mask1_stored_count = worked_out(pool, m + 1), worked_out(pool, at_least_0(16 * m))
                    pool.wait_ge(begun, 1)
                    pool.wait_ge(reach_ready, reach_ready_count)
                    pool.wait_ge(mask1_stored, mask1_stored_count)
                    nc.gpsimd.tensor_scalar(mask1[:, :, :], reach[:, :, :], 0.0, MASKED, ALU.is_le, ALU.mult)\
                      .then_inc(mask1_ready, 1)
                    q_whole_count, stack_in_count = worked_out(pool, m + 1), worked_out(pool, at_least_0(STACKED * m))
                    pool.wait_ge(begun, 1)
                    pool.wait_ge(q_whole_ready, q_whole_count)
                    pool.wait_ge(stack_in, stack_in_count)
                    nc.gpsimd.tensor_scalar(qk[:, 1, :], q_whole[:, :], 1.0, 0.0, ALU.mult, ALU.add)\
                      .then_inc(q_part_hi_ready, 1)
                    pool.wait_ge(q_part_hi_ready, m + 1)
                    nc.gpsimd.tensor_tensor(qk[:, 3, :], q_whole[:, :], qk[:, 1, :].bitcast(fp32), ALU.subtract)\
                      .then_inc(q_part_lo_ready, 1)
                if has(-2):
                    m = n - 2
                    pool.wait_ge(var_ready, m + 1)
                    nc.gpsimd.tensor_tensor(rstd[:, :], var[:, :], half[:, :], ALU.pow).then_inc(rstd_ready, 1)
                    if has(0):
                        rstd_ready_count, x1_stored_count = worked_out(pool, m + 1), worked_out(pool, at_least_0(16 * m))
                        pool.wait_ge(begun, 1)
                        pool.wait_ge(rstd_ready, rstd_ready_count)
                        pool.wait_ge(x1_stored, x1_stored_count)
                        nc.gpsimd.tensor_tensor(yn[:, :, :], y[:, :, :], mv[:, :, 0:1].broadcast_to([P, Q, D]), ALU.subtract)\
                          .then_inc(centred, 1)
                        pool.wait_ge(centred, m + 1)
                        nc.gpsimd.tensor_tensor(yn[:, :, :], yn[:, :, :], rstd[:, :].unsqueeze(2).broadcast_to([P, Q, D]),
                                                ALU.mult).then_inc(yn_ready, Q)
                if has(1):
                    m = n + 1
                    for b in range(2):
                        at = slice(2 * b, 2 * b + 2)
                        first, second, third = (part[:, at, :] for part in v_parts[1 - par])
                        v_whole_count = worked_out(pool, 2 * m + b + 1)
                        pool.wait_ge(begun, 1)
                        pool.wait_ge(v_whole_ready, v_whole_count)
                        nc.gpsimd.tensor_scalar(first, v_whole[:, at, :], 1.0, 0.0, ALU.mult, ALU.add)\
                          .then_inc(v_first_ready, 1)
                        pool.wait_ge(v_first_ready, 2 * m + b + 1)
                        nc.gpsimd.tensor_tensor(v_whole[:, at, :], v_whole[:, at, :], first, ALU.subtract)\
                          .then_inc(v_rest_ready, 1)
                        v_rest_count = worked_out(pool, 2 * m + b + 1)
                        pool.wait_ge(begun, 1)
                        pool.wait_ge(v_rest_ready, v_rest_count)
                        nc.gpsimd.tensor_scalar(second, v_whole[:, at, :], 1.0, 0.0, ALU.mult, ALU.add)\
                          .then_inc(v_second_ready, 1)
                        pool.wait_ge(v_second_ready, 2 * m + b + 1)
                        nc.gpsimd.tensor_tensor(third, v_whole[:, at, :], second, ALU.subtract).then_inc(v_third_ready, 1)
            run(pool, step)

        @block.scalar
        def _(act):
            def copy(dst, src, ready, scale=1.0):
                nc.scalar.activation(dst, src, ACT.Copy, scale=scale).then_inc(ready, 1)

            def copy_of_v(m, b):
                act.wait_ge(v_third_ready, at_least_0(2 * (m - 1) + b + 1))
                act.wait_ge(v_psum, 2 * m + b + 1)
                copy(v_whole[:, 2 * b:2 * b + 2, :], ps_r[b][:, :].rearrange("p (q d) -> p q d", q=2), v_whole_ready)

            def exponentials(i, heads):
                for h in heads:
                    nc.scalar.activation(e[i % 2][:, h, :], s[i % 2][:, h, :], ACT.Exp, bias=shift[i % 2][:, h:h + 1],
                                         scale=SCALE, accum_out=e_sum[i % 2][:, h:h + 1]).then_inc(e_ready, 1)

            def step(n, par, has):
                for i in range(Q):
                    gi = 4 * n + i
                    if i == 2 and has(-1):
                        m = n - 1
                        act.wait_ge(w_psum, at_least_0(2 * m))
                        for t in range(DT):
                            act.wait_ge(oT_psum, 2 * m + t + 1)
                            copy(oT_hi[:, t, :], ps_r[1 + t][:, :], oT_hi_ready)
                    if has(-1) if i == 0 else has(0):
                        act.wait_ge(o_psum, at_least_0(gi - 1))
                        for t in range(DT):
                            act.wait_ge(pT_psum, 2 * (gi - 1) + t + 1)
                            copy(pT_hi[:, t, :], ps_t[t][:, :], pT_hi_ready, LIFT)
                    if i == 3 and has(2):
                        m = n + 2
                        act.wait_ge(v_psum, at_least_0(2 * m))
                        for t in range(DT):
                            act.wait_ge(xT_psum, 2 * m + t + 1)
                            copy(xT_hi[:, t, :], ps_r[2 * (1 - t)][:, :], xT_hi_ready)
                    if i == 1 and has(1):
                        act.wait_ge(qk_psum, 4 * (n + 1) + 3)
                        copy(qk[:, 4, :], ps_r[2][:, :], qk_hi_ready)
                    if has(0):
                        act.wait_ge(shift_ready, gi + 1)
                        act.wait_ge(pT_psum, at_least_0(2 * (gi - 1)))
                        act.wait_ge(e_inv_ready, at_least_0(gi - 1))
                        exponentials(i, range(HALF))
                    if i == 0 and has(1):
                        m = n + 1
                        act.wait_ge(stack_in, at_least_0(STACKED * m))
                        act.wait_ge(qk_psum, 4 * m + 1)
                        copy(qk[:, 0, :], ps_r[0][:, :], qk_hi_ready)
                    if i == 1 and has(1):
                        act.wait_ge(qk_psum, 4 * (n + 1) + 4)
                        copy(qk[:, 5, :], ps_r[0][:, :], qk_hi_ready)
                    if i == 2 and has(1):
                        act.wait_ge(o_psum, at_least_0(4 * n))
                        copy_of_v(n + 1, 0)
                    if has(0):
                        exponentials(i, range(HALF, HEADS))
                    if i == 0 and has(1):
                        m = n + 1
                        act.wait_ge(q_part_lo_ready, at_least_0(m))
                        act.wait_ge(qk_psum, 4 * m + 2)
                        copy(q_whole[:, :], ps_r[1][:, :], q_whole_ready)
                    if i == 2 and has(1):
                        copy_of_v(n + 1, 1)
            run(act, step)

        @block.vector
        def _(dve):
            v = nc.vector
            dve.wait_ge(w_in, 64)
            v.tensor_scalar(w_raw[:, 3, :, :], w_raw[:, 3, :, :], 1.0 / LIFT, None, ALU.mult).then_inc(w_hi_ready, 1)
            dve.wait_ge(w_hi_ready, 1)
            for j in range(4):
                v.tensor_copy(w_hi[:, j, :, :], w_raw[:, j, :, :]).then_inc(w_hi_ready, 1)
            for j in range(4):
                dve.wait_ge(w_hi_ready, j + 2)
                v.tensor_tensor(w_lo[:, j, :, :], w_raw[:, j, :, :], w_hi[:, j, :, :].bitcast(fp32), ALU.subtract)\
                 .then_inc(w_lo_ready, 1)

            def low(dst, src, hi, ready):
                v.tensor_tensor(dst, src, hi.bitcast(fp32), ALU.subtract).then_inc(ready, 1)

            def low_of_q_or_k(m, c):
                dve.wait_ge(qk_hi_ready, 3 * m + max(c, 1))
                plane = 4 * (c // 2) + c % 2
                low(qk[:, plane + 2, :], ps_r[c % 3][:, :], qk[:, plane, :], qk_lo_ready)

            def low_of_x(m, t):
                dve.wait_ge(xT_hi_ready, 2 * m + t + 1)
                low(xT_lo[:, t, :], ps_r[2 * (1 - t)][:, :], xT_hi[:, t, :], xT_lo_ready)

            def residual(m, b):
                at = slice(2 * b, 2 * b + 2)
                dve.wait_ge(w_psum, 2 * m + b + 1)
                v.tensor_tensor(y[:, at, :], ps_r[1 + b][:, :].rearrange("p (q d) -> p q d", q=2),
                                xo[:, at, :], ALU.add).then_inc(y_ready, 1)

            def moments(m, norm_too):
                dve.wait_ge(yn_ready, at_least_0(4 * m))
                for q in range(Q):
                    dve.wait_ge(y_ready, 2 * m + q // 2 + 1)
                    v.bn_stats(stats[:, q, :], y[:, q, :]).then_inc(stats_ready, 1)
                stats_ready_count = worked_out(dve, 4 * m + 4)
                dve.wait_ge(begun, 1)
                dve.wait_ge(stats_ready, stats_ready_count)
                for q in range(Q):
                    v.bn_aggr(mv[:, q, :], stats[:, q, :]).then_inc(mv_ready, 1)
                dve.wait_ge(mv_ready, 4 * m + 4)
                v.tensor_scalar(var[:, :], mv[:, :, 1], EPS, None, ALU.add).then_inc(var_ready, 1)
                if norm_too:
                    dve.wait_ge(rstd_ready, m + 1)
                    dve.wait_ge(x1_stored, at_least_0(16 * m))
                    for q in range(Q):
                        v.tensor_scalar(yn[:, q, :], y[:, q, :], mv[:, q, 0:1], rstd[:, q:q + 1],
                                        ALU.subtract, ALU.mult).then_inc(yn_ready, 1)

            def step(n, par, has):
                for i in range(Q):
                    gi = 4 * n + i
                    if has(0):
                        s_psum_count, e_ready_count = worked_out(dve, gi + 1), worked_out(dve, at_least_0(8 * (gi - 1)))
                        mask0_count = worked_out(dve, n + 1)
                        dve.wait_ge(begun, 1)
                        dve.wait_ge(mask0_ready, mask0_count)
                        dve.wait_ge(s_psum, s_psum_count)
                        dve.wait_ge(e_ready, e_ready_count)
                        for h in range(HEADS):
                            last = v.tensor_tensor_reduce(
                                out=s[i % 2][:, h, :], in0=ps_s[h // HALF][:, (h % HALF) * P:(h % HALF + 1) * P],
                                in1=mask0[par][:, i, :], scale=1.0, scalar=2 * MASKED, op0=ALU.add, op1=ALU.max,
                                accum_out=top[i % 2][:, h:h + 1])
                        last.then_inc(s_ready, 1)
                    if has(-1) if i == 0 else has(0):
                        dve.wait_ge(e_ready, 8 * gi)
                        dve.wait_ge(o_ready, at_least_0(gi - 2))
                        v.reciprocal(e_inv[1 - i % 2][:, :], e_sum[1 - i % 2][:, :]).then_inc(e_inv_ready, 1)
                    if has(0):
                        dve.wait_ge(s_ready, gi + 1)
                        v.tensor_scalar(shift[i % 2][:, :], top[i % 2][:, :], -SCALE, None, ALU.mult).then_inc(shift_ready, 1)
                    if i == 0 and has(-2):
                        residual(n - 2, 1)
                    if i == 2 and has(-1):
                        dve.wait_ge(oT_hi_ready, 2 * (n - 1) + 1)
                        low(oT_lo[:, 0, :], ps_r[1][:, :], oT_hi[:, 0, :], oT_lo_ready)
                    if has(-1) if i < 2 else has(0):
                        k = (i - 2) % Q
                        q = par if i >= 2 else 1 - par
                        dve.wait_ge(o_psum, gi - 1)
                        dve.wait_ge(e_inv_ready, gi - 1)
                        v.scalar_tensor_tensor(
                            out=o[q][:, k, :].rearrange("p (h c) -> p h c", h=HEADS),
                            in0=ps_o[:, 0:D].rearrange("p (h c) -> p h c", h=HEADS), scalar=0.0,
                            in1=e_inv[i % 2][:, :].unsqueeze(2).broadcast_to([P, HEADS, HD]), op0=ALU.max, op1=ALU.mult)\
                         .then_inc(o_ready, 1)
                    if i == 2 and has(-1):
                        m = n - 1
                        dve.wait_ge(oT_hi_ready, 2 * m + 2)
                        low(oT_lo[:, 1, :], ps_r[2][:, :], oT_hi[:, 1, :], oT_lo_ready)
                    if has(-1) if i == 0 else has(0):
                        for t in range(DT):
                            dve.wait_ge(pT_hi_ready, 2 * (gi - 1) + t + 1)
                            v.scalar_tensor_tensor(out=pT_lo[:, t, :], in0=ps_t[t][:, :], scalar=LIFT, in1=pT_hi[:, t, :],
                                                   op0=ALU.mult, op1=ALU.subtract).then_inc(pT_lo_ready, 1)
                            if i == 3 and t == 0 and has(2):
                                low_of_x(n + 2, 0)
                    if i == (0 if has(0) else 2) and has(-2):
                        moments(n - 2, not has(0))
                    if i < 2 and has(1):
                        m = n + 1
                        low_of_q_or_k(m, 2 * i)
                        if i == 1:
                            low_of_q_or_k(m, 3)
                    if i == 3 and has(2):
                        if not has(0):
                            low_of_x(n + 2, 0)
                        low_of_x(n + 2, 1)
                    if i == 3 and has(-1):
                        m = n - 1
                        dve.wait_ge(xo_in, 16 * m + 16)
                        dve.wait_ge(yn_ready, at_least_0(4 * m))
                        residual(m, 0)
            run(dve, step)

        @block.tensor
        def _(pe):
            def split_product(dst, pairs, signal):
                n = 3 * len(pairs)
                c = 0
                for (l_hi, l_lo), (r_hi, r_lo) in pairs:
                    for left, right in ((l_hi, r_hi), (l_hi, r_lo), (l_lo, r_hi)):
                        last = nc.tensor.matmul(dst, left, right, start=(c == 0), stop=(c == n - 1))
                        c += 1
                if signal is not None:
                    last.then_inc(signal, 1)

            def transposes(dst, srcs, signal):
                for j, src in enumerate(srcs):
                    last = nc.tensor.transpose(dst[:, j * P:(j + 1) * P], src, ident[:, :])
                last.then_inc(signal, 1)

            def q_or_k(c):
                at = slice((c % 2) * P, (c % 2 + 1) * P)
                split_product(ps_r[c % 3][:, :],
                              [((w_hi[:, c // 2, t, at], w_lo[:, c // 2, t, at]),
                                (xT_hi[:, t, :], xT_lo[:, t, :])) for t in range(DT)], qk_psum)

            def rows_times(dst, lhs_hi, lhs_lo, j, b, signal):
                for q in (2 * b, 2 * b + 1):
                    rows = slice(q * P, (q + 1) * P)
                    split_product(dst[:, (q % 2) * D:(q % 2 + 1) * D],
                                  [((lhs_hi[:, t, rows], lhs_lo[:, t, rows]),
                                    (w_hi[:, j, t, :], w_lo[:, j, t, :])) for t in range(DT)],
                                  signal if q % 2 else None)

            def o_transposed(n, par, t, has):
                if not has(1):
                    pe.wait_ge(y_ready, at_least_0(2 * (n - 2) + 1 + t))
                transposes(ps_r[1 + t], [o[1 - par][:, q, t * P:(t + 1) * P] for q in range(Q)], oT_psum)

            def step(n, par, has):
                for i in range(Q):
                    gi = 4 * n + i
                    if has(0):
                        pe.wait_ge(stack_in, STACKED * n + STACKED)
                        pe.wait_ge(s_ready, at_least_0(gi))
                        for h in range(HEADS):
                            at = slice((h // HALF) * R + i * P, (h // HALF) * R + (i + 1) * P)
                            last = nc.tensor.matmul(ps_s[h // HALF][:, (h % HALF) * P:(h % HALF + 1) * P],
                                                    qk_st[par][:, 0, h % HALF, at], qk_st[par][:, 1, h % HALF, at],
                                                    start=True, stop=True)
                        last.then_inc(s_psum, 1)
                    if i == 2 and has(-1):
                        pe.wait_ge(o_ready, 4 * (n - 1) + 4)
                        pe.wait_ge(q_whole_ready, upto(n + 2, groups))
                        o_transposed(n, par, 0, has)
                    if has(-1) if i < 2 else has(0):
                        k = (i - 2) % Q
                        q = par if i >= 2 else 1 - par
                        pe.wait_ge(pT_lo_ready, 2 * (gi - 2) + 2)
                        pe.wait_ge(o_ready, at_least_0(gi - 2))
                        if i == 2:
                            pe.wait_ge(v_third_ready, 2 * n + 2)
                        for h in range(HEADS):
                            at = slice((h % HALF) * P, (h % HALF + 1) * P)
                            cols = slice(h * HD, (h + 1) * HD)
                            parts = [(pT_hi, 0), (pT_hi, 1), (pT_hi, 2), (pT_lo, 0), (pT_lo, 1)]
                            for c, (p, j) in enumerate(parts):
                                last = nc.tensor.matmul(ps_o[:, cols],
                                                        p[:, h // HALF, at], v_parts[q][j][:, k, cols],
                                                        start=(c == 0), stop=(c == len(parts) - 1))
                        last.then_inc(o_psum, 1)
                    if i == 2 and has(-1):
                        pe.wait_ge(qk_lo_ready, upto(3 * (n + 1) + 2, 3 * groups))
                        o_transposed(n, par, 1, has)
                    if has(-1) if i == 0 else has(0):
                        pe.wait_ge(pT_lo_ready, at_least_0(2 * (gi - 1)))
                        for t in range(DT):
                            pe.wait_ge(e_ready, 8 * (gi - 1) + HALF * (t + 1))
                            transposes(ps_t[t], [e[1 - i % 2][:, HALF * t + j, :] for j in range(HALF)], pT_psum)
                    if i == 0 and has(1):
                        m = n + 1
                        if isinstance(n, int):
                            pe.wait_ge(w_lo_ready, 4)
                        pe.wait_ge(xT_lo_ready, 2 * m + 2)
                        q_or_k(0)
                        pe.wait_ge(y_ready, at_least_0(2 * (n - 2) + 1))
                        q_or_k(1)
                    if i == 1 and has(1):
                        pe.wait_ge(y_ready, at_least_0(2 * (n - 2) + 2))
                        q_or_k(2)
                        pe.wait_ge(qk_lo_ready, 3 * (n + 1) + 1)
                        q_or_k(3)
                    if i == 2 and has(1):
                        pe.wait_ge(qk_lo_ready, 3 * (n + 1) + 3)
                        rows_times(ps_r[0], xT_hi, xT_lo, 2, 0, v_psum)
                        pe.wait_ge(oT_lo_ready, at_least_0(2 * (n - 1) + 1))
                        rows_times(ps_r[1], xT_hi, xT_lo, 2, 1, v_psum)
                    if i == 3 and has(2):
                        m = n + 2
                        pe.wait_ge(xp_in, 16 * m + 16)
                        pe.wait_ge(oT_lo_ready, at_least_0(2 * (n - 1) + 2))
                        transposes(ps_r[2], [xp[:, q, 0:P] for q in range(Q)], xT_psum)
                        pe.wait_ge(v_whole_ready, at_least_0(2 * (n + 1) + 1))
                        transposes(ps_r[0], [xp[:, q, P:2 * P] for q in range(Q)], xT_psum)
                    if i == 3 and has(-1):
                        m = n - 1
                        pe.wait_ge(oT_lo_ready, 2 * m + 2)
                        pe.wait_ge(v_whole_ready, upto(2 * (n + 1) + 2, 2 * groups))
                        rows_times(ps_r[1], oT_hi, oT_lo, 3, 0, w_psum)
                        pe.wait_ge(xT_lo_ready, upto(2 * (n + 2) + 1, 2 * groups))
                        rows_times(ps_r[2], oT_hi, oT_lo, 3, 1, w_psum)
            run(pe, step)
def program(nc, x, adj, Wq, Wk, Wv, Wo, attn_w, attn_b, W1, b1, W2, b2, g1, beta1, g2, beta2, out):
    graphs = x.shape[0]
    groups = graphs // Q
    layers = attn_w.shape[0]
    x1 = nc.dram_tensor("x1_kept", (groups, P, Q * D), fp32, kind="Internal").ap()
    masks = nc.dram_tensor("masks_kept", (groups, P, Q * P), bf16, kind="Internal").ap()
    x_mid = [nc.dram_tensor(f"x_kept{i}", (groups, P, Q * D), fp32, kind="Internal").ap() for i in range(layers - 1)]
    raw = dict(W1=W1, W2=W2, attn_w=attn_w, attn_b=attn_b, g1=g1, beta1=beta1, g2=g2, beta2=beta2, b1=b1, b2=b2)
    with ExitStack() as ctx:
        def sb(name, shape, dt=fp32):
            return ctx.enter_context(nc.sbuf_tensor(name, shape, dt))

        mem = {"ident": sb("ident", [P, P]), "stage": [sb(f"stage{i}", [P, DT * FF]) for i in range(2)]}
        columns = (("g1", DT), ("beta1", DT), ("b2", DT), ("b1", FT))
        for name, tiles in columns:
            mem[name] = sb(f"{name}_column", [P, layers, tiles])
        ident_ready = ctx.enter_context(nc.semaphore("ident_ready"))
        with nc.Block() as block:
            @block.gpsimd
            def _(pool):
                pool.memset(mem["ident"][:, :], 0.0).then_inc(ident_ready, 1)
                pool.wait_ge(ident_ready, 1)
                pool.affine_select(out=mem["ident"][:, :], in_=mem["ident"][:, :], compare_op=ALU.not_equal, fill=1.0,
                                   base=0, pattern=[[-1, P]], channel_multiplier=1).then_inc(ident_ready, 1)
        first_layer(nc, mem, groups, x, adj, (Wq, Wk, Wv, Wo), raw, [name for name, _ in columns], x1, masks)
        mem["attn_w"] = sb("attn_w_row", [P, layers, 2 * D])
        mem["attn_b"] = sb("attn_b_row", [P, layers])
        mem["g2"] = sb("g2_row", [P, layers, D])
        mem["beta2"] = sb("beta2_row", [P, layers, D])
        for part in ("hi", "lo"):
            for name, tiles in WEIGHTS:
                mem[f"{name}_{part}"] = [sb(f"{name}_{part}{l}", [P, tiles, DT * FF // tiles], fp32r) for l in range(layers)]
        gnn_layers(nc, mem, layers, groups, raw, x1, masks, x_mid, out)


_INS = ["x", "adj", "L0_gnn_Wq", "L0_gnn_Wk", "L0_gnn_Wv", "L0_gnn_Wo", "L1_gnn_attn_w", "L1_gnn_attn_b",
        "L1_gnn_W1", "L1_gnn_b1", "L1_gnn_W2", "L1_gnn_b2", "L1_gnn_g1", "L1_gnn_beta1", "L1_gnn_g2", "L1_gnn_beta2"]


def kernel(**inputs):
    import numpy as _np
    import concourse.bacc as _bacc
    from concourse import mybir as _mybir
    from concourse.bass_utils import run_bass_kernel_spmd as _run

    nc = _bacc.Bacc("TRN2", target_bir_lowering=False, num_devices=1)
    arrays, args = {}, []
    for name in _INS:
        a = _np.ascontiguousarray(inputs[name])
        arrays[f"in_{name}"] = a
        args.append(nc.dram_tensor(f"in_{name}", a.shape, _mybir.dt.from_np(a.dtype), kind="ExternalInput").ap())
    shape = tuple(inputs["x"].shape)
    args.append(nc.dram_tensor("result", shape, _mybir.dt.float32, kind="ExternalOutput").ap())
    program(nc, *args)
    r = _run(nc, [arrays], core_ids=[0])
    return r.results[0]["result"]
```
